# Optimizing a Trainium2 kernel written in Bass

```python
import numpy as np
import jax
import jax.numpy as jnp

def _softmax(x, axis=-1):
    return jax.nn.softmax(x, axis=axis)

def _gelu(x):
    return jax.nn.gelu(x, approximate=True)

def _silu(x):
    return jax.nn.silu(x)

def _sigmoid(x):
    return jax.nn.sigmoid(x)

def _layernorm(x, axis=-1, eps=1e-05):
    m = jnp.mean(x, axis=axis, keepdims=True)
    v = jnp.var(x, axis=axis, keepdims=True)
    return (x - m) / jnp.sqrt(v + eps)

def _scatter_add(tgt, idx, src, axis=0):
    return tgt.at[idx].add(src)

def _segment_sum(src, seg, n):
    return jax.ops.segment_sum(src, seg, n)
kernel_name = 'mk_hybrid_d1_jaxref_r8_09f96b'

def setup_inputs(seed: int=0):
    np.random.seed(seed)
    _w = jnp.asarray

    def _L0_attn_a_setup():
        import jax, jax.numpy as jnp
        import numpy as np
        E = 256
        H = 16
        HD = E // H
        CKV = 64
        CQ = 192
        RD = 64
        SCALE = 1.0 / np.sqrt(HD + RD)

        def _rope(qr, kr, offset=0):
            s = qr.shape[2]
            t = jnp.arange(offset, offset + s, dtype=jnp.float32)
            inv_freq = 1.0 / 10000.0 ** (jnp.arange(0, RD, 2, dtype=jnp.float32) / RD)
            freqs = t[:, None] * inv_freq[None, :]
            cos = jnp.concatenate([jnp.cos(freqs)] * 2, axis=-1)
            sin = jnp.concatenate([jnp.sin(freqs)] * 2, axis=-1)

            def rot(x):
                x1, x2 = (x[..., :RD // 2], x[..., RD // 2:])
                return jnp.concatenate([-x2, x1], axis=-1)
            return (qr * cos + rot(qr) * sin, kr * cos + rot(kr) * sin)
        key = jax.random.key(seed)
        ks = jax.random.split(key, 10)

        def w(k, out_d, in_d):
            return jax.random.normal(k, (out_d, in_d), jnp.float32) * (1.0 / np.sqrt(in_d))
        return {'x': jax.random.normal(ks[0], (2, 256, E), jnp.float32), 'w_dq': w(ks[1], CQ, E), 'w_uq': w(ks[2], H * HD, CQ), 'w_dkv': w(ks[3], CKV, E), 'w_uk': w(ks[4], H * HD, CKV), 'w_uv': w(ks[5], H * HD, CKV), 'w_qr': w(ks[6], H * RD, CQ), 'w_kr': w(ks[7], H * RD, E), 'w_out': w(ks[8], E, E)}
    _L0_attn_a_in = _L0_attn_a_setup()

    def _L0_attn_b_setup():
        import jax, jax.numpy as jnp
        import numpy as np
        D_MODEL = 256
        N_HEADS = 32
        N_KV_HEADS = 8
        HEAD_DIM = D_MODEL // N_HEADS
        ROPE_THETA = 10000.0

        def _build_rope_cache(seq_len, head_dim, theta):
            half = head_dim // 2
            inv_freq = 1.0 / theta ** (jnp.arange(half, dtype=jnp.float32) / half)
            pos = jnp.arange(seq_len, dtype=jnp.float32)
            freqs = jnp.outer(pos, inv_freq)
            return (jnp.cos(freqs), jnp.sin(freqs))

        def _apply_rope(x, cos, sin):
            x_even = x[..., ::2]
            x_odd = x[..., 1::2]
            c = cos[None, None]
            s = sin[None, None]
            rot_even = x_even * c - x_odd * s
            rot_odd = x_even * s + x_odd * c
            return jnp.stack((rot_even, rot_odd), axis=-1).reshape(x.shape)
        key = jax.random.key(seed)
        k0, k1, k2, k3, k4 = jax.random.split(key, 5)
        B, S = (2, 256)
        scale = 0.02
        x = jax.random.normal(k0, (B, S, D_MODEL), dtype=jnp.float32)
        Wq = jax.random.normal(k1, (D_MODEL, N_HEADS * HEAD_DIM), dtype=jnp.float32) * scale
        Wk = jax.random.normal(k2, (D_MODEL, N_KV_HEADS * HEAD_DIM), dtype=jnp.float32) * scale
        Wv = jax.random.normal(k3, (D_MODEL, N_KV_HEADS * HEAD_DIM), dtype=jnp.float32) * scale
        Wo = jax.random.normal(k4, (D_MODEL, D_MODEL), dtype=jnp.float32) * scale
        return {'x': x, 'Wq': Wq, 'Wk': Wk, 'Wv': Wv, 'Wo': Wo}
    _L0_attn_b_in = _L0_attn_b_setup()

    def _L0_ffn_setup():
        import jax, jax.numpy as jnp
        import numpy as np
        H = 256
        I = 688
        E = 8
        TOPK = 2
        key = jax.random.key(seed)
        ks = jax.random.split(key, 5)
        s = 0.02
        x = jax.random.normal(ks[0], (2, 256, H), dtype=jnp.float32)
        router_w = jax.random.normal(ks[1], (E, H), dtype=jnp.float32) * s
        Wg = jax.random.normal(ks[2], (E, I, H), dtype=jnp.float32) * s
        Wu = jax.random.normal(ks[3], (E, I, H), dtype=jnp.float32) * s
        Wd = jax.random.normal(ks[4], (E, H, I), dtype=jnp.float32) * s
        return {'x': x, 'router_w': router_w, 'Wg': Wg, 'Wu': Wu, 'Wd': Wd}
    _L0_ffn_in = _L0_ffn_setup()
    _d = {'L0_attn_a_x': _L0_attn_a_in['x'], 'L0_attn_a_w_dq': _L0_attn_a_in['w_dq'], 'L0_attn_a_w_uq': _L0_attn_a_in['w_uq'], 'L0_attn_a_w_dkv': _L0_attn_a_in['w_dkv'], 'L0_attn_a_w_uk': _L0_attn_a_in['w_uk'], 'L0_attn_a_w_uv': _L0_attn_a_in['w_uv'], 'L0_attn_a_w_qr': _L0_attn_a_in['w_qr'], 'L0_attn_a_w_kr': _L0_attn_a_in['w_kr'], 'L0_attn_a_w_out': _L0_attn_a_in['w_out'], 'L0_attn_b_Wq': _L0_attn_b_in['Wq'], 'L0_attn_b_Wk': _L0_attn_b_in['Wk'], 'L0_attn_b_Wv': _L0_attn_b_in['Wv'], 'L0_attn_b_Wo': _L0_attn_b_in['Wo'], 'L0_ffn_router_w': _L0_ffn_in['router_w'], 'L0_ffn_Wg': _L0_ffn_in['Wg'], 'L0_ffn_Wu': _L0_ffn_in['Wu'], 'L0_ffn_Wd': _L0_ffn_in['Wd']}
    _x0 = _d['L0_attn_a_x']
    _d['L0_attn_a_x'] = jax.random.normal(jax.random.fold_in(jax.random.key(seed), 1), (4, 256, 256), dtype=_x0.dtype)
    del _x0
    return _d

def reference(L0_attn_a_x, L0_attn_a_w_dq, L0_attn_a_w_uq, L0_attn_a_w_dkv, L0_attn_a_w_uk, L0_attn_a_w_uv, L0_attn_a_w_qr, L0_attn_a_w_kr, L0_attn_a_w_out, L0_attn_b_Wq, L0_attn_b_Wk, L0_attn_b_Wv, L0_attn_b_Wo, L0_ffn_router_w, L0_ffn_Wg, L0_ffn_Wu, L0_ffn_Wd):

    def _L0_attn_a_ref(x, w_dq, w_uq, w_dkv, w_uk, w_uv, w_qr, w_kr, w_out):
        import jax, jax.numpy as jnp
        import numpy as np
        E = 256
        H = 16
        HD = E // H
        CKV = 64
        CQ = 192
        RD = 64
        SCALE = 1.0 / np.sqrt(HD + RD)

        def _rope(qr, kr, offset=0):
            s = qr.shape[2]
            t = jnp.arange(offset, offset + s, dtype=jnp.float32)
            inv_freq = 1.0 / 10000.0 ** (jnp.arange(0, RD, 2, dtype=jnp.float32) / RD)
            freqs = t[:, None] * inv_freq[None, :]
            cos = jnp.concatenate([jnp.cos(freqs)] * 2, axis=-1)
            sin = jnp.concatenate([jnp.sin(freqs)] * 2, axis=-1)

            def rot(x):
                x1, x2 = (x[..., :RD // 2], x[..., RD // 2:])
                return jnp.concatenate([-x2, x1], axis=-1)
            return (qr * cos + rot(qr) * sin, kr * cos + rot(kr) * sin)
        b, s, _ = x.shape
        c_q = x @ w_dq.T
        q_c = (c_q @ w_uq.T).reshape(b, s, H, HD).transpose(0, 2, 1, 3)
        c_kv = x @ w_dkv.T
        k_c = (c_kv @ w_uk.T).reshape(b, s, H, HD).transpose(0, 2, 1, 3)
        v = (c_kv @ w_uv.T).reshape(b, s, H, HD).transpose(0, 2, 1, 3)
        q_r = (c_q @ w_qr.T).reshape(b, s, H, RD).transpose(0, 2, 1, 3)
        k_r = (x @ w_kr.T).reshape(b, s, H, RD).transpose(0, 2, 1, 3)
        q_r, k_r = _rope(q_r, k_r, offset=0)
        q = jnp.concatenate([q_c, q_r], axis=-1)
        k = jnp.concatenate([k_c, k_r], axis=-1)
        attn = jnp.einsum('bhqd,bhkd->bhqk', q, k) * SCALE
        mask = jnp.triu(jnp.full((s, s), -jnp.inf, jnp.float32), k=1)
        attn = jax.nn.softmax((attn + mask).astype(jnp.float32), axis=-1).astype(q.dtype)
        out = jnp.einsum('bhqk,bhkd->bhqd', attn, v)
        out = out.transpose(0, 2, 1, 3).reshape(b, s, H * HD)
        return out @ w_out.T

    def _L0_attn_b_ref(x, Wq, Wk, Wv, Wo):
        import jax, jax.numpy as jnp
        import numpy as np
        D_MODEL = 256
        N_HEADS = 32
        N_KV_HEADS = 8
        HEAD_DIM = D_MODEL // N_HEADS
        ROPE_THETA = 10000.0

        def _build_rope_cache(seq_len, head_dim, theta):
            half = head_dim // 2
            inv_freq = 1.0 / theta ** (jnp.arange(half, dtype=jnp.float32) / half)
            pos = jnp.arange(seq_len, dtype=jnp.float32)
            freqs = jnp.outer(pos, inv_freq)
            return (jnp.cos(freqs), jnp.sin(freqs))

        def _apply_rope(x, cos, sin):
            x_even = x[..., ::2]
            x_odd = x[..., 1::2]
            c = cos[None, None]
            s = sin[None, None]
            rot_even = x_even * c - x_odd * s
            rot_odd = x_even * s + x_odd * c
            return jnp.stack((rot_even, rot_odd), axis=-1).reshape(x.shape)
        B, S, _ = x.shape
        q = (x @ Wq).reshape(B, S, N_HEADS, HEAD_DIM).transpose(0, 2, 1, 3)
        k = (x @ Wk).reshape(B, S, N_KV_HEADS, HEAD_DIM).transpose(0, 2, 1, 3)
        v = (x @ Wv).reshape(B, S, N_KV_HEADS, HEAD_DIM).transpose(0, 2, 1, 3)
        cos, sin = _build_rope_cache(S, HEAD_DIM, ROPE_THETA)
        q = _apply_rope(q, cos, sin)
        k = _apply_rope(k, cos, sin)
        repeat = N_HEADS // N_KV_HEADS
        if repeat > 1:
            k = jnp.repeat(k, repeat, axis=1)
            v = jnp.repeat(v, repeat, axis=1)
        scores = jnp.einsum('bhqd,bhkd->bhqk', q, k) / jnp.sqrt(jnp.float32(HEAD_DIM))
        causal = jnp.tril(jnp.ones((S, S), dtype=bool))
        neg = -jnp.finfo(scores.dtype).max
        scores = jnp.where(causal[None, None], scores, neg)
        probs = jax.nn.softmax(scores.astype(jnp.float32), axis=-1).astype(x.dtype)
        out = jnp.einsum('bhqk,bhkd->bhqd', probs, v)
        out = out.transpose(0, 2, 1, 3).reshape(B, S, D_MODEL)
        return out @ Wo

    def _L0_ffn_ref(x, router_w, Wg, Wu, Wd):
        import jax, jax.numpy as jnp
        import numpy as np
        H = 256
        I = 688
        E = 8
        TOPK = 2
        B, S, Hh = x.shape
        xf = x.reshape(-1, Hh)
        logits = xf @ router_w.T
        top_vals, top_idx = jax.lax.top_k(logits, TOPK)
        top_w = jax.nn.softmax(top_vals, axis=-1)
        combine = jnp.sum(jax.nn.one_hot(top_idx, E, dtype=xf.dtype) * top_w[..., None], axis=1)
        out = jnp.zeros_like(xf)
        for e in range(E):
            h = jax.nn.silu(xf @ Wg[e].T) * (xf @ Wu[e].T)
            y = h @ Wd[e].T
            out = out + combine[:, e:e + 1] * y
        return out.reshape(B, S, Hh)
    x = L0_attn_a_x
    x = x + _L0_attn_a_ref(_layernorm(x, axis=-1), L0_attn_a_w_dq, L0_attn_a_w_uq, L0_attn_a_w_dkv, L0_attn_a_w_uk, L0_attn_a_w_uv, L0_attn_a_w_qr, L0_attn_a_w_kr, L0_attn_a_w_out)
    x = x + _L0_ffn_ref(_layernorm(x, axis=-1), L0_ffn_router_w, L0_ffn_Wg, L0_ffn_Wu, L0_ffn_Wd)
    x = x + _L0_attn_b_ref(_layernorm(x, axis=-1), L0_attn_b_Wq, L0_attn_b_Wk, L0_attn_b_Wv, L0_attn_b_Wo)
    x = x + _L0_ffn_ref(_layernorm(x, axis=-1), L0_ffn_router_w, L0_ffn_Wg, L0_ffn_Wu, L0_ffn_Wd)
    return x

_drawn_inputs = setup_inputs


def setup_inputs(seed=0):
    import zlib

    import numpy as np

    out = dict(_drawn_inputs(seed))
    spreads = {}
    factors = {'L0_attn_b_Wq': 8.0, 'L0_attn_b_Wk': 8.0, 'L0_attn_b_Wo': 2.682}
    for name, (base, spread) in spreads.items():
        noise = np.random.default_rng([zlib.crc32(name.encode()), seed]).standard_normal(out[name].shape)
        drawn = base * np.exp(spread * noise) if base else spread * noise
        out[name] = jnp.asarray(drawn.astype(out[name].dtype))
    for name, factor in factors.items():
        out[name] = (out[name] * factor).astype(out[name].dtype)
    return out
```

```python
import math
from contextlib import ExitStack

import numpy as np

import concourse.bass as bass
from concourse import mybir

F32 = mybir.dt.float32
BF16 = mybir.dt.bfloat16
U16 = mybir.dt.uint16
I32 = mybir.dt.int32
U32 = mybir.dt.uint32
ALU = mybir.AluOpType
ACT = mybir.ActivationFunctionType
AX = mybir.AxisListType.X

P = 128
B, S, D = 4, 256, 256
T = B * S
NT = T // P
KD = D // P
EPS = 1e-5

HA, HDA, RD, CQ, CKV = 16, 16, 64, 192, 64
HB, HDB, KVB = 32, 8, 8
GA, GB = HA // 4, HB // 4
SCALE_A = 1.0 / math.sqrt(HDA + RD)
SCALE_B = 1.0 / math.sqrt(HDB)
CQH = CQ // 2
RA = 96
PARTS = 3
RB = PARTS * PARTS * HDB
RBZ = 96
NEG = -1e30

E, I, TOPK = 8, 688, 2
IH = I // 2
GU = 2 * I
CH = [115, 115, 115, 115, 114, 114]
CO = [0, 115, 230, 345, 460, 574]
ROUTED = T * TOPK
SLOTS_T = (ROUTED - E) // P + E
SLOTS = SLOTS_T * P


def shape_constants():
    def bf16(x):
        return (np.ascontiguousarray(x, dtype=np.float32).view(np.uint32) >> 16).astype(np.uint16)

    pos = np.arange(S, dtype=np.float32)
    fa = (1.0 / np.float32(10000.0) ** (np.arange(0, RD, 2, dtype=np.float32) / np.float32(RD))).astype(np.float32)
    aa = (pos[:, None] * fa[None, :]).astype(np.float32).T
    rope_a = np.stack([np.tile(np.cos(aa), (4, 1)), np.tile(np.sin(aa), (4, 1))], 1).astype(np.float32)
    fb = (1.0 / np.float32(10000.0) ** (np.arange(HDB // 2, dtype=np.float32) / np.float32(HDB // 2))).astype(np.float32)
    ab = (pos[:, None] * fb[None, :]).astype(np.float32).T
    rope_b = np.stack([np.tile(np.cos(ab), (HB, 1)), np.tile(np.sin(ab), (HB, 1))], 1).astype(np.float32)
    q = np.arange(P)
    diag = np.where(q[None, :] > q[:, None], NEG, 0.0)
    none = np.zeros((P, P))
    masks = np.stack([np.concatenate([none, diag], 1), np.concatenate([diag.T, none], 1)], 1)
    sel = np.arange(PARTS * 32)[:, None] % 32 == np.arange(32)[None, :]
    tri = q[:, None] < q[None, :]
    e = np.arange(E, dtype=np.float32)
    small = np.concatenate([
        e,
        np.repeat(e[:, None], E, 1).T.reshape(-1) * P,
        (e[None, :] < e[:, None]).astype(np.float32).reshape(-1),
        np.arange(24, dtype=np.float32),
    ]).astype(np.float32)
    small = np.broadcast_to(small, (P, small.size)).copy()
    return {"rope_a": rope_a, "rope_b": rope_b, "masks": bf16(masks), "sel": bf16(sel), "tri": bf16(tri),
            "ident": np.eye(P, dtype=np.float32), "identb": bf16(np.eye(P)),
            "onesb": bf16(np.ones((P, P))), "small": small}


def build_hybrid(nc, dr, out):
    ctx = ExitStack()
    with ctx:
        def sb(name, shape, dt):
            return ctx.enter_context(nc.sbuf_tensor(name, shape, dt))

        def sem(name):
            return ctx.enter_context(nc.semaphore(name))

        wgu = sb("wgu", [P, E * KD * GU], F32)
        R1 = sb("R1", [P, E * 6 * D], F32)
        R2 = sb("R2", [P, 6144], F32)
        xres = sb("xres", [P, NT, D], F32)
        XN = sb("XN", [P, NT * D], F32)
        xnT = sb("xnT", [P, KD, T], F32)
        PTR = sb("PTR", [P, 2 * 3 * 512], F32)
        wqb = sb("wqb", [P, KD, D], F32)
        wkvb = sb("wkvb", [P, KD, 2 * KVB * HDB], F32)
        wob = sb("wob", [P, KD, D], F32)
        vaug = sb("vaug", [P, 2 * HA * 32], F32)
        rope = sb("rope", [P, 2, S], F32)
        ident = sb("ident_sb", [P, P], F32)
        identb = sb("identb_sb", [P, P], BF16)
        masks = sb("masks_sb", [P, 2, 2 * P], BF16)
        sel = sb("sel_sb", [PARTS * 32, 32], BF16)
        xn = XN[:, :].rearrange("p (t d) -> p t d", t=NT)
        wd = R1[0:CH[0], :]

        qst = R1[0:RA, 0:HA * S].rearrange("p (h s) -> p h s", h=HA)
        kst = R1[0:RA, HA * S:2 * HA * S].rearrange("p (h s) -> p h s", h=HA)
        o = 2 * HA * S
        stage = R1[:, o:o + 4 * 2 * S].rearrange("p (n a s) -> p n a s", n=4, a=2)
        o += 4 * 2 * S
        qc = R1[:, o:o + 2 * S].rearrange("p (a s) -> p a s", a=2)
        kc = R1[:, o + 2 * S:o + 4 * S].rearrange("p (a s) -> p a s", a=2)
        o += 4 * S
        cqT = R1[0:CQH, o:o + 2 * S].rearrange("p (a s) -> p a s", a=2)
        ckvT = R1[0:CKV, o + 2 * S:o + 3 * S]
        o = 0
        wdq = R2[:, o:o + KD * CQ].rearrange("p (k n) -> p k n", k=KD); o += KD * CQ
        wdkv = R2[:, o:o + KD * CKV].rearrange("p (k n) -> p k n", k=KD); o += KD * CKV
        wuq = R2[0:CQH, o:o + 2 * D].rearrange("p (k n) -> p k n", k=2); o += 2 * D
        wqr = R2[0:CQH, o:o + 2 * HA * RD].rearrange("p (k n) -> p k n", k=2); o += 2 * HA * RD
        wkr = R2[:, o:o + KD * HA * RD].rearrange("p (k n) -> p k n", k=KD); o += KD * HA * RD
        wuk = R2[0:CKV, o:o + D]; o += D
        wuv = R2[0:CKV, o:o + D]; o += D
        woa = R2[:, o:o + KD * D].rearrange("p (k n) -> p k n", k=KD); o += KD * D
        assert o == 6144
        rt = PTR[:, 0:2048].rearrange("p (n c a s) -> p n c a s", n=2, c=2, a=2)
        PT = PTR[:, :].rearrange("p (n b s) -> p n b s", n=2, b=3)
        oun = XN[:, 0:512].rearrange("p (n s) -> p n s", n=2)
        otok = XN[:, 512:1024].rearrange("p (q d) -> p q d", q=2)
        oT = XN[:, 1024:1536].rearrange("p (k s) -> p k s", k=2)
        nmax = XN[:, 1536:1600].rearrange("p (q h) -> p q h", q=2)
        nrem = XN[:, 1600:1664].rearrange("p (q h) -> p q h", q=2)
        rec = XN[:, 1664:1672].rearrange("p (q j) -> p q j", q=2)
        nparts = XN[:, 1672:1768].bitcast(BF16).rearrange("p (q n h) -> p q n h", q=2, n=PARTS)
        npartf = XN[:, 1672:1768].bitcast(BF16).rearrange("p (q m) -> p q m", q=2)
        nT = XN[0:PARTS * 32, 1768:1896].bitcast(BF16)
        stat = sb("stat", [P, 112], F32)
        bst = stat[:, 0:NT * 6].rearrange("p (t n) -> p t n", t=NT)
        mv = stat[:, 48:48 + NT * 2].rearrange("p (t n) -> p t n", t=NT)
        var = stat[:, 64:72]
        std = stat[:, 72:80]
        rstd = stat[:, 80:88]
        slot = stat[:, 88:104].bitcast(I32)
        w01 = sb("w01", [P, 2, NT], F32)
        o = 0
        xs = R2[:, o:o + 512].rearrange("p (n d) -> p n d", n=2); o += 512
        xsT = R2[:, o:o + 512].rearrange("p (n k s) -> p n k s", n=2, k=KD); o += 512
        sg = R2[:, o:o + I]; o += I
        hh = R2[:, o:o + I]; o += I
        hT = R2[0:CH[0], o:o + 2 * 6 * P].rearrange("p (n c s) -> p n c s", n=2, c=6); o += 2 * 6 * P
        yo = R2[:, o:o + 512].rearrange("p (n d) -> p n d", n=2); o += 512
        rw = R2[:, o:o + KD * E].rearrange("p (k e) -> p k e", k=KD); o += KD * E
        lg = R2[:, o:o + 64].rearrange("p (t e) -> p t e", t=NT); o += 64
        mx = R2[:, o:o + 64].rearrange("p (t e) -> p t e", t=NT); o += 64
        mi = R2[:, o:o + 64].bitcast(U32).rearrange("p (t e) -> p t e", t=NT); o += 64
        idf = R2[:, o:o + 16].rearrange("p (k t) -> p k t", k=2); o += 16
        oh = R2[:, o:o + 128].rearrange("p (k t e) -> p k t e", k=2, t=NT); o += 128
        ohp = R2[:, o:o + 128].rearrange("p (k t e) -> p k t e", k=2, t=NT); o += 128
        cnt = R2[:, o:o + 32].bitcast(BF16); o += 32
        cmp = R2[:, o:o + 64].rearrange("p (e j) -> p e j", e=E); o += 64
        ntl = R2[:, o:o + E]; o += E
        base = R2[:, o:o + E]; o += E
        posb = R2[:, o:o + 64].rearrange("p (t e) -> p t e", t=NT); o += 64
        slf = R2[:, o:o + 16]; o += 16
        ecm = R2[0:1, o:o + 24 * 7].rearrange("p (i e) -> p i e", e=7); o += 168
        eidf = R2[0:1, o:o + 24]; o += 24
        eid = R2[0:1, o:o + 24].bitcast(I32); o += 24
        dlt = R2[:, o:o + NT]; o += NT
        ex1 = R2[:, o:o + NT]; o += NT
        den = R2[:, o:o + NT]; o += NT
        tri = R2[:, o:o + 64].bitcast(BF16); o += 64
        onesb = R2[:, o:o + 64].bitcast(BF16); o += 64
        small = R2[:, o:o + 160]; o += 160
        assert o <= 6144, o
        yg = PTR[:, 0:2048].rearrange("p (n k d) -> p n k d", n=4, k=2)
        qsb = R2[0:RBZ, 0:HB * S // 2].bitcast(BF16).rearrange("p (h s) -> p h s", h=HB)
        ksb = R2[0:RBZ, 4096:4096 + KVB * S // 2].bitcast(BF16).rearrange("p (h s) -> p h s", h=KVB)
        vall = R2[:, 5120:5120 + NT * 64].rearrange("p (t n) -> p t n", t=NT)
        rtb = PTR[:, 0:1024].rearrange("p (c a s) -> p c a s", c=2, a=2)
        rsb = PTR[:, 1024:1536].rearrange("p (a s) -> p a s", a=2)
        rem = PTR[:, 1536:2048].rearrange("p (a s) -> p a s", a=2)
        qparts = PTR[:, 2048:2816].bitcast(BF16).rearrange("p (n a s) -> p n a s", n=PARTS, a=2)

        BK = [ctx.enter_context(nc.psum_tensor(f"bank{i}", [P, 512], F32)) for i in range(8)]

        xs_d = nc.dram_tensor("slots_in", [SLOTS, D], F32, kind="Internal").ap()
        ys_d = nc.dram_tensor("slots_out", [SLOTS, D], F32, kind="Internal").ap()
        q_d = nc.dram_tensor("q_parts", [PARTS, 2, B, HB, HDB // 2, S], BF16, kind="Internal").ap()
        k_d = nc.dram_tensor("k_parts", [PARTS, 2, B, KVB, HDB // 2, S], BF16, kind="Internal").ap()

        s_const = sem("s_const")
        s_x = sem("s_x")
        s_wa = sem("s_wa")
        s_wb = sem("s_wb")
        s_wgu = sem("s_wgu")
        s_wd = sem("s_wd")
        s_zero = sem("s_zero")
        s_init = sem("s_init")
        s_out = sem("s_out")


        def named(prefix, names):
            return {n: sem(f"{prefix}_{n}") for n in names.split()}

        LN = [named(f"ln{l}", "own vareps root normed transposed evac_s evac_v") for l in range(4)]
        AN = ("placed values scores maxima hi rest mid lo max_t max_e shifted exps pv pv_e out_t recips "
              "divided all_t all_e projected added")
        AT = {0: named("at0", AN), 2: named("at2", AN)}
        PA = named("pa", "item evac_s evac_v summed placed_k")
        PB = named("pb", "item prod summed hi rest mid lo stored zeroed vall")
        FN = ("own consts logits count rank1 "
              "slot eid dlt exp1 scatter xs0 xs1 x_t x_e gu silu hid hid_t hte_v hte_s "
              "down y_e ys0 ys1 g0 g1 g2 g3 added")
        FF = {1: named("ff1", FN), 3: named("ff3", FN)}


        def later(eng, sem, count):
            if not (isinstance(count, int) and count == 0):
                eng.wait_ge(sem, count)

        def norm_vector(l, x_ready):
            s = LN[l]
            for t in range(NT):
                if x_ready is not None:
                    nc.vector.wait_ge(*x_ready(t))
                nc.vector.bn_stats(bst[:, t, :], xres[:, t, :]).then_inc(s["own"], 1)
            for t in range(NT):
                nc.vector.wait_ge(s["own"], t + 1)
                nc.vector.bn_aggr(mv[:, t, :], bst[:, t, :]).then_inc(s["own"], 1)
            nc.vector.wait_ge(s["own"], 2 * NT)
            nc.vector.tensor_scalar_add(var, mv[:, :, 1], EPS).then_inc(s["vareps"], 1)
            nc.vector.wait_ge(s["root"], 1)
            nc.vector.reciprocal(rstd, std).then_inc(s["own"], 1)
            nc.vector.wait_ge(s["own"], 2 * NT + 1)
            for t in range(NT):
                nc.vector.tensor_scalar(xn[:, t, :], xres[:, t, :], mv[:, t, 0:1], rstd[:, t:t + 1],
                                        ALU.subtract, ALU.mult).then_inc(s["normed"], 1)
            for t in range(1, NT, 2):
                nc.vector.wait_ge(s["transposed"], t + 1)
                nc.vector.tensor_copy(xnT[:, :, t * P:(t + 1) * P],
                                      BK[t % 4][:, 0:KD * P].rearrange("p (k s) -> p k s", k=KD)
                                      ).then_inc(s["evac_v"], 1)

        def norm_scalar(l):
            s = LN[l]
            nc.scalar.wait_ge(s["vareps"], 1)
            nc.scalar.activation(std, var, ACT.Sqrt).then_inc(s["root"], 1)
            for t in range(0, NT, 2):
                nc.scalar.wait_ge(s["transposed"], t + 1)
                nc.scalar.activation(xnT[:, :, t * P:(t + 1) * P],
                                     BK[t % 4][:, 0:KD * P].rearrange("p (k s) -> p k s", k=KD),
                                     ACT.Copy).then_inc(s["evac_s"], 1)

        def norm_tensor(l):
            s = LN[l]
            for t in range(NT):
                nc.tensor.wait_ge(s["normed"], t + 1)
                if t >= 4:
                    nc.tensor.wait_ge(s["evac_v" if t % 2 else "evac_s"], (t - 4) // 2 + 1)
                for k in range(KD):
                    last = nc.tensor.transpose(BK[t % 4][:, k * P:(k + 1) * P], xn[:, t, k * P:(k + 1) * P], ident[:, :])
                last.then_inc(s["transposed"], 1)

        def wait_normed(eng, l):
            eng.wait_ge(LN[l]["evac_s"], NT // 2)
            eng.wait_ge(LN[l]["evac_v"], NT // 2)

        def heads(l):
            if l == 0:
                return GA, (lambda h: qst[:, h, :]), (lambda h: kst[:, h, :]), (lambda h: h), HDA, SCALE_A, woa
            return GB, (lambda h: qsb[:, h, :]), (lambda h: ksb[:, h // 4, :]), (lambda h: h // 4), HDB, SCALE_B, wob

        def attend_tensor(l, b):
            s = AT[l]
            G, q, k, v, hd, scale, wo = heads(l)
            va = vaug[:, 0:2 * v(4 * G - 1) * 32 + 64].rearrange("p (n h c) -> p n h c", n=2, c=32)
            if l == 0:
                nc.tensor.wait_ge(PA["evac_v"], (b + 1) * len(BY_V))
                nc.tensor.wait_ge(PA["evac_s"], (b + 1) * len(BY_S))
                nc.tensor.wait_ge(PA["placed_k"], b * PLACED_K + PLACED_K)
                nc.tensor.wait_ge(s["placed"], b * PLACED_A + PLACED_A)
            else:
                nc.tensor.wait_ge(PB["vall"], 1)
                nc.tensor.wait_ge(PB["prod"], B + 1)
                nc.tensor.wait_ge(s["placed"], b * PLACED_B + PLACED_B)
            for g in range(G):
                bank = BK[3 * (g % 2):3 * (g % 2) + 3]
                if g >= 2:
                    nc.tensor.wait_ge(s["maxima"], b * 3 * G + 3 * (g - 1))
                nc.tensor.matmul(bank[0][:, :].rearrange("p (n s) -> p n s", n=4), identb[:, :],
                                 masks[:, 0, None, P:2 * P].broadcast_to([P, 4, P]),
                                 start=True, stop=False, skip_group_check=True)
                for j in range(4):
                    h = 4 * g + j
                    last = nc.tensor.matmul(bank[0][:, j * P:(j + 1) * P], q(h)[:, 0:P], k(h)[:, 0:P],
                                            start=False, stop=j == 3, skip_group_check=True)
                last.then_inc(s["scores"], 1)
                for i in range(2):
                    nc.tensor.matmul(bank[1 + i][:, :].rearrange("p (n s) -> p n s", n=2), identb[:, :],
                                     masks[:, 0, None, :].broadcast_to([P, 2, S]),
                                     start=True, stop=False, skip_group_check=True)
                    for j in range(2):
                        h = 4 * g + 2 * i + j
                        last = nc.tensor.matmul(bank[1 + i][:, j * S:(j + 1) * S], q(h)[:, P:S], k(h)[:, :],
                                                start=False, stop=j == 1, skip_group_check=True)
                    last.then_inc(s["scores"], 1)
            nc.tensor.wait_ge(s["lo"], b + 1)
            later(nc.tensor, s["all_e"], b)
            for t in range(2):
                last = nc.tensor.transpose(BK[7][0:PARTS * 32, :].bitcast(BF16)[:, t * P:(t + 1) * P],
                                           npartf[:, t, :], identb[:, :])
            last.then_inc(s["max_t"], 1)
            nc.tensor.wait_ge(s["max_e"], b + 1)

            def pv(g):
                n = g % 2
                nc.tensor.wait_ge(s["exps"], b * 3 * G + 3 * (g + 1))
                if g == 0:
                    later(nc.tensor, s["added"], b)
                    if l == 0:
                        nc.tensor.wait_ge(PA["evac_s"], (b + 1) * len(BY_S))
                    else:
                        nc.tensor.wait_ge(s["values"], b + 1)
                else:
                    nc.tensor.wait_ge(s["pv_e"], b * G + g)
                for j in range(4):
                    nc.tensor.matmul(BK[6][32 * j:32 * j + 32, 0:S], va[:, 0, v(4 * g + j), :],
                                     PT[:, n, j // 2, (j % 2) * S:(j % 2 + 1) * S],
                                     start=True, stop=False, skip_group_check=True, tile_position=(0, 32 * j))
                for j in range(4):
                    last = nc.tensor.matmul(BK[6][32 * j:32 * j + 32, P:S], va[:, 1, v(4 * g + j), :],
                                            PT[:, n, 2, j * P:(j + 1) * P],
                                            start=False, stop=True, skip_group_check=True, tile_position=(0, 32 * j))
                last.then_inc(s["pv"], 1)

            def out_t(g):
                nc.tensor.wait_ge(s["pv_e"], b * G + g + 1)
                if g >= 1:
                    nc.tensor.wait_ge(s["divided"], b * G + g)
                for t in range(2):
                    last = nc.tensor.transpose(BK[7][:, t * P:(t + 1) * P], oun[:, g % 2, t * P:(t + 1) * P], ident[:, :])
                last.then_inc(s["out_t"], 1)

            for g in range(G + 2):
                if g < G:
                    bank = BK[3 * (g % 2):3 * (g % 2) + 3]
                    if g < 2:
                        nc.tensor.wait_ge(s["maxima"], (b + 1) * 3 * G)
                    else:
                        nc.tensor.wait_ge(s["exps"], b * 3 * G + 3 * (g - 1))
                    for i in range(2):
                        nc.tensor.matmul(bank[i][:, :].rearrange("p (n s) -> p n s", n=2), identb[:, :],
                                         masks[:, 1, None, :].broadcast_to([P, 2, S]),
                                         start=True, stop=False, skip_group_check=True)
                        for j in range(2):
                            h = 4 * g + 2 * i + j
                            nc.tensor.matmul(bank[i][:, j * S:(j + 1) * S], sel[:, h:h + 1].broadcast_to([PARTS * 32, P]),
                                             nT[:, :], start=False, stop=False, skip_group_check=True)
                            last = nc.tensor.matmul(bank[i][:, j * S:(j + 1) * S], k(h)[:, 0:P], q(h)[:, :],
                                                    start=False, stop=j == 1, skip_group_check=True)
                        last.then_inc(s["shifted"], 1)
                    nc.tensor.matmul(bank[2][:, :].rearrange("p (n s) -> p n s", n=4), identb[:, :],
                                     masks[:, 1, None, 0:P].broadcast_to([P, 4, P]),
                                     start=True, stop=False, skip_group_check=True)
                    for j in range(4):
                        h = 4 * g + j
                        nc.tensor.matmul(bank[2][:, j * P:(j + 1) * P], sel[:, h:h + 1].broadcast_to([PARTS * 32, P]),
                                         nT[:, P:S], start=False, stop=False, skip_group_check=True)
                        last = nc.tensor.matmul(bank[2][:, j * P:(j + 1) * P], k(h)[:, P:S], q(h)[:, P:S],
                                                start=False, stop=j == 3, skip_group_check=True)
                    last.then_inc(s["shifted"], 1)
                if 1 <= g <= G:
                    pv(g - 1)
                if g >= 2:
                    out_t(g - 2)
            nc.tensor.wait_ge(s["divided"], b * G + G)
            for kk in range(KD):
                for t in range(2):
                    last = nc.tensor.transpose(BK[7][:, (2 * kk + t) * P:(2 * kk + t + 1) * P],
                                               otok[:, t, kk * P:(kk + 1) * P], ident[:, :])
            last.then_inc(s["all_t"], 1)
            nc.tensor.wait_ge(s["all_e"], b + 1)
            for t in range(2):
                for kk in range(KD):
                    last = nc.tensor.matmul(BK[6][:, t * D:(t + 1) * D], oT[:, kk, t * P:(t + 1) * P], wo[:, kk, :],
                                            start=kk == 0, stop=kk == KD - 1)
            last.then_inc(s["projected"], 1)

        def attend_vector(l, b):
            s = AT[l]
            G, q, k, v, hd, scale, wo = heads(l)
            nh = 4 * G
            for g in range(G):
                bank = BK[3 * (g % 2):3 * (g % 2) + 3]
                nc.vector.wait_ge(s["scores"], b * 3 * G + 3 * g + 1)
                if g == 0:
                    later(nc.vector, s["max_t"], b)
                nc.vector.tensor_reduce(nmax[:, 0, 4 * g:4 * g + 4], bank[0][:, :].rearrange("p (n s) -> p n s", n=4),
                                        AX, ALU.max, negate=True).then_inc(s["maxima"], 1)
                for i in range(2):
                    nc.vector.wait_ge(s["scores"], b * 3 * G + 3 * g + 2 + i)
                    nc.vector.tensor_reduce(nmax[:, 1, 4 * g + 2 * i:4 * g + 2 * i + 2],
                                            bank[1 + i][:, :].rearrange("p (n s) -> p n s", n=2),
                                            AX, ALU.max, negate=True).then_inc(s["maxima"], 1)
            nc.vector.wait_ge(s["maxima"], (b + 1) * 3 * G)
            nc.vector.tensor_copy(nparts[:, :, 0, 0:nh], nmax[:, :, 0:nh]).then_inc(s["hi"], 1)
            nc.vector.wait_ge(s["hi"], b + 1)
            nc.vector.tensor_tensor(nrem[:, :, 0:nh], nmax[:, :, 0:nh], nparts[:, :, 0, 0:nh], ALU.subtract).then_inc(s["rest"], 1)
            nc.vector.wait_ge(s["rest"], b + 1)
            nc.vector.tensor_copy(nparts[:, :, 1, 0:nh], nrem[:, :, 0:nh]).then_inc(s["mid"], 1)
            nc.vector.wait_ge(s["mid"], b + 1)
            nc.vector.tensor_tensor(nparts[:, :, 2, 0:nh], nrem[:, :, 0:nh], nparts[:, :, 1, 0:nh], ALU.subtract).then_inc(s["lo"], 1)

            def divide(g):
                tt = BK[7][:, 0:S].rearrange("p (q j c) -> p q j c", q=2, c=32)
                nc.vector.wait_ge(s["out_t"], b * G + g + 1)
                nc.vector.reciprocal(rec[:, :, :], tt[:, :, :, hd]).then_inc(s["recips"], 1)
                nc.vector.wait_ge(s["recips"], b * G + g + 1)
                if g == 0:
                    later(nc.vector, s["all_t"], b)
                nc.vector.tensor_tensor(otok[:, :, 4 * g * hd:4 * (g + 1) * hd].rearrange("p q (j c) -> p q j c", j=4),
                                        tt[:, :, :, 0:hd], rec[:, :, :, None].broadcast_to([P, 2, 4, hd]),
                                        ALU.mult).then_inc(s["divided"], 1)

            for g in range(G):
                nc.vector.wait_ge(s["pv"], b * G + g + 1)
                if g >= 2:
                    nc.vector.wait_ge(s["out_t"], b * G + g - 1)
                nc.vector.tensor_copy(oun[:, g % 2, :], BK[6][:, 0:S]).then_inc(s["pv_e"], 1)
                if g >= 1:
                    divide(g - 1)
            divide(G - 1)
            nc.vector.wait_ge(s["projected"], b + 1)
            xb = xres[:, bass.ds(2 * b, 2), :]
            nc.vector.tensor_tensor(xb, xb, BK[6][:, :].rearrange("p (q d) -> p q d", q=2), ALU.add).then_inc(s["added"], 1)

        def attend_scalar(l, b):
            s = AT[l]
            G, q, k, v, hd, scale, wo = heads(l)
            nc.scalar.wait_ge(s["max_t"], b + 1)
            nc.scalar.activation(nT[:, :], BK[7][0:PARTS * 32, :].bitcast(BF16)[:, 0:S], ACT.Copy).then_inc(s["max_e"], 1)
            for g in range(G):
                bank = BK[3 * (g % 2):3 * (g % 2) + 3]
                for i in range(3):
                    nc.scalar.wait_ge(s["shifted"], b * 3 * G + 3 * g + i + 1)
                    if i == 0:
                        later(nc.scalar, s["pv"], b * G + max(g - 1, 0))
                    nc.scalar.activation(PT[:, g % 2, i, :], bank[i][:, :], ACT.Exp, scale=scale).then_inc(s["exps"], 1)
            nc.scalar.wait_ge(s["all_t"], b + 1)
            nc.scalar.activation(oT[:, :, :], BK[7][:, :].rearrange("p (k s) -> p k s", k=KD), ACT.Copy).then_inc(s["all_e"], 1)

        ITEMS = 13
        BY_V = [1, 2, 3, 4, 5, 9, 10, 11, 12]
        BY_S = [0, 6, 7, 8]
        ROT = [2, 3, 4, 5, 9, 10, 11, 12]
        PLACED_A = 16 * (2 * 8 + 4 * 8)
        PLACED_K = 16 * 4 * 8

        def wait_item(eng, b, i):
            if i in BY_V:
                eng.wait_ge(PA["evac_v"], b * len(BY_V) + BY_V.index(i) + 1)
            else:
                eng.wait_ge(PA["evac_s"], b * len(BY_S) + BY_S.index(i) + 1)

        def project_a_tensor(b):
            xb = [xnT[:, kk, bass.ds(b * S, S)] for kk in range(KD)]
            for i in range(ITEMS):
                bk = BK[i % 6]
                if i == 0:
                    later(nc.tensor, AT[0]["exps"], b * 3 * GA)
                elif i >= 6:
                    wait_item(nc.tensor, b, i - 6)
                if i == 0:
                    ops = [(bk[0:CQH, m * S:(m + 1) * S], wdq[:, kk, m * CQH:(m + 1) * CQH], xb[kk], kk)
                           for m in range(2) for kk in range(KD)]
                elif i == 1:
                    ops = [(bk[0:CKV, 0:S], wdkv[:, kk, :], xb[kk], kk) for kk in range(KD)]
                elif i < 6:
                    ops = [(bk[:, a * S:(a + 1) * S], wkr[:, kk, ((i - 2) * 2 + a) * P:((i - 2) * 2 + a + 1) * P], xb[kk], kk)
                           for a in range(2) for kk in range(KD)]
                elif i == 6:
                    ops = [(bk[:, m * S:(m + 1) * S], wuq[:, kk, m * P:(m + 1) * P], cqT[:, kk, :], kk)
                           for m in range(2) for kk in range(2)]
                elif i == 7:
                    wait_item(nc.tensor, b, 1)
                    ops = [(bk[:, m * S:(m + 1) * S], wuk[:, m * P:(m + 1) * P], ckvT[:, :], None) for m in range(2)]
                elif i == 8:
                    ops = [(bk[:, m * D:(m + 1) * D], ckvT[:, m * P:(m + 1) * P], wuv[:, :], None) for m in range(2)]
                else:
                    ops = [(bk[:, a * S:(a + 1) * S], wqr[:, kk, ((i - 9) * 2 + a) * P:((i - 9) * 2 + a + 1) * P], cqT[:, kk, :], kk)
                           for a in range(2) for kk in range(2)]
                for dst, w, r, kk in ops:
                    last = nc.tensor.matmul(dst, w, r, start=kk in (0, None), stop=kk in (1, None))
                last.then_inc(PA["item"], 1)

        def project_a_vector(b):
            for i in BY_V:
                bk = BK[i % 6]
                nc.vector.wait_ge(PA["item"], b * ITEMS + i + 1)
                if i == 1:
                    nc.vector.tensor_copy(ckvT[:, :], bk[0:CKV, 0:S]).then_inc(PA["evac_v"], 1)
                    continue
                r = ROT.index(i)
                if r >= 2:
                    nc.vector.wait_ge(PA["summed"], b * len(ROT) + r - 1)
                v = bk[:, :].rearrange("p (a s) -> p a s", a=2)
                nc.vector.tensor_tensor(rt[:, r % 2, 0, :, :], v, rope[:, 0, None, :].broadcast_to([P, 2, S]), ALU.mult)
                nc.vector.tensor_tensor(rt[:, r % 2, 1, :, :], v, rope[:, 1, None, :].broadcast_to([P, 2, S]),
                                        ALU.mult).then_inc(PA["evac_v"], 1)

        def project_a_scalar(b):
            for i in BY_S:
                bk = BK[i % 6]
                nc.scalar.wait_ge(PA["item"], b * ITEMS + i + 1)
                if i == 0:
                    dst, src = cqT[:, :, :], bk[0:CQH, :].rearrange("p (a s) -> p a s", a=2)
                elif i == 6:
                    later(nc.scalar, AT[0]["placed"], b * PLACED_A)
                    dst, src = qc[:, :, :], bk[:, :].rearrange("p (a s) -> p a s", a=2)
                elif i == 7:
                    dst, src = kc[:, :, :], bk[:, :].rearrange("p (a s) -> p a s", a=2)
                else:
                    dst = vaug[:, :].rearrange("p (n h c) -> p n h c", n=2, c=32)[:, :, :, 0:HDA]
                    src = bk[:, :].rearrange("p (n h c) -> p n h c", n=2, c=HDA)
                nc.scalar.activation(dst, src, ACT.Copy).then_inc(PA["evac_s"], 1)

        def project_a_gpsimd(b):
            for r in range(len(ROT)):
                nc.gpsimd.wait_ge(PA["evac_v"], b * len(BY_V) + BY_V.index(ROT[r]) + 1)
                if r == 0:
                    later(nc.gpsimd, AT[0]["placed"], b * PLACED_A)
                if r == 4:
                    nc.gpsimd.wait_ge(PA["placed_k"], b * PLACED_K + PLACED_K)
                t = rt[:, r % 2, :, :, :]
                nc.gpsimd.tensor_tensor(stage[:, r % 4, 0, :], t[:, 0, 0, :], t[:, 1, 1, :], ALU.subtract)
                nc.gpsimd.tensor_tensor(stage[:, r % 4, 1, :], t[:, 0, 1, :], t[:, 1, 0, :], ALU.add).then_inc(PA["summed"], 1)

        def place_a_sync(b):
            later(nc.sync, AT[0]["shifted"], b * 3 * GA)
            for r in range(len(ROT)):
                nc.sync.wait_ge(PA["summed"], b * len(ROT) + r + 1)
                dst, s, g = (kst, PA["placed_k"], r) if r < 4 else (qst, AT[0]["placed"], r - 4)
                for a in range(2):
                    for j in range(4):
                        nc.sync.dma_start(dst[32 + 32 * a:64 + 32 * a, 4 * g + j, :],
                                          stage[32 * j:32 * j + 32, r % 4, a, :]).then_inc(s, 16)
                if r == 3:
                    for i, dst, src in ((6, qst, qc), (7, kst, kc)):
                        wait_item(nc.sync, b, i)
                        for j in range(8):
                            nc.sync.dma_start(dst[0:16, j:16:8, :], src[16 * j:16 * j + 16, :, :]).then_inc(AT[0]["placed"], 16)

        PLACED_B = 16 * 2 * PARTS * PARTS * 2

        def project_b_tensor():
            s = PB
            for i in range(B + 1):
                bk = BK[i % 2]
                if i >= 2:
                    nc.tensor.wait_ge(s["prod"], i - 1)
                for a in range(2):
                    if i < B:
                        for kk in range(KD):
                            last = nc.tensor.matmul(bk[:, a * S:(a + 1) * S], wqb[:, kk, a * P:(a + 1) * P],
                                                    xnT[:, kk, i * S:(i + 1) * S], start=kk == 0, stop=kk == KD - 1)
                    else:
                        for b in range(B):
                            for kk in range(KD):
                                last = nc.tensor.matmul(bk[32 * b:32 * b + 32, a * S:(a + 1) * S],
                                                        wkvb[:, kk, a * 32:(a + 1) * 32], xnT[:, kk, b * S:(b + 1) * S],
                                                        start=kk == 0, stop=kk == KD - 1,
                                                        tile_position=(0, 32 * b), skip_group_check=True)
                last.then_inc(s["item"], 1)
            for t in range(NT):
                for kk in range(KD):
                    last = nc.tensor.matmul(BK[2][:, t * 64:(t + 1) * 64], xnT[:, kk, t * P:(t + 1) * P],
                                            wkvb[:, kk, 64:128], start=kk == 0, stop=kk == KD - 1)
            last.then_inc(s["item"], 1)

        def project_b_vector():
            s = PB
            nc.vector.memset(R2[64:RBZ, 0:5120], 0.0).then_inc(s["zeroed"], 1)
            for i in range(B + 1):
                bk = BK[i % 2][:, :].rearrange("p (a s) -> p a s", a=2)
                nc.vector.wait_ge(s["item"], i + 1)
                later(nc.vector, s["summed"], i)
                nc.vector.tensor_tensor(rtb[:, 0, :, :], bk, rope[:, 0, None, :].broadcast_to([P, 2, S]), ALU.mult)
                nc.vector.tensor_tensor(rtb[:, 1, :, :], bk, rope[:, 1, None, :].broadcast_to([P, 2, S]),
                                        ALU.mult).then_inc(s["prod"], 1)
                nc.vector.wait_ge(s["summed"], i + 1)
                if i > 0:
                    nc.vector.wait_ge(s["stored"], 16 * 2 * PARTS * i)
                nc.vector.tensor_copy(qparts[:, 0, :, :], rsb[:, :, :]).then_inc(s["hi"], 1)
                nc.vector.wait_ge(s["hi"], i + 1)
                nc.vector.tensor_tensor(rem[:, :, :], rsb[:, :, :], qparts[:, 0, :, :], ALU.subtract).then_inc(s["rest"], 1)
                nc.vector.wait_ge(s["rest"], i + 1)
                nc.vector.tensor_copy(qparts[:, 1, :, :], rem[:, :, :]).then_inc(s["mid"], 1)
                nc.vector.wait_ge(s["mid"], i + 1)
                nc.vector.tensor_tensor(qparts[:, 2, :, :], rem[:, :, :], qparts[:, 1, :, :], ALU.subtract).then_inc(s["lo"], 1)

        def project_b_gpsimd():
            s = PB
            for i in range(B + 1):
                nc.gpsimd.wait_ge(s["prod"], i + 1)
                later(nc.gpsimd, s["lo"], i)
                nc.gpsimd.tensor_tensor(rsb[:, 0, :], rtb[:, 0, 0, :], rtb[:, 1, 1, :], ALU.subtract)
                nc.gpsimd.tensor_tensor(rsb[:, 1, :], rtb[:, 0, 1, :], rtb[:, 1, 0, :], ALU.add).then_inc(s["summed"], 1)

        def project_b_scalar():
            nc.scalar.wait_ge(PB["item"], B + 2)
            nc.scalar.activation(vall[:, :, :], BK[2][:, :].rearrange("p (t n) -> p t n", t=NT), ACT.Copy).then_inc(PB["vall"], 1)

        def values_b_scalar(b):
            va = vaug[:, 0:2 * KVB * 32].rearrange("p (n h c) -> p n h c", n=2, c=32)
            nc.scalar.wait_ge(PB["vall"], 1)
            later(nc.scalar, AT[2]["pv"], b * GB)
            nc.scalar.activation(va[:, :, :, 0:HDB], vall[:, bass.ds(2 * b, 2), :].rearrange("p n (h c) -> p n h c", c=HDB),
                                 ACT.Copy).then_inc(AT[2]["values"], 1)

        def store_b_sync():
            for i in range(B + 1):
                nc.sync.wait_ge(PB["lo"], i + 1)
                for n in range(PARTS):
                    for a in range(2):
                        if i < B:
                            dst = q_d[n, a, i].rearrange("h i s -> (h i) s")
                        else:
                            dst = k_d[n, a].rearrange("b h i s -> (b h i) s")
                        nc.sync.dma_start(dst, qparts[:, n, a, :]).then_inc(PB["stored"], 16)
            nc.sync.wait_ge(PB["stored"], 16 * 2 * PARTS * (B + 1))
            nc.sync.wait_ge(PB["zeroed"], 1)

        def place_b_sync(b):
            later(nc.sync, AT[2]["shifted"], b * 3 * GB)
            for n in range(PARTS):
                for m in range(PARTS):
                    for a in range(2):
                        r = (n * PARTS + m) * HDB + a * (HDB // 2)
                        for dst, src in ((qsb, q_d[n, a, bass.ds(b, 1)]), (ksb, k_d[m, a, bass.ds(b, 1)])):
                            nc.sync.dma_start(dst[r:r + HDB // 2, :, :],
                                              src.rearrange("o h i s -> (o i) h s")).then_inc(AT[2]["placed"], 16)

        def route_tensor(l):
            s = FF[l]
            for t in range(NT):
                for kk in range(KD):
                    last = nc.tensor.matmul(BK[7][:, t * E:(t + 1) * E], xnT[:, kk, t * P:(t + 1) * P], rw[:, kk, :],
                                            start=kk == 0, stop=kk == KD - 1)
            last.then_inc(s["logits"], 1)
            nc.tensor.wait_ge(s["count"], 1)
            for t in range(NT + 1):
                for u in range(t + 1) if t < NT else range(NT):
                    if t < NT:
                        lhsT = tri if u == t else onesb
                        stop = u == t
                    else:
                        lhsT, stop = onesb, u == NT - 1
                    last = nc.tensor.matmul(BK[6][:, t * E:(t + 1) * E], lhsT[:, :], cnt[:, u * E:(u + 1) * E],
                                            start=u == 0, stop=stop)
            last.then_inc(s["rank1"], 1)

        owned = {1: 0, 3: 0}

        def route_vector(l):
            s = FF[l]
            v = nc.vector

            def link(*ops):
                for op in ops:
                    op.then_inc(s["own"], 1)
                owned[l] += len(ops)
                v.wait_ge(s["own"], owned[l])

            v.wait_ge(s["consts"], 16 * 4)
            v.wait_ge(s["logits"], 1)
            link(v.tensor_copy(lg, BK[7][:, 0:NT * E].rearrange("p (t e) -> p t e", t=NT)))
            link(*[v.max(mx[:, t, :], lg[:, t, :]) for t in range(NT)])
            v.tensor_tensor(dlt, mx[:, :, 1], mx[:, :, 0], ALU.subtract).then_inc(s["dlt"], 1)
            link(*[v.max_index(mi[:, t, :], mx[:, t, :], lg[:, t, :]) for t in range(NT)])
            link(v.tensor_copy(idf, mi[:, :, 0:2].rearrange("p t k -> p k t")))
            link(*[v.tensor_tensor(oh[:, k, :, :], small[:, None, 0:E].broadcast_to([P, NT, E]),
                                   idf[:, k, :, None].broadcast_to([P, NT, E]), ALU.is_equal) for k in range(TOPK)])
            v.tensor_tensor(cnt.rearrange("p (t e) -> p t e", t=NT), oh[:, 0, :, :], oh[:, 1, :, :], ALU.add).then_inc(s["count"], 1)
            v.wait_ge(s["exp1"], 1)
            link(v.tensor_scalar_add(den, ex1, 1.0))
            link(v.reciprocal(w01[:, 0, :], den))
            link(v.tensor_tensor(w01[:, 1, :], ex1, w01[:, 0, :], ALU.mult))
            v.wait_ge(s["rank1"], 1)
            link(v.tensor_tensor(cmp, BK[6][:, NT * E:(NT + 1) * E, None].broadcast_to([P, E, 8]),
                                 small[:, 8:72].rearrange("p (e j) -> p e j", e=E), ALU.is_gt))
            link(v.tensor_reduce(ntl, cmp, AX, ALU.add))
            link(v.tensor_tensor(cmp, ntl[:, None, :].broadcast_to([P, E, E]),
                                 small[:, 72:136].rearrange("p (e j) -> p e j", e=E), ALU.mult))
            link(v.tensor_reduce(base, cmp, AX, ALU.add))
            link(v.scalar_tensor_tensor(out=posb, in0=base[:, None, :].broadcast_to([P, NT, E]), scalar=float(P),
                                        in1=BK[6][:, 0:NT * E].rearrange("p (t e) -> p t e", t=NT),
                                        op0=ALU.mult, op1=ALU.add))
            link(v.tensor_tensor(ohp, oh, posb[:, None, :, :].broadcast_to([P, 2, NT, E]), ALU.mult))
            link(v.tensor_reduce(slf.rearrange("p (k t) -> p k t", k=2), ohp, AX, ALU.add))
            v.tensor_copy(slot, slf).then_inc(s["slot"], 1)
            link(v.tensor_tensor(ecm, small[0:1, 136:160, None].broadcast_to([1, 24, 7]),
                                 base[0:1, None, 1:E].broadcast_to([1, 24, 7]), ALU.is_ge))
            link(v.tensor_reduce(eidf, ecm, AX, ALU.add))
            v.tensor_copy(eid, eidf).then_inc(s["eid"], 1)

        def route_scalar(l):
            s = FF[l]
            nc.scalar.wait_ge(s["dlt"], 1)
            nc.scalar.activation(ex1, dlt, ACT.Exp).then_inc(s["exp1"], 1)

        def scatter_gpsimd(l):
            s = FF[l]
            nc.gpsimd.wait_ge(s["slot"], 1)
            nc.gpsimd.wait_ge(LN[l]["normed"], NT)
            if l == 1:
                nc.gpsimd.wait_ge(s_zero, 16)
            for t in range(NT):
                for k in range(TOPK):
                    nc.gpsimd.indirect_dma_start(
                        xs_d[:, :], bass.IndirectOffsetOnAxis(ap=slot[:, k * NT + t:k * NT + t + 1], axis=0),
                        xn[:, t, :], None).then_inc(s["scatter"], 16)

        def load_tile(l, i, n, p):
            s = FF[l]
            nc.sync.dma_start(xs[:, p, :], xs_d[bass.ds(i * P, P), :]).then_inc(s[f"xs{p}"], 16)

        def tile_sync(l, i, n, p, load):
            s = FF[l]
            if load:
                nc.sync.wait_ge(s["x_t"], i + 1)
                load_tile(l, i + 2, n + 1, p)
            nc.sync.wait_ge(s["y_e"], i + 1)
            nc.sync.dma_start(ys_d[bass.ds(i * P, P), :], yo[:, p, :]).then_inc(s[f"ys{p}"], 16)

        def tile_transpose(l, i, n, p):
            s = FF[l]
            nc.tensor.wait_ge(s[f"xs{p}"], 16 * (n + 1))
            later(nc.tensor, s["x_e"], i)
            for kk in range(KD):
                last = nc.tensor.transpose(BK[6][:, kk * P:(kk + 1) * P], xs[:, p, kk * P:(kk + 1) * P], ident[:, :])
            last.then_inc(s["x_t"], 1)

        def tile_up(l, i, n, p):
            s = FF[l]
            e = nc.tensor.value_load(eid[0:1, bass.ds(i, 1)], min_val=0, max_val=E - 1)
            nc.tensor.wait_ge(s["x_e"], i + 1)
            for half in range(2):
                later(nc.tensor, s["hid"], 2 * i)
                for gu in range(2):
                    for kk in range(KD):
                        last = nc.tensor.matmul(BK[2 * half + gu][:, 0:IH], xsT[:, p, kk, :],
                                                wgu[:, bass.ds(e * (KD * GU) + (kk * GU + gu * I + half * IH), IH)],
                                                start=kk == 0, stop=kk == KD - 1)
                    last.then_inc(s["gu"], 1)
            return e

        def tile_hidden(l, i, n, p):
            s = FF[l]
            nc.tensor.wait_ge(s["hid"], 2 * i + 2)
            later(nc.tensor, s["hte_v"], i)
            later(nc.tensor, s["hte_s"], i)
            for c in range(6):
                last = nc.tensor.transpose(BK[4 + c // 4][0:CH[c], (c % 4) * P:(c % 4 + 1) * P],
                                           hh[:, CO[c]:CO[c] + CH[c]], ident[:, :])
                if c in (3, 5):
                    last.then_inc(s["hid_t"], 1)

        def tile_down(l, i, n, p):
            s = FF[l]
            e = nc.tensor.value_load(eid[0:1, bass.ds(i, 1)], min_val=0, max_val=E - 1)
            nc.tensor.wait_ge(s["hte_v"], i + 1)
            nc.tensor.wait_ge(s["hte_s"], i + 1)
            later(nc.tensor, s["y_e"], i)
            for c in range(6):
                last = nc.tensor.matmul(BK[7][:, 0:D], hT[0:CH[c], p, c, :],
                                        wd[0:CH[c], bass.ds(e * (6 * D) + c * D, D)], start=c == 0, stop=c == 5)
            last.then_inc(s["down"], 1)

        def tile_scalar(l, i, n, p):
            s = FF[l]
            a = nc.scalar
            a.wait_ge(s["x_t"], i + 1)
            later(a, s["gu"], 4 * n)
            a.activation(xsT[:, p, :, :], BK[6][:, 0:S].rearrange("p (k s) -> p k s", k=KD), ACT.Copy).then_inc(s["x_e"], 1)
            for half in range(2):
                a.wait_ge(s["gu"], 4 * i + 2 * half + 1)
                later(a, s["hid"], 2 * i)
                a.activation(sg[:, half * IH:(half + 1) * IH], BK[2 * half][:, 0:IH], ACT.Silu).then_inc(s["silu"], 1)

        def tile_scalar_2(l, i, n, p):
            s = FF[l]
            a = nc.scalar
            a.wait_ge(s["hid_t"], 2 * i + 2)
            a.activation(hT[0:CH[5], p, 4:6, :], BK[5][0:CH[5], 0:2 * P].rearrange("p (c s) -> p c s", c=2),
                         ACT.Copy).then_inc(s["hte_s"], 1)

        def tile_scalar_y(l, i, n, p):
            s = FF[l]
            a = nc.scalar
            a.wait_ge(s["down"], i + 1)
            later(a, s[f"ys{p}"], 16 * n)
            a.activation(yo[:, p, :], BK[7][:, 0:D], ACT.Copy).then_inc(s["y_e"], 1)

        def tile_vector(l, i, n, p):
            s = FF[l]
            v = nc.vector
            for half in range(2):
                v.wait_ge(s["silu"], 2 * i + half + 1)
                v.wait_ge(s["gu"], 4 * i + 2 * half + 2)
                later(v, s["hid_t"], 2 * i)
                v.tensor_tensor(hh[:, half * IH:(half + 1) * IH], sg[:, half * IH:(half + 1) * IH],
                                BK[2 * half + 1][:, 0:IH], ALU.mult).then_inc(s["hid"], 1)
            v.wait_ge(s["hid_t"], 2 * i + 1)
            v.tensor_copy(hT[:, p, 0:4, :], BK[4][0:CH[0], :].rearrange("p (c s) -> p c s", c=4)).then_inc(s["hte_v"], 1)

        def experts_tensor(l):
            s = FF[l]
            nc.tensor.wait_ge(s["eid"], 1)
            nc.tensor.wait_ge(s_wgu, 16 * E)

            def step(i, n, p, nxt):
                if nxt:
                    tile_transpose(l, i + 1, n + p, 1 - p)
                tile_up(l, i, n, p)
                tile_down(l, i - 1, n + p - 1, 1 - p)
                tile_hidden(l, i, n, p)

            tile_transpose(l, 0, 0, 0)
            tile_transpose(l, 1, 0, 1)
            tile_up(l, 0, 0, 0)
            tile_hidden(l, 0, 0, 0)
            nc.tensor.wait_ge(s_wd, 32 * E)
            step(1, 0, 1, True)
            step(2, 1, 0, True)
            with nc.tensor.Fori(1, (SLOTS_T - 3) // 2) as r:
                step(2 * r + 1, r, 1, True)
                step(2 * r + 2, r + 1, 0, True)
            step(SLOTS_T - 2, (SLOTS_T - 2) // 2, 1, True)
            step(SLOTS_T - 1, (SLOTS_T - 1) // 2, 0, False)
            tile_down(l, SLOTS_T - 1, (SLOTS_T - 1) // 2, 0)

        def experts_scalar(l):
            def step(i, n, p):
                tile_scalar(l, i, n, p)
                tile_scalar_y(l, i - 1, n + p - 1, 1 - p)
                tile_scalar_2(l, i, n, p)

            tile_scalar(l, 0, 0, 0)
            tile_scalar_2(l, 0, 0, 0)
            step(1, 0, 1)
            step(2, 1, 0)
            with nc.scalar.Fori(1, (SLOTS_T - 1) // 2) as r:
                step(2 * r + 1, r, 1)
                step(2 * r + 2, r + 1, 0)
            tile_scalar_y(l, SLOTS_T - 1, (SLOTS_T - 1) // 2, 0)

        def experts_vector(l):
            tile_vector(l, 0, 0, 0)
            with nc.vector.Fori(0, (SLOTS_T - 1) // 2) as r:
                tile_vector(l, 2 * r + 1, r, 1)
                tile_vector(l, 2 * r + 2, r + 1, 0)

        def experts_sync(l):
            s = FF[l]
            nc.sync.wait_ge(s["scatter"], 16 * TOPK * NT)
            load_tile(l, 0, 0, 0)
            load_tile(l, 1, 0, 1)
            with nc.sync.Fori(0, (SLOTS_T - 3) // 2) as r:
                tile_sync(l, 2 * r, r, 0, True)
                tile_sync(l, 2 * r + 1, r, 1, True)
            tile_sync(l, SLOTS_T - 3, (SLOTS_T - 3) // 2, 0, True)
            tile_sync(l, SLOTS_T - 2, (SLOTS_T - 2) // 2, 1, False)
            tile_sync(l, SLOTS_T - 1, (SLOTS_T - 1) // 2, 0, False)

        def gather_gpsimd(l):
            s = FF[l]
            nc.gpsimd.wait_ge(s["ys0"], 16 * ((SLOTS_T + 1) // 2))
            nc.gpsimd.wait_ge(s["ys1"], 16 * (SLOTS_T // 2))
            for t in range(NT):
                if t >= 4:
                    nc.gpsimd.wait_ge(s["added"], t - 3)
                for k in range(TOPK):
                    nc.gpsimd.indirect_dma_start(
                        yg[:, t % 4, k, :], None, ys_d[:, :],
                        bass.IndirectOffsetOnAxis(ap=slot[:, k * NT + t:k * NT + t + 1], axis=0)
                    ).then_inc(s[f"g{t % 4}"], 16)

        def combine_vector(l):
            s = FF[l]
            for t in range(NT):
                nc.vector.wait_ge(s[f"g{t % 4}"], 32 * (t // 4 + 1))
                nc.vector.scalar_tensor_tensor(out=xres[:, t, :], in0=yg[:, t % 4, 0, :], scalar=w01[:, 0, t:t + 1],
                                               in1=xres[:, t, :], op0=ALU.mult, op1=ALU.add).then_inc(s["own"], 1)
                owned[l] += 1
                nc.vector.wait_ge(s["own"], owned[l])
                nc.vector.scalar_tensor_tensor(out=xres[:, t, :], in0=yg[:, t % 4, 1, :], scalar=w01[:, 1, t:t + 1],
                                               in1=xres[:, t, :], op0=ALU.mult, op1=ALU.add).then_inc(s["added"], 1)

        def route_consts_sync(l):
            s = FF[l]
            nc.sync.wait_ge(AT[l - 1]["projected"], B)
            for dst, src in ((tri.bitcast(U16), "tri"), (onesb.bitcast(U16), "onesb"), (small, "small"), (rw, "rw")):
                nc.sync.dma_start(dst, dr[src]).then_inc(s["consts"], 16)

        block = ctx.enter_context(nc.Block())

        @block.sync
        def _(sp):
            xd = dr["x"].rearrange("(t p) d -> p t d", p=P)
            for t in range(0, NT, 2):
                sp.dma_start(xres[:, t:t + 2, :], xd[:, t:t + 2, :]).then_inc(s_x, 16)
            for dst, src in ((ident[:, :], "ident"), (identb[:, :].bitcast(U16), "identb"), (masks[:, :, :].bitcast(U16), "masks"),
                             (sel[:, :].bitcast(U16), "sel"), (rope[:, :, :], "rope_a")):
                sp.dma_start(dst, dr[src]).then_inc(s_const, 16)
            for dst, src in ((wdq, "wdq"), (wdkv, "wdkv"), (wkr, "wkr"), (wuq, "wuq"), (wuk, "wuk"), (wuv, "wuv"),
                             (wqr, "wqr"), (woa, "woa")):
                sp.dma_start(dst, dr[src]).then_inc(s_wa, 16)
            sp.wait_ge(s_wa, 16 * 8)
            for e in range(E):
                sp.dma_start(wgu[:, e * KD * GU:(e + 1) * KD * GU].rearrange("p (k n) -> p k n", k=KD),
                             dr["wgu"][e].rearrange("(k p) n -> p k n", p=P)).then_inc(s_wgu, 16)
            for dst, src in ((wqb[:, :, :], "wqb"), (wkvb[:, :, :], "wkvb"), (wob[:, :, :], "wob")):
                sp.dma_start(dst, dr[src].rearrange("(k p) n -> p k n", p=P)).then_inc(s_wb, 16)
            sp.wait_ge(s_init, 3)
            place_a_sync(0)
            with sp.Fori(1, B) as b:
                place_a_sync(b)
            route_consts_sync(1)
            sp.wait_ge(AT[0]["shifted"], B * 3 * GA)
            wdv = R1[:, :].rearrange("p (e m) -> p e m", e=E)
            for e in range(E):
                sp.dma_start(wdv[0:CH[0], e, 0:4 * D], dr["wd4"][e]).then_inc(s_wd, 16)
                sp.dma_start(wdv[0:CH[5], e, 4 * D:6 * D], dr["wd2"][e]).then_inc(s_wd, 16)
            experts_sync(1)
            sp.wait_ge(PA["evac_v"], B * len(BY_V))
            sp.dma_start(rope[:, :, :], dr["rope_b"]).then_inc(s_const, 16)
            store_b_sync()
            place_b_sync(0)
            with sp.Fori(1, B) as b:
                place_b_sync(b)
            route_consts_sync(3)
            experts_sync(3)
            od = out.rearrange("(t p) d -> p t d", p=P)
            for t in range(NT):
                sp.wait_ge(FF[3]["added"], t + 1)
                sp.dma_start(od[:, t, :], xres[:, t, :]).then_inc(s_out, 16)
            sp.wait_ge(s_out, 16 * NT)

        @block.gpsimd
        def _(pool):
            pool.memset(PTR[:, :], 0.0).then_inc(s_init, 1)
            pool.memset(vaug[:, :], 1.0).then_inc(s_init, 1)
            pool.memset(R1[0:32, 0:2 * HA * S], 0.0).then_inc(s_init, 1)
            pool.wait_ge(s_init, 3)
            pool.dma_start(xs_d.rearrange("(n p) d -> p n d", p=P),
                           PTR[:, None, 0:D].broadcast_to([P, SLOTS_T, D])).then_inc(s_zero, 16)
            pool.wait_ge(s_zero, 16)
            project_a_gpsimd(0)
            with pool.Fori(1, B) as b:
                project_a_gpsimd(b)
            scatter_gpsimd(1)
            gather_gpsimd(1)
            pool.wait_ge(AT[0]["pv"], B * GA)
            pool.memset(vaug[:, :], 1.0).then_inc(s_init, 1)
            project_b_gpsimd()
            scatter_gpsimd(3)
            gather_gpsimd(3)

        @block.vector
        def _(dve):
            norm_vector(0, lambda t: (s_x, 16 * 4))
            dve.memset(nparts[:, :, :, :], 0.0)
            dve.wait_ge(s_const, 16 * 5)
            dve.wait_ge(s_zero, 16)
            project_a_vector(0)
            attend_vector(0, 0)
            with dve.Fori(1, B) as b:
                project_a_vector(b)
                attend_vector(0, b)
            norm_vector(1, lambda t: (AT[0]["added"], B))
            route_vector(1)
            experts_vector(1)
            combine_vector(1)
            norm_vector(2, lambda t: (FF[1]["added"], t + 1))
            dve.wait_ge(s_const, 16 * 6)
            project_b_vector()
            attend_vector(2, 0)
            with dve.Fori(1, B) as b:
                attend_vector(2, b)
            norm_vector(3, lambda t: (AT[2]["added"], B))
            route_vector(3)
            experts_vector(3)
            combine_vector(3)

        @block.scalar
        def _(act):
            norm_scalar(0)
            act.wait_ge(s_init, 2)
            project_a_scalar(0)
            attend_scalar(0, 0)
            with act.Fori(1, B) as b:
                project_a_scalar(b)
                attend_scalar(0, b)
            norm_scalar(1)
            route_scalar(1)
            experts_scalar(1)
            norm_scalar(2)
            project_b_scalar()
            act.wait_ge(s_init, 4)
            values_b_scalar(0)
            attend_scalar(2, 0)
            with act.Fori(1, B) as b:
                values_b_scalar(b)
                attend_scalar(2, b)
            norm_scalar(3)
            route_scalar(3)
            experts_scalar(3)

        @block.tensor
        def _(pe):
            pe.wait_ge(s_const, 16 * 5)
            norm_tensor(0)
            wait_normed(pe, 0)
            pe.wait_ge(s_wa, 16 * 8)
            project_a_tensor(0)
            attend_tensor(0, 0)
            with pe.Fori(1, B) as b:
                project_a_tensor(b)
                attend_tensor(0, b)
            norm_tensor(1)
            wait_normed(pe, 1)
            pe.wait_ge(FF[1]["consts"], 16 * 4)
            route_tensor(1)
            experts_tensor(1)
            norm_tensor(2)
            wait_normed(pe, 2)
            pe.wait_ge(s_wb, 16 * 3)
            project_b_tensor()
            attend_tensor(2, 0)
            with pe.Fori(1, B) as b:
                attend_tensor(2, b)
            norm_tensor(3)
            wait_normed(pe, 3)
            pe.wait_ge(FF[3]["consts"], 16 * 4)
            route_tensor(3)
            experts_tensor(3)


def kernel(**inputs):
    import concourse.bacc as bacc
    from concourse.bass_utils import run_bass_kernel_spmd

    a = {n: np.asarray(v) for n, v in inputs.items()}
    f = "L0_attn_a_"

    def rotated(w, k):
        w = w.reshape(GA, 4, 2, 32, -1).transpose(4, 0, 2, 1, 3).reshape(-1, HA * RD)
        return w.reshape(k, -1, HA * RD).transpose(1, 0, 2)

    def chunked(w, k):
        return w.T.reshape(k, -1, w.shape[0]).transpose(1, 0, 2)

    def even_odd(w, h):
        return w.reshape(D, h, HDB // 2, 2).transpose(0, 3, 1, 2).reshape(D, -1)

    down = a["L0_ffn_Wd"].transpose(0, 2, 1)
    arrays = {
        "x": a[f + "x"].reshape(T, D),
        "wdq": chunked(a[f + "w_dq"], KD), "wdkv": chunked(a[f + "w_dkv"], KD),
        "wuq": chunked(a[f + "w_uq"], 2), "wqr": rotated(a[f + "w_qr"], 2), "wkr": rotated(a[f + "w_kr"], KD),
        "wuk": a[f + "w_uk"].T, "wuv": a[f + "w_uv"].T, "woa": chunked(a[f + "w_out"], KD),
        "wqb": even_odd(a["L0_attn_b_Wq"], HB),
        "wkvb": np.concatenate([even_odd(a["L0_attn_b_Wk"], KVB), a["L0_attn_b_Wv"]], 1),
        "wob": a["L0_attn_b_Wo"],
        "rw": chunked(a["L0_ffn_router_w"], KD),
        "wgu": np.concatenate([a["L0_ffn_Wg"].transpose(0, 2, 1), a["L0_ffn_Wu"].transpose(0, 2, 1)], 2),
        "wd4": down[:, 0:CO[4]].reshape(E, 4, CH[0], D).transpose(0, 2, 1, 3).reshape(E, CH[0], 4 * D),
        "wd2": down[:, CO[4]:I].reshape(E, 2, CH[5], D).transpose(0, 2, 1, 3).reshape(E, CH[5], 2 * D),
        **shape_constants(),
    }
    arrays = {n: np.ascontiguousarray(v) for n, v in arrays.items()}
    nc = bacc.Bacc("TRN2", target_bir_lowering=False, num_devices=1)
    dr = {n: nc.dram_tensor(f"in_{n}", v.shape, mybir.dt.from_np(v.dtype), kind="ExternalInput").ap()
          for n, v in arrays.items()}
    out = nc.dram_tensor("out", [T, D], F32, kind="ExternalOutput").ap()
    build_hybrid(nc, dr, out)
    r = run_bass_kernel_spmd(nc, [{f"in_{n}": v for n, v in arrays.items()}], core_ids=[0])
    return r.results[0]["out"].reshape(B, S, D)
```

```python
import math
from contextlib import ExitStack

import numpy as np

import concourse.bass as bass
from concourse import mybir

F32 = mybir.dt.float32
BF16 = mybir.dt.bfloat16
U16 = mybir.dt.uint16
I32 = mybir.dt.int32
U32 = mybir.dt.uint32
ALU = mybir.AluOpType
ACT = mybir.ActivationFunctionType
AX = mybir.AxisListType.X

P = 128
B, S, D = 4, 256, 256
T = B * S
NT = T // P
KD = D // P
EPS = 1e-5

HA, HDA, RD, CQ, CKV = 16, 16, 64, 192, 64
HB, HDB, KVB = 32, 8, 8
GA, GB = HA // 4, HB // 4
SCALE_A = 1.0 / math.sqrt(HDA + RD)
SCALE_B = 1.0 / math.sqrt(HDB)
CQH = CQ // 2
RA = 96
PARTS = 3
RB = PARTS * PARTS * HDB
RBZ = 96
NEG = -1e30

E, I, TOPK = 8, 688, 2
IH = I // 2
GU = 2 * I
CH = [115, 115, 115, 115, 114, 114]
CO = [0, 115, 230, 345, 460, 574]
ROUTED = T * TOPK
SLOTS_T = (ROUTED - E) // P + E
SLOTS = SLOTS_T * P


def shape_constants():
    def bf16(x):
        return (np.ascontiguousarray(x, dtype=np.float32).view(np.uint32) >> 16).astype(np.uint16)

    pos = np.arange(S, dtype=np.float32)
    fa = (1.0 / np.float32(10000.0) ** (np.arange(0, RD, 2, dtype=np.float32) / np.float32(RD))).astype(np.float32)
    aa = (pos[:, None] * fa[None, :]).astype(np.float32).T
    rope_a = np.stack([np.tile(np.cos(aa), (4, 1)), np.tile(np.sin(aa), (4, 1))], 1).astype(np.float32)
    fb = (1.0 / np.float32(10000.0) ** (np.arange(HDB // 2, dtype=np.float32) / np.float32(HDB // 2))).astype(np.float32)
    ab = (pos[:, None] * fb[None, :]).astype(np.float32).T
    rope_b = np.stack([np.repeat(np.cos(ab), HB, 0), np.repeat(np.sin(ab), HB, 0)], 1).astype(np.float32)
    rope_k = np.stack([np.tile(np.repeat(f(ab), KVB, 0), (B, 1)) for f in (np.cos, np.sin)], 1).astype(np.float32)
    q = np.arange(P)
    diag = np.where(q[None, :] > q[:, None], NEG, 0.0)
    none = np.zeros((P, P))
    masks = np.stack([np.concatenate([none, diag], 1), np.concatenate([diag.T, none], 1)], 1)
    sel = np.arange(PARTS * 32)[:, None] % 32 == np.arange(32)[None, :]
    tri = q[:, None] < q[None, :]
    e = np.arange(E, dtype=np.float32)
    small = np.concatenate([
        e,
        np.repeat(e[:, None], E, 1).T.reshape(-1) * P,
        (e[None, :] < e[:, None]).astype(np.float32).reshape(-1),
        np.arange(24, dtype=np.float32),
    ]).astype(np.float32)
    small = np.broadcast_to(small, (P, small.size)).copy()
    return {"rope_a": rope_a, "rope_b": rope_b, "rope_k": rope_k, "masks": bf16(masks), "sel": bf16(sel), "tri": bf16(tri),
            "ident": np.eye(P, dtype=np.float32), "identb": bf16(np.eye(P)),
            "onesb": bf16(np.ones((P, P))), "small": small}


def build_hybrid(nc, dr, out):
    ctx = ExitStack()
    with ctx:
        def sb(name, shape, dt):
            return ctx.enter_context(nc.sbuf_tensor(name, shape, dt))

        def sem(name):
            return ctx.enter_context(nc.semaphore(name))

        wgu = sb("wgu", [P, E * KD * GU], F32)
        R1 = sb("R1", [P, E * 6 * D], F32)
        R2 = sb("R2", [P, 6144], F32)
        xres = sb("xres", [P, NT, D], F32)
        XN = sb("XN", [P, NT * D], F32)
        xnT = sb("xnT", [P, KD, T], F32)
        PTR = sb("PTR", [P, 2 * 3 * 512], F32)
        wqb = sb("wqb", [P, KD, D], F32)
        wkvb = sb("wkvb", [P, KD, 2 * KVB * HDB], F32)
        wob = sb("wob", [P, KD, D], F32)
        vaug = sb("vaug", [P, 2 * HA * 32], F32)
        rope = sb("rope", [P, 2, S], F32)
        ident = sb("ident_sb", [P, P], F32)
        identb = sb("identb_sb", [P, P], BF16)
        masks = sb("masks_sb", [P, 2, 2 * P], BF16)
        sel = sb("sel_sb", [PARTS * 32, 32], BF16)
        xn = XN[:, :].rearrange("p (t d) -> p t d", t=NT)
        wd = R1[0:CH[0], :]

        def room(o, n):
            return wgu[:, o:o + n]

        ODD = 5 * KD * GU
        stacks = [(R1[0:RA, 0:HA * S], R1[0:RA, HA * S:2 * HA * S]),
                  (room(ODD, HA * S)[0:RA, :], room(ODD + HA * S, HA * S)[0:RA, :])]
        qst, kst = ([st[i].rearrange("p (h s) -> p h s", h=HA) for st in stacks] for i in range(2))
        o = 2 * HA * S
        stage = [R1[:, o + i * 2048:o + (i + 1) * 2048].rearrange("p (n a s) -> p n a s", n=4, a=2) for i in range(2)]
        o = 3 * KD * GU
        qc = room(o, 2 * S).rearrange("p (a s) -> p a s", a=2); o += 2 * S
        kc = room(o, 2 * S).rearrange("p (a s) -> p a s", a=2); o += 2 * S
        cqT = room(o, 2 * S)[0:CQH, :].rearrange("p (a s) -> p a s", a=2); o += 2 * S
        ckvT = room(o, S)[0:CKV, :]; o += S
        rt = room(o, 2048).rearrange("p (n c a s) -> p n c a s", n=2, c=2, a=2); o += 2048
        vaug2 = room(o, 2 * HA * 32); o += 2 * HA * 32
        assert o <= ODD
        o = 0
        wdq = R2[:, o:o + KD * CQ].rearrange("p (k n) -> p k n", k=KD); o += KD * CQ
        wdkv = R2[:, o:o + KD * CKV].rearrange("p (k n) -> p k n", k=KD); o += KD * CKV
        wuq = R2[0:CQH, o:o + 2 * D].rearrange("p (k n) -> p k n", k=2); o += 2 * D
        wqr = R2[0:CQH, o:o + 2 * HA * RD].rearrange("p (k n) -> p k n", k=2); o += 2 * HA * RD
        wkr = R2[:, o:o + KD * HA * RD].rearrange("p (k n) -> p k n", k=KD); o += KD * HA * RD
        wuk = R2[0:CKV, o:o + D]; o += D
        wuv = R2[0:CKV, o:o + D]; o += D
        woa = R2[:, o:o + KD * D].rearrange("p (k n) -> p k n", k=KD); o += KD * D
        assert o == 6144
        PT = PTR[:, :].rearrange("p (n b s) -> p n b s", n=2, b=3)
        oun = XN[:, 0:512].rearrange("p (n s) -> p n s", n=2)
        otok = XN[:, 512:1024].rearrange("p (q d) -> p q d", q=2)
        oT = XN[:, 1024:1536].rearrange("p (k s) -> p k s", k=2)
        nmax = XN[:, 1536:1600].rearrange("p (q h) -> p q h", q=2)
        nrem = XN[:, 1600:1664].rearrange("p (q h) -> p q h", q=2)
        rec = XN[:, 1664:1672].rearrange("p (q j) -> p q j", q=2)
        nparts = XN[:, 1672:1768].bitcast(BF16).rearrange("p (q n h) -> p q n h", q=2, n=PARTS)
        npartf = XN[:, 1672:1768].bitcast(BF16).rearrange("p (q m) -> p q m", q=2)
        nT = XN[0:PARTS * 32, 1768:1896].bitcast(BF16)
        stat = sb("stat", [P, 112], F32)
        bst = stat[:, 0:NT * 6].rearrange("p (t n) -> p t n", t=NT)
        mv = stat[:, 48:48 + NT * 2].rearrange("p (t n) -> p t n", t=NT)
        var = stat[:, 64:72]
        std = stat[:, 72:80]
        rstd = stat[:, 80:88]
        slot = stat[:, 88:104].bitcast(I32)
        w01 = sb("w01", [P, 2, NT], F32)
        o = 0
        xs = R2[:, o:o + 512].rearrange("p (n d) -> p n d", n=2); o += 512
        xsT = R2[:, o:o + 512].rearrange("p (n k s) -> p n k s", n=2, k=KD); o += 512
        sg = R2[:, o:o + I]; o += I
        hh = R2[:, o:o + I]; o += I
        hT = R2[0:CH[0], o:o + 2 * 6 * P].rearrange("p (n c s) -> p n c s", n=2, c=6); o += 2 * 6 * P
        yo = R2[:, o:o + 512].rearrange("p (n d) -> p n d", n=2); o += 512
        rw = R2[:, o:o + KD * E].rearrange("p (k e) -> p k e", k=KD); o += KD * E
        lg = R2[:, o:o + 64].rearrange("p (t e) -> p t e", t=NT); o += 64
        mx = R2[:, o:o + 64].rearrange("p (t e) -> p t e", t=NT); o += 64
        mi = R2[:, o:o + 64].bitcast(U32).rearrange("p (t e) -> p t e", t=NT); o += 64
        idf = R2[:, o:o + 16].rearrange("p (k t) -> p k t", k=2); o += 16
        oh = R2[:, o:o + 128].rearrange("p (k t e) -> p k t e", k=2, t=NT); o += 128
        ohp = R2[:, o:o + 128].rearrange("p (k t e) -> p k t e", k=2, t=NT); o += 128
        cnt = R2[:, o:o + 32].bitcast(BF16); o += 32
        cmp = R2[:, o:o + 64].rearrange("p (e j) -> p e j", e=E); o += 64
        ntl = R2[:, o:o + E]; o += E
        base = R2[:, o:o + E]; o += E
        posb = R2[:, o:o + 64].rearrange("p (t e) -> p t e", t=NT); o += 64
        slf = R2[:, o:o + 16]; o += 16
        ecm = R2[0:1, o:o + 24 * 7].rearrange("p (i e) -> p i e", e=7); o += 168
        eidf = R2[0:1, o:o + 24]; o += 24
        eid = R2[0:1, o:o + 24].bitcast(I32); o += 24
        dlt = R2[:, o:o + NT]; o += NT
        ex1 = R2[:, o:o + NT]; o += NT
        den = R2[:, o:o + NT]; o += NT
        tri = R2[:, o:o + 64].bitcast(BF16); o += 64
        onesb = R2[:, o:o + 64].bitcast(BF16); o += 64
        small = R2[:, o:o + 160]; o += 160
        assert o <= 6144, o
        yg = PTR[:, 0:2048].rearrange("p (n k d) -> p n k d", n=4, k=2)
        qsb = R2[0:RBZ, 0:HB * S // 2].bitcast(BF16).rearrange("p (h s) -> p h s", h=HB)
        ksb = R2[0:RBZ, 4096:4096 + KVB * S // 2].bitcast(BF16).rearrange("p (h s) -> p h s", h=KVB)
        vall = R2[:, 5120:5120 + NT * 64].rearrange("p (t n) -> p t n", t=NT)
        rtb = PTR[:, 0:2048].rearrange("p (m c a s) -> p m c a s", m=2, c=2, a=2)
        rsb = PTR[:, 2048:3072].rearrange("p (m a s) -> p m a s", m=2, a=2)
        rem = XN[:, 0:512].rearrange("p (a s) -> p a s", a=2)
        qparts = XN[:, 512:2048].bitcast(BF16).rearrange("p (m n a s) -> p m n a s", m=2, n=PARTS, a=2)
        ropek = R2[:, 5632:6144].rearrange("p (c s) -> p c s", c=2)

        BK = [ctx.enter_context(nc.psum_tensor(f"bank{i}", [P, 512], F32)) for i in range(8)]

        xs_d = nc.dram_tensor("slots_in", [SLOTS, D], F32, kind="Internal").ap()
        ys_d = nc.dram_tensor("slots_out", [SLOTS, D], F32, kind="Internal").ap()
        q_d = nc.dram_tensor("q_parts", [B, PARTS * HDB, HB, S], BF16, kind="Internal").ap()
        k_d = nc.dram_tensor("k_parts", [B, PARTS * HDB, KVB, S], BF16, kind="Internal").ap()

        s_const = sem("s_const")
        s_x = sem("s_x")
        s_wa = sem("s_wa")
        s_wb = sem("s_wb")
        s_wgu = sem("s_wgu")
        s_wd = sem("s_wd")
        s_zero = sem("s_zero")
        s_init = sem("s_init")
        s_out = sem("s_out")


        def named(prefix, names):
            return {n: sem(f"{prefix}_{n}") for n in names.split()}

        LN = [named(f"ln{l}", "own vareps root normed transposed evac_s evac_v") for l in range(4)]
        AN = ("placed values scores maxima hi rest mid lo max_t max_e shifted exps pv pv_e out_t recips "
              "divided all_t all_e projected added")
        AT = {0: named("at0", AN), 2: named("at2", AN)}
        PA = named("pa", "item evac_s evac_v summed placed_k")
        PB = named("pb", "placed_2 item prod summed hi rest mid lo stored0 stored1 zeroed vall")
        FN = ("own consts logits count rank1 "
              "slot eid dlt exp1 scatter xs0 xs1 x_t x_e gu silu hid hid_t hte_v hte_s "
              "down y_e ys0 ys1 g0 g1 g2 g3 added")
        FF = {1: named("ff1", FN), 3: named("ff3", FN)}


        def later(eng, sem, count):
            if not (isinstance(count, int) and count == 0):
                eng.wait_ge(sem, count)

        def norm_vector(l, x_ready):
            s = LN[l]
            for t in range(NT):
                if x_ready is not None:
                    nc.vector.wait_ge(*x_ready(t))
                nc.vector.bn_stats(bst[:, t, :], xres[:, t, :]).then_inc(s["own"], 1)
            for t in range(NT):
                nc.vector.wait_ge(s["own"], t + 1)
                nc.vector.bn_aggr(mv[:, t, :], bst[:, t, :]).then_inc(s["own"], 1)
            nc.vector.wait_ge(s["own"], 2 * NT)
            nc.vector.tensor_scalar_add(var, mv[:, :, 1], EPS).then_inc(s["vareps"], 1)
            nc.vector.wait_ge(s["root"], 1)
            nc.vector.reciprocal(rstd, std).then_inc(s["own"], 1)
            nc.vector.wait_ge(s["own"], 2 * NT + 1)
            for t in range(NT):
                nc.vector.tensor_scalar(xn[:, t, :], xres[:, t, :], mv[:, t, 0:1], rstd[:, t:t + 1],
                                        ALU.subtract, ALU.mult).then_inc(s["normed"], 1)
            for t in range(1, NT, 2):
                nc.vector.wait_ge(s["transposed"], t + 1)
                nc.vector.tensor_copy(xnT[:, :, t * P:(t + 1) * P],
                                      BK[t % 4][:, 0:KD * P].rearrange("p (k s) -> p k s", k=KD)
                                      ).then_inc(s["evac_v"], 1)

        def norm_scalar(l):
            s = LN[l]
            nc.scalar.wait_ge(s["vareps"], 1)
            nc.scalar.activation(std, var, ACT.Sqrt).then_inc(s["root"], 1)
            for t in range(0, NT, 2):
                nc.scalar.wait_ge(s["transposed"], t + 1)
                nc.scalar.activation(xnT[:, :, t * P:(t + 1) * P],
                                     BK[t % 4][:, 0:KD * P].rearrange("p (k s) -> p k s", k=KD),
                                     ACT.Copy).then_inc(s["evac_s"], 1)

        def norm_tensor(l):
            s = LN[l]
            for t in range(NT):
                nc.tensor.wait_ge(s["normed"], t + 1)
                if t >= 4:
                    nc.tensor.wait_ge(s["evac_v" if t % 2 else "evac_s"], (t - 4) // 2 + 1)
                for k in range(KD):
                    last = nc.tensor.transpose(BK[t % 4][:, k * P:(k + 1) * P], xn[:, t, k * P:(k + 1) * P], ident[:, :])
                last.then_inc(s["transposed"], 1)

        def wait_normed(eng, l):
            eng.wait_ge(LN[l]["evac_s"], NT // 2)
            eng.wait_ge(LN[l]["evac_v"], NT // 2)

        def heads(l, b=0):
            if l == 0:
                return GA, (lambda h: qst[b % 2][:, h, :]), (lambda h: kst[b % 2][:, h, :]), (lambda h: h), HDA, SCALE_A, woa
            return GB, (lambda h: qsb[:, h, :]), (lambda h: ksb[:, h // 4, :]), (lambda h: h // 4), HDB, SCALE_B, wob

        def scores_tensor(l, b, groups):
            s = AT[l]
            G, q, k, v, hd, scale, wo = heads(l, b)
            for g in groups:
                if g == 0 and l == 0:
                    if b == 0:
                        nc.tensor.wait_ge(PA["evac_v"], 2 * len(BY_V))
                        nc.tensor.wait_ge(PA["evac_s"], 2 * len(BY_S))
                    nc.tensor.wait_ge(PA["placed_k"], b * PLACED_K + PLACED_K)
                    nc.tensor.wait_ge(s["placed"], b * PLACED_A + PLACED_A)
                if g == 0 and l == 2:
                    if isinstance(b, int) and b == 0:
                        nc.tensor.wait_ge(PB["vall"], 1)
                        nc.tensor.wait_ge(PB["prod"], B + 1)
                    nc.tensor.wait_ge(s["placed"], b * PLACED_B + PLACED_B)
                if g == G // 2 and l == 2:
                    nc.tensor.wait_ge(PB["placed_2"], b * PLACED_B + PLACED_B)
                bank = BK[3 * (g % 2):3 * (g % 2) + 3]
                if g >= 2:
                    nc.tensor.wait_ge(s["maxima"], b * 3 * G + 3 * (g - 1))
                nc.tensor.matmul(bank[0][:, :].rearrange("p (n s) -> p n s", n=4), identb[:, :],
                                 masks[:, 0, None, P:2 * P].broadcast_to([P, 4, P]),
                                 start=True, stop=False, skip_group_check=True)
                for j in range(4):
                    h = 4 * g + j
                    last = nc.tensor.matmul(bank[0][:, j * P:(j + 1) * P], q(h)[:, 0:P], k(h)[:, 0:P],
                                            start=False, stop=j == 3, skip_group_check=True)
                last.then_inc(s["scores"], 1)
                for i in range(2):
                    nc.tensor.matmul(bank[1 + i][:, :].rearrange("p (n s) -> p n s", n=2)[:, :, P:S], identb[:, :],
                                     masks[:, 0, None, P:2 * P].broadcast_to([P, 2, P]),
                                     start=True, stop=False, skip_group_check=True)
                    for j in range(2):
                        h = 4 * g + 2 * i + j
                        last = nc.tensor.matmul(bank[1 + i][:, j * S:(j + 1) * S], q(h)[:, P:S], k(h)[:, :],
                                                start=False, stop=j == 1, skip_group_check=True)
                    last.then_inc(s["scores"], 1)

        def attend_tensor(l, b):
            s = AT[l]
            G, q, k, v, hd, scale, wo = heads(l, b)
            va = (vaug2 if l == 0 and b % 2 == 0 else vaug)[:, 0:2 * v(4 * G - 1) * 32 + 64].rearrange(
                "p (n h c) -> p n h c", n=2, c=32)
            nc.tensor.wait_ge(s["lo"], b + 1)
            later(nc.tensor, s["all_e"], b)
            for t in range(2):
                last = nc.tensor.transpose(BK[7][0:PARTS * 32, :].bitcast(BF16)[:, t * P:(t + 1) * P],
                                           npartf[:, t, :], identb[:, :])
            last.then_inc(s["max_t"], 1)
            nc.tensor.wait_ge(s["max_e"], b + 1)
            if l == 0 and 0 < b < B - 1:
                nc.tensor.wait_ge(PA["evac_v"], (b + 2) * len(BY_V))
                nc.tensor.wait_ge(PA["evac_s"], (b + 2) * len(BY_S))

            def pv(g):
                n = g % 2
                nc.tensor.wait_ge(s["exps"], b * 3 * G + 3 * (g + 1))
                if g == 0:
                    later(nc.tensor, s["added"], b)
                    if l == 0:
                        nc.tensor.wait_ge(PA["evac_s"], (b + 1) * len(BY_S))
                    else:
                        nc.tensor.wait_ge(s["values"], b + 1)
                else:
                    nc.tensor.wait_ge(s["pv_e"], b * G + g)
                for j in range(4):
                    nc.tensor.matmul(BK[6][32 * j:32 * j + 32, 0:S], va[:, 0, v(4 * g + j), :],
                                     PT[:, n, j // 2, (j % 2) * S:(j % 2 + 1) * S],
                                     start=True, stop=False, skip_group_check=True, tile_position=(0, 32 * j))
                for j in range(4):
                    last = nc.tensor.matmul(BK[6][32 * j:32 * j + 32, P:S], va[:, 1, v(4 * g + j), :],
                                            PT[:, n, 2, j * P:(j + 1) * P],
                                            start=False, stop=True, skip_group_check=True, tile_position=(0, 32 * j))
                last.then_inc(s["pv"], 1)

            def out_t(g):
                nc.tensor.wait_ge(s["pv_e"], b * G + g + 1)
                if g >= 1:
                    nc.tensor.wait_ge(s["divided"], b * G + g)
                for t in range(2):
                    last = nc.tensor.transpose(BK[7][:, t * P:(t + 1) * P], oun[:, g % 2, t * P:(t + 1) * P], ident[:, :])
                last.then_inc(s["out_t"], 1)

            for g in range(G + 2):
                if g < G:
                    bank = BK[3 * (g % 2):3 * (g % 2) + 3]
                    if g < 2:
                        nc.tensor.wait_ge(s["maxima"], (b + 1) * 3 * G)
                    else:
                        nc.tensor.wait_ge(s["exps"], b * 3 * G + 3 * (g - 1))
                    for i in range(2):
                        nc.tensor.matmul(bank[i][:, :].rearrange("p (n s) -> p n s", n=2)[:, :, 0:P], identb[:, :],
                                         masks[:, 1, None, 0:P].broadcast_to([P, 2, P]),
                                         start=True, stop=False, skip_group_check=True)
                        for j in range(2):
                            h = 4 * g + 2 * i + j
                            nc.tensor.matmul(bank[i][:, j * S:(j + 1) * S], sel[:, h:h + 1].broadcast_to([PARTS * 32, P]),
                                             nT[:, :], start=False, stop=False, skip_group_check=True)
                            last = nc.tensor.matmul(bank[i][:, j * S:(j + 1) * S], k(h)[:, 0:P], q(h)[:, :],
                                                    start=False, stop=j == 1, skip_group_check=True)
                        last.then_inc(s["shifted"], 1)
                    nc.tensor.matmul(bank[2][:, :].rearrange("p (n s) -> p n s", n=4), identb[:, :],
                                     masks[:, 1, None, 0:P].broadcast_to([P, 4, P]),
                                     start=True, stop=False, skip_group_check=True)
                    for j in range(4):
                        h = 4 * g + j
                        nc.tensor.matmul(bank[2][:, j * P:(j + 1) * P], sel[:, h:h + 1].broadcast_to([PARTS * 32, P]),
                                         nT[:, P:S], start=False, stop=False, skip_group_check=True)
                        last = nc.tensor.matmul(bank[2][:, j * P:(j + 1) * P], k(h)[:, P:S], q(h)[:, P:S],
                                                start=False, stop=j == 3, skip_group_check=True)
                    last.then_inc(s["shifted"], 1)
                if 1 <= g <= G:
                    pv(g - 1)
                if g >= 2:
                    out_t(g - 2)

        def out_tensor(l, b):
            s = AT[l]
            G, q, k, v, hd, scale, wo = heads(l)
            nc.tensor.wait_ge(s["divided"], b * G + G)
            for kk in range(KD):
                for t in range(2):
                    last = nc.tensor.transpose(BK[7][:, (2 * kk + t) * P:(2 * kk + t + 1) * P],
                                               otok[:, t, kk * P:(kk + 1) * P], ident[:, :])
            last.then_inc(s["all_t"], 1)
            nc.tensor.wait_ge(s["all_e"], b + 1)
            for t in range(2):
                for kk in range(KD):
                    last = nc.tensor.matmul(BK[6][:, t * D:(t + 1) * D], oT[:, kk, t * P:(t + 1) * P], wo[:, kk, :],
                                            start=kk == 0, stop=kk == KD - 1)
            last.then_inc(s["projected"], 1)

        def add_vector(l, b):
            s = AT[l]
            nc.vector.wait_ge(s["projected"], b + 1)
            xb = xres[:, bass.ds(2 * b, 2), :]
            nc.vector.tensor_tensor(xb, xb, BK[6][:, :].rearrange("p (q d) -> p q d", q=2), ALU.add).then_inc(s["added"], 1)

        def maxima_vector(l, b, before):
            s = AT[l]
            G, q, k, v, hd, scale, wo = heads(l)
            nh = 4 * G
            for g in range(G):
                bank = BK[3 * (g % 2):3 * (g % 2) + 3]
                nc.vector.wait_ge(s["scores"], b * 3 * G + 3 * g + 1)
                if g == 0:
                    later(nc.vector, s["max_t"], b)
                nc.vector.tensor_reduce(nmax[:, 0, 4 * g:4 * g + 4], bank[0][:, :].rearrange("p (n s) -> p n s", n=4),
                                        AX, ALU.max, negate=True).then_inc(s["maxima"], 1)
                for i in range(2):
                    nc.vector.wait_ge(s["scores"], b * 3 * G + 3 * g + 2 + i)
                    nc.vector.tensor_reduce(nmax[:, 1, 4 * g + 2 * i:4 * g + 2 * i + 2],
                                            bank[1 + i][:, :].rearrange("p (n s) -> p n s", n=2),
                                            AX, ALU.max, negate=True).then_inc(s["maxima"], 1)
                if g == 3 and before:
                    add_vector(l, b - 1)
            nc.vector.wait_ge(s["maxima"], (b + 1) * 3 * G)
            nc.vector.tensor_copy(nparts[:, :, 0, 0:nh], nmax[:, :, 0:nh]).then_inc(s["hi"], 1)
            nc.vector.wait_ge(s["hi"], b + 1)
            nc.vector.tensor_tensor(nrem[:, :, 0:nh], nmax[:, :, 0:nh], nparts[:, :, 0, 0:nh], ALU.subtract).then_inc(s["rest"], 1)
            nc.vector.wait_ge(s["rest"], b + 1)
            nc.vector.tensor_copy(nparts[:, :, 1, 0:nh], nrem[:, :, 0:nh]).then_inc(s["mid"], 1)
            nc.vector.wait_ge(s["mid"], b + 1)
            nc.vector.tensor_tensor(nparts[:, :, 2, 0:nh], nrem[:, :, 0:nh], nparts[:, :, 1, 0:nh], ALU.subtract).then_inc(s["lo"], 1)

        def attend_vector(l, b):
            s = AT[l]
            G, q, k, v, hd, scale, wo = heads(l)

            def divide(g):
                tt = BK[7][:, 0:S].rearrange("p (q j c) -> p q j c", q=2, c=32)
                nc.vector.wait_ge(s["out_t"], b * G + g + 1)
                nc.vector.reciprocal(rec[:, :, :], tt[:, :, :, hd]).then_inc(s["recips"], 1)
                nc.vector.wait_ge(s["recips"], b * G + g + 1)
                if g == 0:
                    later(nc.vector, s["all_t"], b)
                nc.vector.tensor_tensor(otok[:, :, 4 * g * hd:4 * (g + 1) * hd].rearrange("p q (j c) -> p q j c", j=4),
                                        tt[:, :, :, 0:hd], rec[:, :, :, None].broadcast_to([P, 2, 4, hd]),
                                        ALU.mult).then_inc(s["divided"], 1)

            for g in range(G):
                nc.vector.wait_ge(s["pv"], b * G + g + 1)
                if g >= 2:
                    nc.vector.wait_ge(s["out_t"], b * G + g - 1)
                nc.vector.tensor_copy(oun[:, g % 2, :], BK[6][:, 0:S]).then_inc(s["pv_e"], 1)
                if g >= 1:
                    divide(g - 1)
            divide(G - 1)

        def attend_scalar(l, b):
            s = AT[l]
            G, q, k, v, hd, scale, wo = heads(l)
            nc.scalar.wait_ge(s["max_t"], b + 1)
            nc.scalar.activation(nT[:, :], BK[7][0:PARTS * 32, :].bitcast(BF16)[:, 0:S], ACT.Copy).then_inc(s["max_e"], 1)
            for g in range(G):
                bank = BK[3 * (g % 2):3 * (g % 2) + 3]
                for i in range(3):
                    nc.scalar.wait_ge(s["shifted"], b * 3 * G + 3 * g + i + 1)
                    if i == 0:
                        later(nc.scalar, s["pv"], b * G + max(g - 1, 0))
                    nc.scalar.activation(PT[:, g % 2, i, :], bank[i][:, :], ACT.Exp, scale=scale).then_inc(s["exps"], 1)

        def out_scalar(l, b):
            s = AT[l]
            nc.scalar.wait_ge(s["all_t"], b + 1)
            nc.scalar.activation(oT[:, :, :], BK[7][:, :].rearrange("p (k s) -> p k s", k=KD), ACT.Copy).then_inc(s["all_e"], 1)

        ITEMS = 13
        BY_V = [1, 2, 3, 4, 5, 9, 10, 11, 12]
        BY_S = [0, 6, 7, 8]
        ROT = [2, 3, 4, 5, 9, 10, 11, 12]
        PLACED_A = 16 * (2 * 8 + 8)
        PLACED_K = 16 * 8

        def wait_item(eng, b, i):
            if i in BY_V:
                eng.wait_ge(PA["evac_v"], b * len(BY_V) + BY_V.index(i) + 1)
            else:
                eng.wait_ge(PA["evac_s"], b * len(BY_S) + BY_S.index(i) + 1)

        def project_a_tensor(b):
            xb = [xnT[:, kk, bass.ds(b * S, S)] for kk in range(KD)]
            for i in range(ITEMS):
                bk = BK[i % 6]
                if i >= 6:
                    wait_item(nc.tensor, b, i - 6)
                elif b == 1:
                    wait_item(nc.tensor, 0, i + 6 if i else 12)
                elif b > 1 and i == 0:
                    nc.tensor.wait_ge(AT[0]["maxima"], b * 3 * GA)
                if i == 0:
                    ops = [(bk[0:CQH, m * S:(m + 1) * S], wdq[:, kk, m * CQH:(m + 1) * CQH], xb[kk], kk)
                           for m in range(2) for kk in range(KD)]
                elif i == 1:
                    ops = [(bk[0:CKV, 0:S], wdkv[:, kk, :], xb[kk], kk) for kk in range(KD)]
                elif i < 6:
                    ops = [(bk[:, a * S:(a + 1) * S], wkr[:, kk, ((i - 2) * 2 + a) * P:((i - 2) * 2 + a + 1) * P], xb[kk], kk)
                           for a in range(2) for kk in range(KD)]
                elif i == 6:
                    ops = [(bk[:, m * S:(m + 1) * S], wuq[:, kk, m * P:(m + 1) * P], cqT[:, kk, :], kk)
                           for m in range(2) for kk in range(2)]
                elif i == 7:
                    wait_item(nc.tensor, b, 1)
                    ops = [(bk[:, m * S:(m + 1) * S], wuk[:, m * P:(m + 1) * P], ckvT[:, :], None) for m in range(2)]
                elif i == 8:
                    ops = [(bk[:, m * D:(m + 1) * D], ckvT[:, m * P:(m + 1) * P], wuv[:, :], None) for m in range(2)]
                else:
                    ops = [(bk[:, a * S:(a + 1) * S], wqr[:, kk, ((i - 9) * 2 + a) * P:((i - 9) * 2 + a + 1) * P], cqT[:, kk, :], kk)
                           for a in range(2) for kk in range(2)]
                for dst, w, r, kk in ops:
                    last = nc.tensor.matmul(dst, w, r, start=kk in (0, None), stop=kk in (1, None))
                last.then_inc(PA["item"], 1)

        def project_a_vector(b):
            for i in BY_V:
                bk = BK[i % 6]
                nc.vector.wait_ge(PA["item"], b * ITEMS + i + 1)
                if i == 1:
                    nc.vector.tensor_copy(ckvT[:, :], bk[0:CKV, 0:S]).then_inc(PA["evac_v"], 1)
                    continue
                r = ROT.index(i)
                if b * len(ROT) + r >= 2:
                    nc.vector.wait_ge(PA["summed"], b * len(ROT) + r - 1)
                v = bk[:, :].rearrange("p (a s) -> p a s", a=2)
                nc.vector.tensor_tensor(rt[:, r % 2, 0, :, :], v, rope[:, 0, None, :].broadcast_to([P, 2, S]), ALU.mult)
                nc.vector.tensor_tensor(rt[:, r % 2, 1, :, :], v, rope[:, 1, None, :].broadcast_to([P, 2, S]),
                                        ALU.mult).then_inc(PA["evac_v"], 1)

        def project_a_scalar(b):
            for i in BY_S:
                bk = BK[i % 6]
                nc.scalar.wait_ge(PA["item"], b * ITEMS + i + 1)
                if i == 0:
                    dst, src = cqT[:, :, :], bk[0:CQH, :].rearrange("p (a s) -> p a s", a=2)
                elif i == 6:
                    later(nc.scalar, AT[0]["placed"], b * PLACED_A)
                    dst, src = qc[:, :, :], bk[:, :].rearrange("p (a s) -> p a s", a=2)
                elif i == 7:
                    dst, src = kc[:, :, :], bk[:, :].rearrange("p (a s) -> p a s", a=2)
                else:
                    dst = (vaug if b % 2 else vaug2)[:, :].rearrange("p (n h c) -> p n h c", n=2, c=32)[:, :, :, 0:HDA]
                    src = bk[:, :].rearrange("p (n h c) -> p n h c", n=2, c=HDA)
                nc.scalar.activation(dst, src, ACT.Copy).then_inc(PA["evac_s"], 1)

        def project_a_gpsimd(b):
            for r in range(len(ROT)):
                nc.gpsimd.wait_ge(PA["evac_v"], b * len(BY_V) + BY_V.index(ROT[r]) + 1)
                dst = stage[r // 4][:, r % 4, :, :]
                if r == 0:
                    later(nc.gpsimd, PA["placed_k"], b * PLACED_K)
                if r == 4:
                    later(nc.gpsimd, AT[0]["placed"], b * PLACED_A)
                t = rt[:, r % 2, :, :, :]
                nc.gpsimd.tensor_tensor(dst[:, 0, :], t[:, 0, 0, :], t[:, 1, 1, :], ALU.subtract)
                nc.gpsimd.tensor_tensor(dst[:, 1, :], t[:, 0, 1, :], t[:, 1, 0, :], ALU.add).then_inc(PA["summed"], 1)

        def place_a_sync(b):
            if b >= 2:
                nc.sync.wait_ge(AT[0]["shifted"], (b - 1) * 3 * GA)

            def rotated(dst, n, s):
                nc.sync.wait_ge(PA["summed"], b * len(ROT) + 4 * (n + 1))
                for a in range(2):
                    for j in range(4):
                        nc.sync.dma_start(dst[32 + 32 * a:64 + 32 * a, j:HA:4, :],
                                          stage[n][32 * j:32 * j + 32, :, a, :]).then_inc(s, 16)

            rotated(kst[b % 2], 0, PA["placed_k"])
            for i, dst, src in ((6, qst[b % 2], qc), (7, kst[b % 2], kc)):
                wait_item(nc.sync, b, i)
                for j in range(8):
                    nc.sync.dma_start(dst[0:16, j:16:8, :], src[16 * j:16 * j + 16, :, :]).then_inc(AT[0]["placed"], 16)
            rotated(qst[b % 2], 1, AT[0]["placed"])

        PLACED_B = 16 * (PARTS + PARTS * PARTS)
        STORED_Q, STORED_K = 16 * 2 * PARTS, 16 * 2 * PARTS * B

        def project_b_tensor():
            s = PB
            for i in range(B + 1):
                bk = BK[i % 2]
                if i >= 2:
                    nc.tensor.wait_ge(s["prod"], i - 1)
                for a in range(2):
                    if i < B:
                        for kk in range(KD):
                            last = nc.tensor.matmul(bk[:, a * S:(a + 1) * S], wqb[:, kk, a * P:(a + 1) * P],
                                                    xnT[:, kk, i * S:(i + 1) * S], start=kk == 0, stop=kk == KD - 1)
                    else:
                        for b in range(B):
                            for kk in range(KD):
                                last = nc.tensor.matmul(bk[32 * b:32 * b + 32, a * S:(a + 1) * S],
                                                        wkvb[:, kk, a * 32:(a + 1) * 32], xnT[:, kk, b * S:(b + 1) * S],
                                                        start=kk == 0, stop=kk == KD - 1,
                                                        tile_position=(0, 32 * b), skip_group_check=True)
                last.then_inc(s["item"], 1)
            for t in range(NT):
                for kk in range(KD):
                    last = nc.tensor.matmul(BK[2][:, t * 64:(t + 1) * 64], xnT[:, kk, t * P:(t + 1) * P],
                                            wkvb[:, kk, 64:128], start=kk == 0, stop=kk == KD - 1)
            last.then_inc(s["item"], 1)

        def project_b_vector():
            s = PB
            nc.vector.memset(R2[64:RBZ, 0:5120], 0.0).then_inc(s["zeroed"], 1)

            def split(i):
                hi, mid, lo = (qparts[:, i % 2, n, :, :] for n in range(PARTS))
                rs = rsb[:, i % 2, :, :]
                nc.vector.wait_ge(s["summed"], i + 1)
                if i >= 2:
                    nc.vector.wait_ge(s[f"stored{i % 2}"], STORED_Q * (i // 2))
                nc.vector.tensor_copy(hi, rs).then_inc(s["hi"], 1)
                nc.vector.wait_ge(s["hi"], i + 1)
                nc.vector.tensor_tensor(rem[:, :, :], rs, hi, ALU.subtract).then_inc(s["rest"], 1)
                nc.vector.wait_ge(s["rest"], i + 1)
                nc.vector.tensor_copy(mid, rem[:, :, :]).then_inc(s["mid"], 1)
                nc.vector.wait_ge(s["mid"], i + 1)
                nc.vector.tensor_tensor(lo, rem[:, :, :], mid, ALU.subtract).then_inc(s["lo"], 1)

            for i in range(B + 1):
                bk = BK[i % 2][:, :].rearrange("p (a s) -> p a s", a=2)
                table = rope if i < B else ropek
                nc.vector.wait_ge(s["item"], i + 1)
                if i >= 2:
                    nc.vector.wait_ge(s["summed"], i - 1)
                nc.vector.tensor_tensor(rtb[:, i % 2, 0, :, :], bk, table[:, 0, None, :].broadcast_to([P, 2, S]), ALU.mult)
                nc.vector.tensor_tensor(rtb[:, i % 2, 1, :, :], bk, table[:, 1, None, :].broadcast_to([P, 2, S]),
                                        ALU.mult).then_inc(s["prod"], 1)
                if i >= 1:
                    split(i - 1)
            split(B)

        def project_b_gpsimd():
            s = PB
            for i in range(B + 1):
                m = i % 2
                nc.gpsimd.wait_ge(s["prod"], i + 1)
                if i >= 2:
                    nc.gpsimd.wait_ge(s["lo"], i - 1)
                nc.gpsimd.tensor_tensor(rsb[:, m, 0, :], rtb[:, m, 0, 0, :], rtb[:, m, 1, 1, :], ALU.subtract)
                nc.gpsimd.tensor_tensor(rsb[:, m, 1, :], rtb[:, m, 0, 1, :], rtb[:, m, 1, 0, :], ALU.add).then_inc(s["summed"], 1)

        def project_b_scalar():
            nc.scalar.wait_ge(PB["item"], B + 2)
            nc.scalar.activation(vall[:, :, :], BK[2][:, :].rearrange("p (t n) -> p t n", t=NT), ACT.Copy).then_inc(PB["vall"], 1)

        def values_b_scalar(b):
            va = vaug[:, 0:2 * KVB * 32].rearrange("p (n h c) -> p n h c", n=2, c=32)
            nc.scalar.wait_ge(PB["vall"], 1)
            later(nc.scalar, AT[2]["pv"], b * GB)
            nc.scalar.activation(va[:, :, :, 0:HDB], vall[:, bass.ds(2 * b, 2), :].rearrange("p n (h c) -> p n h c", c=HDB),
                                 ACT.Copy).then_inc(AT[2]["values"], 1)

        def store_b_sync():
            half = HDB // 2
            for i in range(B + 1):
                nc.sync.wait_ge(PB["lo"], i + 1)
                for n in range(PARTS):
                    for a in range(2):
                        r = n * HDB + a * half
                        for b in range(B) if i == B else [i]:
                            if i < B:
                                dst, src = q_d[b, r:r + half], qparts[:, i % 2, n, a, :]
                            else:
                                dst, src = k_d[b, r:r + half], qparts[32 * b:32 * b + 32, i % 2, n, a, :]
                            nc.sync.dma_start(dst.rearrange("i h s -> (i h) s"), src).then_inc(PB[f"stored{i % 2}"], 16)
            nc.sync.wait_ge(PB["stored0"], STORED_Q * 2 + STORED_K)
            nc.sync.wait_ge(PB["stored1"], STORED_Q * 2)
            nc.sync.wait_ge(PB["zeroed"], 1)

        def place_b_sync(b):
            for half in range(2):
                if not (isinstance(b, int) and b == 0):
                    nc.sync.wait_ge(AT[2]["shifted"], (b - 1) * 3 * GB + (half + 1) * 3 * GB // 2)
                s = PB["placed_2"] if half else AT[2]["placed"]
                hq, hk = slice(half * HB // 2, (half + 1) * HB // 2), slice(half * KVB // 2, (half + 1) * KVB // 2)
                for m in range(PARTS):
                    r = m * PARTS * HDB
                    nc.sync.dma_start(qsb[r:r + PARTS * HDB, hq, :],
                                      q_d[bass.ds(b, 1), :, hq, :].rearrange("o r h s -> (o r) h s")).then_inc(s, 16)
                    for n in range(PARTS):
                        nc.sync.dma_start(ksb[r + n * HDB:r + (n + 1) * HDB, hk, :],
                                          k_d[bass.ds(b, 1), m * HDB:(m + 1) * HDB, hk, :].rearrange("o r h s -> (o r) h s")
                                          ).then_inc(s, 16)

        def route_tensor(l):
            s = FF[l]
            for t in range(NT):
                for kk in range(KD):
                    last = nc.tensor.matmul(BK[7][:, t * E:(t + 1) * E], xnT[:, kk, t * P:(t + 1) * P], rw[:, kk, :],
                                            start=kk == 0, stop=kk == KD - 1)
            last.then_inc(s["logits"], 1)
            nc.tensor.wait_ge(s["count"], 1)
            for t in range(NT + 1):
                for u in range(t + 1) if t < NT else range(NT):
                    if t < NT:
                        lhsT = tri if u == t else onesb
                        stop = u == t
                    else:
                        lhsT, stop = onesb, u == NT - 1
                    last = nc.tensor.matmul(BK[6][:, t * E:(t + 1) * E], lhsT[:, :], cnt[:, u * E:(u + 1) * E],
                                            start=u == 0, stop=stop)
            last.then_inc(s["rank1"], 1)

        owned = {1: 0, 3: 0}

        def route_vector(l):
            s = FF[l]
            v = nc.vector

            def link(*ops):
                for op in ops:
                    op.then_inc(s["own"], 1)
                owned[l] += len(ops)
                v.wait_ge(s["own"], owned[l])

            v.wait_ge(s["consts"], 16 * 4)
            v.wait_ge(s["logits"], 1)
            link(v.tensor_copy(lg, BK[7][:, 0:NT * E].rearrange("p (t e) -> p t e", t=NT)))
            link(*[v.max(mx[:, t, :], lg[:, t, :]) for t in range(NT)])
            v.tensor_tensor(dlt, mx[:, :, 1], mx[:, :, 0], ALU.subtract).then_inc(s["dlt"], 1)
            link(*[v.max_index(mi[:, t, :], mx[:, t, :], lg[:, t, :]) for t in range(NT)])
            link(v.tensor_copy(idf, mi[:, :, 0:2].rearrange("p t k -> p k t")))
            link(*[v.tensor_tensor(oh[:, k, :, :], small[:, None, 0:E].broadcast_to([P, NT, E]),
                                   idf[:, k, :, None].broadcast_to([P, NT, E]), ALU.is_equal) for k in range(TOPK)])
            v.tensor_tensor(cnt.rearrange("p (t e) -> p t e", t=NT), oh[:, 0, :, :], oh[:, 1, :, :], ALU.add).then_inc(s["count"], 1)
            v.wait_ge(s["exp1"], 1)
            link(v.tensor_scalar_add(den, ex1, 1.0))
            link(v.reciprocal(w01[:, 0, :], den))
            link(v.tensor_tensor(w01[:, 1, :], ex1, w01[:, 0, :], ALU.mult))
            v.wait_ge(s["rank1"], 1)
            link(v.tensor_tensor(cmp, BK[6][:, NT * E:(NT + 1) * E, None].broadcast_to([P, E, 8]),
                                 small[:, 8:72].rearrange("p (e j) -> p e j", e=E), ALU.is_gt))
            link(v.tensor_reduce(ntl, cmp, AX, ALU.add))
            link(v.tensor_tensor(cmp, ntl[:, None, :].broadcast_to([P, E, E]),
                                 small[:, 72:136].rearrange("p (e j) -> p e j", e=E), ALU.mult))
            link(v.tensor_reduce(base, cmp, AX, ALU.add))
            link(v.scalar_tensor_tensor(out=posb, in0=base[:, None, :].broadcast_to([P, NT, E]), scalar=float(P),
                                        in1=BK[6][:, 0:NT * E].rearrange("p (t e) -> p t e", t=NT),
                                        op0=ALU.mult, op1=ALU.add))
            link(v.tensor_tensor(ohp, oh, posb[:, None, :, :].broadcast_to([P, 2, NT, E]), ALU.mult))
            link(v.tensor_reduce(slf.rearrange("p (k t) -> p k t", k=2), ohp, AX, ALU.add))
            v.tensor_copy(slot, slf).then_inc(s["slot"], 1)
            link(v.tensor_tensor(ecm, small[0:1, 136:160, None].broadcast_to([1, 24, 7]),
                                 base[0:1, None, 1:E].broadcast_to([1, 24, 7]), ALU.is_ge))
            link(v.tensor_reduce(eidf, ecm, AX, ALU.add))
            v.tensor_copy(eid, eidf).then_inc(s["eid"], 1)

        def route_scalar(l):
            s = FF[l]
            nc.scalar.wait_ge(s["dlt"], 1)
            nc.scalar.activation(ex1, dlt, ACT.Exp).then_inc(s["exp1"], 1)

        def scatter_gpsimd(l):
            s = FF[l]
            nc.gpsimd.wait_ge(s["slot"], 1)
            nc.gpsimd.wait_ge(LN[l]["normed"], NT)
            if l == 1:
                nc.gpsimd.wait_ge(s_zero, 16)
            for t in range(NT):
                for k in range(TOPK):
                    nc.gpsimd.indirect_dma_start(
                        xs_d[:, :], bass.IndirectOffsetOnAxis(ap=slot[:, k * NT + t:k * NT + t + 1], axis=0),
                        xn[:, t, :], None).then_inc(s["scatter"], 16)

        def load_tile(l, i, n, p):
            s = FF[l]
            nc.sync.dma_start(xs[:, p, :], xs_d[bass.ds(i * P, P), :]).then_inc(s[f"xs{p}"], 16)

        def store_tile(l, i, n, p):
            s = FF[l]
            nc.sync.wait_ge(s["y_e"], i + 1)
            nc.sync.dma_start(ys_d[bass.ds(i * P, P), :], yo[:, p, :]).then_inc(s[f"ys{p}"], 16)

        def tile_sync(l, i, n, p, load=True):
            if load:
                nc.sync.wait_ge(FF[l]["x_t"], i + 1)
                load_tile(l, i + 2, n + 1, p)
            store_tile(l, i - 2, n - 1, p)

        def tile_transpose(l, i, n, p):
            s = FF[l]
            nc.tensor.wait_ge(s[f"xs{p}"], 16 * (n + 1))
            later(nc.tensor, s["x_e"], i)
            for kk in range(KD):
                last = nc.tensor.transpose(BK[6][:, kk * P:(kk + 1) * P], xs[:, p, kk * P:(kk + 1) * P], ident[:, :])
            last.then_inc(s["x_t"], 1)

        def expert_of(i):
            return nc.tensor.value_load(eid[0:1, bass.ds(i, 1)], min_val=0, max_val=E - 1)

        def tile_up(l, i, n, p, e):
            s = FF[l]
            nc.tensor.wait_ge(s["x_e"], i + 1)
            for half in range(2):
                later(nc.tensor, s["hid"], 2 * i)
                for gu in range(2):
                    for kk in range(KD):
                        last = nc.tensor.matmul(BK[2 * half + gu][:, 0:IH], xsT[:, p, kk, :],
                                                wgu[:, bass.ds(e * (KD * GU) + (kk * GU + gu * I + half * IH), IH)],
                                                start=kk == 0, stop=kk == KD - 1)
                    last.then_inc(s["gu"], 1)

        def tile_hidden(l, i, n, p):
            s = FF[l]
            nc.tensor.wait_ge(s["hid"], 2 * i + 2)
            later(nc.tensor, s["hte_v"], i)
            later(nc.tensor, s["hte_s"], i)
            for c in range(6):
                last = nc.tensor.transpose(BK[4 + c // 4][0:CH[c], (c % 4) * P:(c % 4 + 1) * P],
                                           hh[:, CO[c]:CO[c] + CH[c]], ident[:, :])
                if c in (3, 5):
                    last.then_inc(s["hid_t"], 1)

        def tile_down(l, i, n, p, e):
            s = FF[l]
            nc.tensor.wait_ge(s["hte_v"], i + 1)
            nc.tensor.wait_ge(s["hte_s"], i + 1)
            later(nc.tensor, s["y_e"], i)
            for c in range(6):
                last = nc.tensor.matmul(BK[7][:, 0:D], hT[0:CH[c], p, c, :],
                                        wd[0:CH[c], bass.ds(e * (6 * D) + c * D, D)], start=c == 0, stop=c == 5)
            last.then_inc(s["down"], 1)

        def tile_scalar_x(l, i, n, p):
            s = FF[l]
            a = nc.scalar
            a.wait_ge(s["x_t"], i + 1)
            a.activation(xsT[:, p, :, :], BK[6][:, 0:S].rearrange("p (k s) -> p k s", k=KD), ACT.Copy).then_inc(s["x_e"], 1)

        def tile_scalar(l, i, n, p):
            s = FF[l]
            a = nc.scalar
            for half in range(2):
                a.wait_ge(s["gu"], 4 * i + 2 * half + 1)
                later(a, s["hid"], 2 * i)
                a.activation(sg[:, half * IH:(half + 1) * IH], BK[2 * half][:, 0:IH], ACT.Silu).then_inc(s["silu"], 1)

        def tile_scalar_2(l, i, n, p):
            s = FF[l]
            a = nc.scalar
            a.wait_ge(s["hid_t"], 2 * i + 2)
            a.activation(hT[0:CH[5], p, 4:6, :], BK[5][0:CH[5], 0:2 * P].rearrange("p (c s) -> p c s", c=2),
                         ACT.Copy).then_inc(s["hte_s"], 1)

        def tile_scalar_y(l, i, n, p):
            s = FF[l]
            a = nc.scalar
            a.wait_ge(s["down"], i + 1)
            later(a, s[f"ys{p}"], 16 * n)
            a.activation(yo[:, p, :], BK[7][:, 0:D], ACT.Copy).then_inc(s["y_e"], 1)

        def tile_vector(l, i, n, p):
            s = FF[l]
            v = nc.vector
            for half in range(2):
                v.wait_ge(s["silu"], 2 * i + half + 1)
                v.wait_ge(s["gu"], 4 * i + 2 * half + 2)
                later(v, s["hid_t"], 2 * i)
                v.tensor_tensor(hh[:, half * IH:(half + 1) * IH], sg[:, half * IH:(half + 1) * IH],
                                BK[2 * half + 1][:, 0:IH], ALU.mult).then_inc(s["hid"], 1)
            v.wait_ge(s["hid_t"], 2 * i + 1)
            v.tensor_copy(hT[:, p, 0:4, :], BK[4][0:CH[0], :].rearrange("p (c s) -> p c s", c=4)).then_inc(s["hte_v"], 1)

        def experts_tensor(l):
            s = FF[l]
            nc.tensor.wait_ge(s["eid"], 1)
            nc.tensor.wait_ge(s_wgu, 16 * E)

            def step(i, n, p, nxt=True):
                e, before = expert_of(i), expert_of(i - 1)
                tile_hidden(l, i - 1, n + p - 1, 1 - p)
                if nxt:
                    tile_transpose(l, i + 1, n + p, 1 - p)
                tile_up(l, i, n, p, e)
                tile_down(l, i - 1, n + p - 1, 1 - p, before)

            tile_transpose(l, 0, 0, 0)
            tile_transpose(l, 1, 0, 1)
            tile_up(l, 0, 0, 0, expert_of(0))
            nc.tensor.wait_ge(s_wd, 32 * E)
            step(1, 0, 1)
            step(2, 1, 0)
            with nc.tensor.Fori(1, (SLOTS_T - 3) // 2) as r:
                step(2 * r + 1, r, 1)
                step(2 * r + 2, r + 1, 0)
            step(SLOTS_T - 2, (SLOTS_T - 2) // 2, 1)
            step(SLOTS_T - 1, (SLOTS_T - 1) // 2, 0, nxt=False)
            tile_hidden(l, SLOTS_T - 1, (SLOTS_T - 1) // 2, 0)
            tile_down(l, SLOTS_T - 1, (SLOTS_T - 1) // 2, 0, expert_of(SLOTS_T - 1))

        def experts_scalar(l):
            def step(i, n, p, nxt=True):
                tile_scalar_2(l, i - 1, n + p - 1, 1 - p)
                if nxt:
                    tile_scalar_x(l, i + 1, n + p, 1 - p)
                tile_scalar(l, i, n, p)
                tile_scalar_y(l, i - 1, n + p - 1, 1 - p)

            tile_scalar_x(l, 0, 0, 0)
            tile_scalar_x(l, 1, 0, 1)
            tile_scalar(l, 0, 0, 0)
            step(1, 0, 1)
            step(2, 1, 0)
            with nc.scalar.Fori(1, (SLOTS_T - 3) // 2) as r:
                step(2 * r + 1, r, 1)
                step(2 * r + 2, r + 1, 0)
            step(SLOTS_T - 2, (SLOTS_T - 2) // 2, 1)
            step(SLOTS_T - 1, (SLOTS_T - 1) // 2, 0, nxt=False)
            tile_scalar_2(l, SLOTS_T - 1, (SLOTS_T - 1) // 2, 0)
            tile_scalar_y(l, SLOTS_T - 1, (SLOTS_T - 1) // 2, 0)

        def experts_vector(l):
            tile_vector(l, 0, 0, 0)
            with nc.vector.Fori(0, (SLOTS_T - 1) // 2) as r:
                tile_vector(l, 2 * r + 1, r, 1)
                tile_vector(l, 2 * r + 2, r + 1, 0)

        def experts_sync(l):
            s = FF[l]
            nc.sync.wait_ge(s["scatter"], 16 * TOPK * NT)
            load_tile(l, 0, 0, 0)
            load_tile(l, 1, 0, 1)
            for i in range(2):
                nc.sync.wait_ge(s["x_t"], i + 1)
                load_tile(l, i + 2, 1, i)
            with nc.sync.Fori(1, (SLOTS_T - 3) // 2) as r:
                tile_sync(l, 2 * r, r, 0)
                tile_sync(l, 2 * r + 1, r, 1)
            tile_sync(l, SLOTS_T - 3, (SLOTS_T - 3) // 2, 0)
            for i in range(SLOTS_T - 2, SLOTS_T + 2):
                store_tile(l, i - 2, i // 2 - 1, i % 2)

        def gather_gpsimd(l):
            s = FF[l]
            nc.gpsimd.wait_ge(s["ys0"], 16 * ((SLOTS_T + 1) // 2))
            nc.gpsimd.wait_ge(s["ys1"], 16 * (SLOTS_T // 2))
            for t in range(NT):
                if t >= 4:
                    nc.gpsimd.wait_ge(s["added"], t - 3)
                for k in range(TOPK):
                    nc.gpsimd.indirect_dma_start(
                        yg[:, t % 4, k, :], None, ys_d[:, :],
                        bass.IndirectOffsetOnAxis(ap=slot[:, k * NT + t:k * NT + t + 1], axis=0)
                    ).then_inc(s[f"g{t % 4}"], 16)

        def combine_vector(l):
            s = FF[l]
            for t in range(NT):
                nc.vector.wait_ge(s[f"g{t % 4}"], 32 * (t // 4 + 1))
                nc.vector.scalar_tensor_tensor(out=xres[:, t, :], in0=yg[:, t % 4, 0, :], scalar=w01[:, 0, t:t + 1],
                                               in1=xres[:, t, :], op0=ALU.mult, op1=ALU.add).then_inc(s["own"], 1)
                owned[l] += 1
                nc.vector.wait_ge(s["own"], owned[l])
                nc.vector.scalar_tensor_tensor(out=xres[:, t, :], in0=yg[:, t % 4, 1, :], scalar=w01[:, 1, t:t + 1],
                                               in1=xres[:, t, :], op0=ALU.mult, op1=ALU.add).then_inc(s["added"], 1)

        def route_consts_sync(l):
            s = FF[l]
            nc.sync.wait_ge(AT[l - 1]["projected"], B)
            for dst, src in ((tri.bitcast(U16), "tri"), (onesb.bitcast(U16), "onesb"), (small, "small"), (rw, "rw")):
                nc.sync.dma_start(dst, dr[src]).then_inc(s["consts"], 16)

        INIT = 5

        block = ctx.enter_context(nc.Block())

        @block.sync
        def _(sp):
            xd = dr["x"].rearrange("(t p) d -> p t d", p=P)
            for t in range(0, NT, 2):
                sp.dma_start(xres[:, t:t + 2, :], xd[:, t:t + 2, :]).then_inc(s_x, 16)
            for dst, src in ((ident[:, :], "ident"), (identb[:, :].bitcast(U16), "identb"), (masks[:, :, :].bitcast(U16), "masks"),
                             (sel[:, :].bitcast(U16), "sel"), (rope[:, :, :], "rope_a")):
                sp.dma_start(dst, dr[src]).then_inc(s_const, 16)
            for dst, src in ((wdq, "wdq"), (wdkv, "wdkv"), (wkr, "wkr"), (wuq, "wuq"), (wuk, "wuk"), (wuv, "wuv"),
                             (wqr, "wqr"), (woa, "woa")):
                sp.dma_start(dst, dr[src]).then_inc(s_wa, 16)
            sp.wait_ge(s_wa, 16 * 8)
            for e in range(3):
                sp.dma_start(wgu[:, e * KD * GU:(e + 1) * KD * GU].rearrange("p (k n) -> p k n", k=KD),
                             dr["wgu"][e].rearrange("(k p) n -> p k n", p=P)).then_inc(s_wgu, 16)
            for dst, src in ((wqb[:, :, :], "wqb"), (wkvb[:, :, :], "wkvb"), (wob[:, :, :], "wob")):
                sp.dma_start(dst, dr[src].rearrange("(k p) n -> p k n", p=P)).then_inc(s_wb, 16)
            sp.wait_ge(s_init, INIT)
            for b in range(B):
                place_a_sync(b)
            sp.wait_ge(AT[0]["shifted"], (B - 1) * 3 * GA)
            sp.wait_ge(PA["placed_k"], B * PLACED_K)
            sp.wait_ge(AT[0]["placed"], B * PLACED_A)
            wdv = R1[:, :].rearrange("p (e m) -> p e m", e=E)
            for e in range(E):
                sp.dma_start(wdv[0:CH[0], e, 0:4 * D], dr["wd4"][e]).then_inc(s_wd, 16)
                sp.dma_start(wdv[0:CH[5], e, 4 * D:6 * D], dr["wd2"][e]).then_inc(s_wd, 16)
            sp.wait_ge(AT[0]["pv"], (B - 1) * GA)
            for e in range(3, E):
                if e == 5:
                    sp.wait_ge(AT[0]["shifted"], B * 3 * GA)
                sp.dma_start(wgu[:, e * KD * GU:(e + 1) * KD * GU].rearrange("p (k n) -> p k n", k=KD),
                             dr["wgu"][e].rearrange("(k p) n -> p k n", p=P)).then_inc(s_wgu, 16)
            route_consts_sync(1)
            experts_sync(1)
            sp.wait_ge(PA["evac_v"], B * len(BY_V))
            sp.dma_start(rope[:, :, :], dr["rope_b"]).then_inc(s_const, 16)
            sp.wait_ge(FF[1]["eid"], 1)
            sp.dma_start(ropek, dr["rope_k"]).then_inc(s_const, 16)
            store_b_sync()
            place_b_sync(0)
            with sp.Fori(1, B) as b:
                place_b_sync(b)
            route_consts_sync(3)
            experts_sync(3)
            od = out.rearrange("(t p) d -> p t d", p=P)
            for t in range(NT):
                sp.wait_ge(FF[3]["added"], t + 1)
                sp.dma_start(od[:, t, :], xres[:, t, :]).then_inc(s_out, 16)
            sp.wait_ge(s_out, 16 * NT)

        @block.gpsimd
        def _(pool):
            pool.memset(PTR[:, :], 0.0).then_inc(s_init, 1)
            pool.memset(vaug[:, :], 1.0).then_inc(s_init, 1)
            pool.memset(vaug2, 1.0).then_inc(s_init, 1)
            pool.memset(R1[0:32, 0:2 * HA * S], 0.0).then_inc(s_init, 1)
            pool.memset(room(ODD, 2 * HA * S)[0:32, :], 0.0).then_inc(s_init, 1)
            pool.wait_ge(s_init, INIT)
            pool.wait_ge(s_wa, 16 * 8)
            pool.dma_start(xs_d.rearrange("(n p) d -> p n d", p=P),
                           PTR[:, None, 0:D].broadcast_to([P, SLOTS_T, D])).then_inc(s_zero, 16)
            for b in range(B):
                project_a_gpsimd(b)
            scatter_gpsimd(1)
            gather_gpsimd(1)
            pool.wait_ge(AT[0]["pv"], B * GA)
            pool.memset(vaug[:, :], 1.0).then_inc(s_init, 1)
            project_b_gpsimd()
            scatter_gpsimd(3)
            gather_gpsimd(3)

        @block.vector
        def _(dve):
            norm_vector(0, lambda t: (s_x, 16 * 4))
            dve.memset(nparts[:, :, :, :], 0.0)
            dve.wait_ge(s_const, 16 * 5)
            project_a_vector(0)
            project_a_vector(1)
            for b in range(B):
                maxima_vector(0, b, b > 0)
                if 0 < b < B - 1:
                    project_a_vector(b + 1)
                attend_vector(0, b)
            add_vector(0, B - 1)
            norm_vector(1, lambda t: (AT[0]["added"], B))
            route_vector(1)
            experts_vector(1)
            combine_vector(1)
            norm_vector(2, lambda t: (FF[1]["added"], t + 1))
            dve.wait_ge(s_const, 16 * 7)
            project_b_vector()
            maxima_vector(2, 0, False)
            attend_vector(2, 0)
            with dve.Fori(1, B) as b:
                maxima_vector(2, b, True)
                attend_vector(2, b)
            add_vector(2, B - 1)
            norm_vector(3, lambda t: (AT[2]["added"], B))
            route_vector(3)
            experts_vector(3)
            combine_vector(3)

        @block.scalar
        def _(act):
            norm_scalar(0)
            act.wait_ge(s_init, INIT)
            act.wait_ge(s_zero, 16)
            project_a_scalar(0)
            project_a_scalar(1)
            for b in range(B):
                if b > 0:
                    out_scalar(0, b - 1)
                if 0 < b < B - 1:
                    project_a_scalar(b + 1)
                attend_scalar(0, b)
            out_scalar(0, B - 1)
            norm_scalar(1)
            route_scalar(1)
            experts_scalar(1)
            norm_scalar(2)
            project_b_scalar()
            act.wait_ge(s_init, INIT + 1)
            values_b_scalar(0)
            attend_scalar(2, 0)
            with act.Fori(1, B) as b:
                out_scalar(2, b - 1)
                values_b_scalar(b)
                attend_scalar(2, b)
            out_scalar(2, B - 1)
            norm_scalar(3)
            route_scalar(3)
            experts_scalar(3)

        @block.tensor
        def _(pe):
            pe.wait_ge(s_const, 16 * 5)
            norm_tensor(0)
            wait_normed(pe, 0)
            pe.wait_ge(s_wa, 16 * 8)
            project_a_tensor(0)
            project_a_tensor(1)
            for b in range(B):
                scores_tensor(0, b, range(2))
                if b > 0:
                    out_tensor(0, b - 1)
                scores_tensor(0, b, range(2, GA))
                if 0 < b < B - 1:
                    project_a_tensor(b + 1)
                attend_tensor(0, b)
            out_tensor(0, B - 1)
            norm_tensor(1)
            wait_normed(pe, 1)
            pe.wait_ge(FF[1]["consts"], 16 * 4)
            route_tensor(1)
            experts_tensor(1)
            norm_tensor(2)
            wait_normed(pe, 2)
            pe.wait_ge(s_wb, 16 * 3)
            project_b_tensor()
            scores_tensor(2, 0, range(GB))
            attend_tensor(2, 0)
            with pe.Fori(1, B) as b:
                scores_tensor(2, b, range(2))
                out_tensor(2, b - 1)
                scores_tensor(2, b, range(2, GB))
                attend_tensor(2, b)
            out_tensor(2, B - 1)
            norm_tensor(3)
            wait_normed(pe, 3)
            pe.wait_ge(FF[3]["consts"], 16 * 4)
            route_tensor(3)
            experts_tensor(3)


def kernel(**inputs):
    import concourse.bacc as bacc
    from concourse.bass_utils import run_bass_kernel_spmd

    a = {n: np.asarray(v) for n, v in inputs.items()}
    f = "L0_attn_a_"

    def rotated(w, k):
        w = w.reshape(GA, 4, 2, 32, -1).transpose(4, 0, 2, 1, 3).reshape(-1, HA * RD)
        return w.reshape(k, -1, HA * RD).transpose(1, 0, 2)

    def chunked(w, k):
        return w.T.reshape(k, -1, w.shape[0]).transpose(1, 0, 2)

    def even_odd(w, h):
        return w.reshape(D, h, HDB // 2, 2).transpose(0, 3, 2, 1).reshape(D, -1)

    down = a["L0_ffn_Wd"].transpose(0, 2, 1)
    arrays = {
        "x": a[f + "x"].reshape(T, D),
        "wdq": chunked(a[f + "w_dq"], KD), "wdkv": chunked(a[f + "w_dkv"], KD),
        "wuq": chunked(a[f + "w_uq"], 2), "wqr": rotated(a[f + "w_qr"], 2), "wkr": rotated(a[f + "w_kr"], KD),
        "wuk": a[f + "w_uk"].T, "wuv": a[f + "w_uv"].T, "woa": chunked(a[f + "w_out"], KD),
        "wqb": even_odd(a["L0_attn_b_Wq"], HB),
        "wkvb": np.concatenate([even_odd(a["L0_attn_b_Wk"], KVB), a["L0_attn_b_Wv"]], 1),
        "wob": a["L0_attn_b_Wo"],
        "rw": chunked(a["L0_ffn_router_w"], KD),
        "wgu": np.concatenate([a["L0_ffn_Wg"].transpose(0, 2, 1), a["L0_ffn_Wu"].transpose(0, 2, 1)], 2),
        "wd4": down[:, 0:CO[4]].reshape(E, 4, CH[0], D).transpose(0, 2, 1, 3).reshape(E, CH[0], 4 * D),
        "wd2": down[:, CO[4]:I].reshape(E, 2, CH[5], D).transpose(0, 2, 1, 3).reshape(E, CH[5], 2 * D),
        **shape_constants(),
    }
    arrays = {n: np.ascontiguousarray(v) for n, v in arrays.items()}
    nc = bacc.Bacc("TRN2", target_bir_lowering=False, num_devices=1)
    dr = {n: nc.dram_tensor(f"in_{n}", v.shape, mybir.dt.from_np(v.dtype), kind="ExternalInput").ap()
          for n, v in arrays.items()}
    out = nc.dram_tensor("out", [T, D], F32, kind="ExternalOutput").ap()
    build_hybrid(nc, dr, out)
    r = run_bass_kernel_spmd(nc, [{f"in_{n}": v for n, v in arrays.items()}], core_ids=[0])
    return r.results[0]["out"].reshape(B, S, D)
```

```python
import math
from contextlib import ExitStack

import numpy as np

import concourse.bass as bass
from concourse import mybir

F32 = mybir.dt.float32
BF16 = mybir.dt.bfloat16
U16 = mybir.dt.uint16
I32 = mybir.dt.int32
U32 = mybir.dt.uint32
ALU = mybir.AluOpType
ACT = mybir.ActivationFunctionType
AX = mybir.AxisListType.X

P = 128
B, S, D = 4, 256, 256
T = B * S
NT = T // P
KD = D // P
EPS = 1e-5

HA, HDA, RD, CQ, CKV = 16, 16, 64, 192, 64
HB, HDB, KVB = 32, 8, 8
GA, GB = HA // 4, HB // 4
SCALE_A = 1.0 / math.sqrt(HDA + RD)
SCALE_B = 1.0 / math.sqrt(HDB)
CQH = CQ // 2
RA = 96
PARTS = 3
RB = PARTS * PARTS * HDB
RBZ = 96
NEG = -1e30

E, I, TOPK = 8, 688, 2
IH = I // 2
GU = 2 * I
CH = [115, 115, 115, 115, 114, 114]
CO = [0, 115, 230, 345, 460, 574]
ROUTED = T * TOPK
SLOTS_T = (ROUTED - E) // P + E
SLOTS = SLOTS_T * P


def shape_constants():
    def bf16(x):
        return (np.ascontiguousarray(x, dtype=np.float32).view(np.uint32) >> 16).astype(np.uint16)

    pos = np.arange(S, dtype=np.float32)
    fa = (1.0 / np.float32(10000.0) ** (np.arange(0, RD, 2, dtype=np.float32) / np.float32(RD))).astype(np.float32)
    aa = (pos[:, None] * fa[None, :]).astype(np.float32).T
    rope_a = np.stack([np.tile(np.cos(aa), (4, 1)), np.tile(np.sin(aa), (4, 1))], 1).astype(np.float32)
    fb = (1.0 / np.float32(10000.0) ** (np.arange(HDB // 2, dtype=np.float32) / np.float32(HDB // 2))).astype(np.float32)
    ab = (pos[:, None] * fb[None, :]).astype(np.float32).T
    rope_b = np.stack([np.repeat(np.cos(ab), HB, 0), np.repeat(np.sin(ab), HB, 0)], 1).astype(np.float32)
    rope_k = np.stack([np.tile(np.repeat(f(ab), KVB, 0), (B, 1)) for f in (np.cos, np.sin)], 1).astype(np.float32)
    q = np.arange(P)
    diag = np.where(q[None, :] > q[:, None], NEG, 0.0)
    none = np.zeros((P, P))
    masks = np.stack([np.concatenate([none, diag], 1), np.concatenate([diag.T, none], 1)], 1)
    sel = np.arange(PARTS * 32)[:, None] % 32 == np.arange(32)[None, :]
    tri = q[:, None] < q[None, :]
    e = np.arange(E, dtype=np.float32)
    small = np.concatenate([
        e,
        np.repeat(e[:, None], E, 1).T.reshape(-1) * P,
        (e[None, :] < e[:, None]).astype(np.float32).reshape(-1),
        np.arange(24, dtype=np.float32),
    ]).astype(np.float32)
    small = np.broadcast_to(small, (P, small.size)).copy()
    return {"rope_a": rope_a, "rope_b": rope_b, "rope_k": rope_k, "masks": bf16(masks), "sel": bf16(sel), "tri": bf16(tri),
            "ident": np.eye(P, dtype=np.float32), "identb": bf16(np.eye(P)),
            "onesb": bf16(np.ones((P, P))), "small": small,
            "ids": (np.arange(TOPK * NT)[None, :] * P + q[:, None]).astype(np.int32),
            "unused": (TOPK * T + np.arange(SLOTS).reshape(-1, P)).astype(np.int32)}


def build_hybrid(nc, dr, out):
    ctx = ExitStack()
    with ctx:
        def sb(name, shape, dt):
            return ctx.enter_context(nc.sbuf_tensor(name, shape, dt))

        def sem(name):
            return ctx.enter_context(nc.semaphore(name))

        wgu = sb("wgu", [P, E * KD * GU], F32)
        R1 = sb("R1", [P, E * 6 * D], F32)
        R2 = sb("R2", [P, 6144], F32)
        xres = sb("xres", [P, NT, D], F32)
        XN = sb("XN", [P, NT * D], F32)
        xnT = sb("xnT", [P, KD, T], F32)
        PTR = sb("PTR", [P, 2 * 3 * 512], F32)
        wqb = sb("wqb", [P, KD, D], F32)
        wkvb = sb("wkvb", [P, KD, 2 * KVB * HDB], F32)
        wob = sb("wob", [P, KD, D], F32)
        vaug = sb("vaug", [P, 2 * HA * 32], F32)
        rope = sb("rope", [P, 2, S], F32)
        ident = sb("ident_sb", [P, P], F32)
        identb = sb("identb_sb", [P, P], BF16)
        masks = sb("masks_sb", [P, 2, 2 * P], BF16)
        sel = sb("sel_sb", [PARTS * 32, 32], BF16)
        xn = XN[:, :].rearrange("p (t d) -> p t d", t=NT)
        wd = R1[0:CH[0], :]

        def room(o, n):
            return wgu[:, o:o + n]

        ODD = 5 * KD * GU
        stacks = [(R1[0:RA, 0:HA * S], R1[0:RA, HA * S:2 * HA * S]),
                  (room(ODD, HA * S)[0:RA, :], room(ODD + HA * S, HA * S)[0:RA, :])]
        qst, kst = ([st[i].rearrange("p (h s) -> p h s", h=HA) for st in stacks] for i in range(2))
        o = 2 * HA * S
        stage = [R1[:, o + i * 2048:o + (i + 1) * 2048].rearrange("p (n a s) -> p n a s", n=4, a=2) for i in range(2)]
        o = 3 * KD * GU
        qc = room(o, 2 * S).rearrange("p (a s) -> p a s", a=2); o += 2 * S
        kc = room(o, 2 * S).rearrange("p (a s) -> p a s", a=2); o += 2 * S
        cqT = room(o, 2 * S)[0:CQH, :].rearrange("p (a s) -> p a s", a=2); o += 2 * S
        ckvT = room(o, S)[0:CKV, :]; o += S
        rt = room(o, 2048).rearrange("p (n c a s) -> p n c a s", n=2, c=2, a=2); o += 2048
        vaug2 = room(o, 2 * HA * 32); o += 2 * HA * 32
        assert o <= ODD
        o = 0
        wdq = R2[:, o:o + KD * CQ].rearrange("p (k n) -> p k n", k=KD); o += KD * CQ
        wdkv = R2[:, o:o + KD * CKV].rearrange("p (k n) -> p k n", k=KD); o += KD * CKV
        wuq = R2[0:CQH, o:o + 2 * D].rearrange("p (k n) -> p k n", k=2); o += 2 * D
        wqr = R2[0:CQH, o:o + 2 * HA * RD].rearrange("p (k n) -> p k n", k=2); o += 2 * HA * RD
        wkr = R2[:, o:o + KD * HA * RD].rearrange("p (k n) -> p k n", k=KD); o += KD * HA * RD
        wuk = R2[0:CKV, o:o + D]; o += D
        wuv = R2[0:CKV, o:o + D]; o += D
        woa = R2[:, o:o + KD * D].rearrange("p (k n) -> p k n", k=KD); o += KD * D
        assert o == 6144
        PT = PTR[:, :].rearrange("p (n b s) -> p n b s", n=2, b=3)
        oun = XN[:, 0:512].rearrange("p (n s) -> p n s", n=2)
        otok = XN[:, 512:1024].rearrange("p (q d) -> p q d", q=2)
        oT = XN[:, 1024:1536].rearrange("p (k s) -> p k s", k=2)
        nmax = XN[:, 1536:1600].rearrange("p (q h) -> p q h", q=2)
        nrem = XN[:, 1600:1664].rearrange("p (q h) -> p q h", q=2)
        rec = XN[:, 1664:1672].rearrange("p (q j) -> p q j", q=2)
        nparts = XN[:, 1672:1768].bitcast(BF16).rearrange("p (q n h) -> p q n h", q=2, n=PARTS)
        npartf = XN[:, 1672:1768].bitcast(BF16).rearrange("p (q m) -> p q m", q=2)
        nTs = [XN[0:PARTS * 32, c:c + 128].bitcast(BF16) for c in (1768, 1896)]
        stat = sb("stat", [P, 112], F32)
        bst = stat[:, 0:NT * 6].rearrange("p (t n) -> p t n", t=NT)
        mv = stat[:, 48:48 + NT * 2].rearrange("p (t n) -> p t n", t=NT)
        var = stat[:, 64:72]
        std = stat[:, 72:80]
        rstd = stat[:, 80:88]
        slot = stat[:, 88:104].bitcast(I32)
        w01 = sb("w01", [P, 2, NT], F32)
        o = 0
        xs = R2[:, o:o + 512].rearrange("p (n d) -> p n d", n=2); o += 512
        xsT = R2[:, o:o + 512].rearrange("p (n k s) -> p n k s", n=2, k=KD); o += 512
        sg = R2[:, o:o + I]; o += I
        hh = R2[:, o:o + I]; o += I
        hT = R2[0:CH[0], o:o + 2 * 6 * P].rearrange("p (n c s) -> p n c s", n=2, c=6); o += 2 * 6 * P
        yo = R2[:, o:o + 512].rearrange("p (n d) -> p n d", n=2); o += 512
        rw = R2[:, o:o + KD * E].rearrange("p (k e) -> p k e", k=KD); o += KD * E
        lg = R2[:, o:o + 64].rearrange("p (t e) -> p t e", t=NT); o += 64
        mx = R2[:, o:o + 64].rearrange("p (t e) -> p t e", t=NT); o += 64
        mi = R2[:, o:o + 64].bitcast(U32).rearrange("p (t e) -> p t e", t=NT); o += 64
        idf = R2[:, o:o + 16].rearrange("p (k t) -> p k t", k=2); o += 16
        oh = R2[:, o:o + 128].rearrange("p (k t e) -> p k t e", k=2, t=NT); o += 128
        ohp = R2[:, o:o + 128].rearrange("p (k t e) -> p k t e", k=2, t=NT); o += 128
        cnt = R2[:, o:o + 32].bitcast(BF16); o += 32
        cmp = R2[:, o:o + 64].rearrange("p (e j) -> p e j", e=E); o += 64
        ntl = R2[:, o:o + E]; o += E
        base = R2[:, o:o + E]; o += E
        posb = R2[:, o:o + 64].rearrange("p (t e) -> p t e", t=NT); o += 64
        slf = R2[:, o:o + 16]; o += 16
        ecm = R2[0:1, o:o + 24 * 7].rearrange("p (i e) -> p i e", e=7); o += 168
        eidf = R2[0:1, o:o + 24]; o += 24
        eid = R2[0:1, o:o + 24].bitcast(I32); o += 24
        dlt = R2[:, o:o + NT]; o += NT
        ex1 = R2[:, o:o + NT]; o += NT
        den = R2[:, o:o + NT]; o += NT
        tri = R2[:, o:o + 64].bitcast(BF16); o += 64
        onesb = R2[:, o:o + 64].bitcast(BF16); o += 64
        small = R2[:, o:o + 160]; o += 160
        ids = R2[:, o:o + 16].bitcast(I32); o += 16
        rows = R2[:, o:o + 2].bitcast(I32); o += 2
        assert o <= 6144, o
        yg = PTR[:, 0:2048].rearrange("p (n k d) -> p n k d", n=4, k=2)
        heads_b = [room(6 * KD * GU, (HB + KVB) * S // 2), R2[:, 0:(HB + KVB) * S // 2]]
        qsb = [st[0:RBZ, 0:HB * S // 2].bitcast(BF16).rearrange("p (h s) -> p h s", h=HB) for st in heads_b]
        ksb = [st[0:RBZ, HB * S // 2:].bitcast(BF16).rearrange("p (h s) -> p h s", h=KVB) for st in heads_b]
        vall = R2[:, 5120:5120 + NT * 64].rearrange("p (t n) -> p t n", t=NT)
        rtb = PTR[:, 0:2048].rearrange("p (m c a s) -> p m c a s", m=2, c=2, a=2)
        rsb = PTR[:, 2048:3072].rearrange("p (m a s) -> p m a s", m=2, a=2)
        rem = XN[:, 0:512].rearrange("p (a s) -> p a s", a=2)
        qparts = XN[:, 512:2048].bitcast(BF16).rearrange("p (m n a s) -> p m n a s", m=2, n=PARTS, a=2)
        ropek = R2[:, 5632:6144].rearrange("p (c s) -> p c s", c=2)

        BK = [ctx.enter_context(nc.psum_tensor(f"bank{i}", [P, 512], F32)) for i in range(8)]

        xs_d = nc.dram_tensor("slots_in", [SLOTS, D], F32, kind="Internal").ap()
        y_d = nc.dram_tensor("rows_out", [TOPK * T + SLOTS, D], F32, kind="Internal").ap()
        rows_d = {l: nc.dram_tensor(f"row_of_slot{l}", [SLOTS, 1], I32, kind="Internal").ap() for l in (1, 3)}
        q_d = nc.dram_tensor("q_parts", [B, PARTS * HDB, HB, S], BF16, kind="Internal").ap()
        k_d = nc.dram_tensor("k_parts", [B, PARTS * HDB, KVB, S], BF16, kind="Internal").ap()

        s_const = sem("s_const")
        s_x = [sem(f"s_x{b}") for b in range(B)]
        s_wa = sem("s_wa")
        s_wb = sem("s_wb")
        s_wgu = sem("s_wgu")
        s_wd = sem("s_wd")
        s_rows = sem("s_rows")
        s_zero = sem("s_zero")
        s_init = sem("s_init")
        s_out = sem("s_out")


        s_own = sem("s_own")

        def named(prefix, names):
            return {n: sem(f"{prefix}_{n}") for n in names.split()}

        LN = [named(f"ln{l}", "vareps root normed transposed evac") for l in range(4)]
        AN = ("placed values scores maxima lo max_t max_e shifted exps pv pv_e out_t "
              "divided all_t all_e projected added")
        AT = {0: named("at0", AN), 2: named("at2", AN)}
        PA = named("pa", "item evac_s evac_v summed placed_k")
        PB = named("pb", "placed_2 item prod summed lo stored_k stored0 stored1 zeroed vall")
        FN = ("consts logits count rank1 "
              "slot eid dlt exp1 scatter xs0 xs1 x_t x_e gu silu hid hid_t hte_v hte_s "
              "down y_e row0 row1 rows ys0 ys1 g0 g1 g2 g3 added")
        FF = {1: named("ff1", FN), 3: named("ff3", FN)}


        def later(eng, sem, count):
            if not (isinstance(count, int) and count == 0):
                eng.wait_ge(sem, count)

        own = [0]

        def link(*ops):
            for op in ops:
                op.then_inc(s_own, 1)
            own[0] += len(ops)
            nc.vector.wait_ge(s_own, own[0])

        def stats_vector(l, b, x_ready=None):
            s = LN[l]
            v = nc.vector
            tiles = range(2 * b, 2 * b + 2)
            if x_ready is not None:
                v.wait_ge(*x_ready)
            link(*[v.bn_stats(bst[:, t, :], xres[:, t, :]) for t in tiles])
            link(*[v.bn_aggr(mv[:, t, :], bst[:, t, :]) for t in tiles])
            v.tensor_scalar_add(var[:, 2 * b:2 * b + 2], mv[:, 2 * b:2 * b + 2, 1], EPS).then_inc(s["vareps"], 1)

        def normed_vector(l, b):
            s = LN[l]
            v = nc.vector
            v.wait_ge(s["root"], b + 1)
            link(v.reciprocal(rstd[:, 2 * b:2 * b + 2], std[:, 2 * b:2 * b + 2]))
            for t in range(2 * b, 2 * b + 2):
                last = v.tensor_scalar(xn[:, t, :], xres[:, t, :], mv[:, t, 0:1], rstd[:, t:t + 1],
                                       ALU.subtract, ALU.mult)
                last.then_inc(s["normed"], 1)

        def root_scalar(l, b):
            s = LN[l]
            nc.scalar.wait_ge(s["vareps"], b + 1)
            nc.scalar.activation(std[:, 2 * b:2 * b + 2], var[:, 2 * b:2 * b + 2], ACT.Sqrt).then_inc(s["root"], 1)

        def evac_scalar(l, b):
            s = LN[l]
            nc.scalar.wait_ge(s["transposed"], b + 1)
            nc.scalar.activation(xnT[:, :, b * S:(b + 1) * S], BK[b][:, :].rearrange("p (k s) -> p k s", k=KD),
                                 ACT.Copy).then_inc(s["evac"], 1)

        def norm_tensor(l, b):
            s = LN[l]
            nc.tensor.wait_ge(s["normed"], 2 * b + 2)
            for k in range(KD):
                for t in range(2):
                    last = nc.tensor.transpose(BK[b][:, k * S + t * P:k * S + (t + 1) * P],
                                               xn[:, 2 * b + t, k * P:(k + 1) * P], ident[:, :])
            last.then_inc(s["transposed"], 1)

        def norm_vector(l, ahead):
            for b in range(B + 1):
                if b < B:
                    stats_vector(l, b, ahead(b))
                if b >= 1:
                    normed_vector(l, b - 1)

        def norm_scalar(l):
            for b in range(B + 1):
                if b < B:
                    root_scalar(l, b)
                if b >= 1:
                    evac_scalar(l, b - 1)

        def heads(l, b=0):
            if l == 0:
                return GA, (lambda h: qst[b % 2][:, h, :]), (lambda h: kst[b % 2][:, h, :]), (lambda h: h), HDA, SCALE_A, woa
            return (GB, (lambda h: qsb[b % 2][:, h, :]), (lambda h: ksb[b % 2][:, h // 4, :]), (lambda h: h // 4), HDB,
                    SCALE_B, wob)

        def values_of(l, b):
            n = HA if l == 0 else KVB
            return (vaug2 if l == 0 and b % 2 == 0 else vaug)[:, 0:2 * n * 32].rearrange("p (n h c) -> p n h c", n=2, c=32)

        def banks(l, g, shifted):
            first = 3 * (g % 2) if l == 0 else 0 if shifted else 3
            return BK[first:first + 3]

        def scores_tensor(l, b, g):
            s = AT[l]
            G, q, k, v, hd, scale, wo = heads(l, b)
            bank = banks(l, g, False)
            if g == 0 and l == 0:
                if b == 0:
                    nc.tensor.wait_ge(PA["evac_v"], 2 * len(BY_V) - len(LATE))
                    nc.tensor.wait_ge(PA["evac_s"], 2 * len(BY_S))
                nc.tensor.wait_ge(PA["placed_k"], b * PLACED_K + PLACED_K)
                nc.tensor.wait_ge(s["placed"], b * PLACED_A + PLACED_A)
            if g == 0 and l == 2:
                if b == 0:
                    nc.tensor.wait_ge(PB["vall"], 1)
                    nc.tensor.wait_ge(PB["prod"], B + 1)
                nc.tensor.wait_ge(s["placed"], b * PLACED_B + PLACED_B)
            if g == G // 2 and l == 2:
                nc.tensor.wait_ge(PB["placed_2"], b * PLACED_B + PLACED_B)

            def free(i):
                if l == 2:
                    later(nc.tensor, s["maxima"], max(3 * (b * G + g - 1) + i + 1, 0))
                    if i == 2 and g == 0:
                        later(nc.tensor, s["max_e"], b)
                elif i == 0 and g >= 2:
                    nc.tensor.wait_ge(s["maxima"], b * 3 * G + 3 * (g - 1))

            free(0)
            nc.tensor.matmul(bank[0][:, :].rearrange("p (n s) -> p n s", n=4), identb[:, :],
                             masks[:, 0, None, P:2 * P].broadcast_to([P, 4, P]),
                             start=True, stop=False, skip_group_check=True)
            for j in range(4):
                h = 4 * g + j
                last = nc.tensor.matmul(bank[0][:, j * P:(j + 1) * P], q(h)[:, 0:P], k(h)[:, 0:P],
                                        start=False, stop=j == 3, skip_group_check=True)
            last.then_inc(s["scores"], 1)
            for i in range(2):
                free(1 + i)
                nc.tensor.matmul(bank[1 + i][:, :].rearrange("p (n s) -> p n s", n=2)[:, :, P:S], identb[:, :],
                                 masks[:, 0, None, P:2 * P].broadcast_to([P, 2, P]),
                                 start=True, stop=False, skip_group_check=True)
                for j in range(2):
                    h = 4 * g + 2 * i + j
                    last = nc.tensor.matmul(bank[1 + i][:, j * S:(j + 1) * S], q(h)[:, P:S], k(h)[:, :],
                                            start=False, stop=j == 1, skip_group_check=True)
                last.then_inc(s["scores"], 1)

        def max_tensor(l, b):
            s = AT[l]
            nc.tensor.wait_ge(s["lo"], b + 1)
            if l == 0:
                later(nc.tensor, s["all_e"], b)
            for t in range(2):
                last = nc.tensor.transpose(BK[5 if l else 7][0:PARTS * 32, :].bitcast(BF16)[:, t * P:(t + 1) * P],
                                           npartf[:, t, :], identb[:, :])
            last.then_inc(s["max_t"], 1)

        def shifted_tensor(l, b, g):
            s = AT[l]
            G, q, k, v, hd, scale, wo = heads(l, b)
            bank, nT = banks(l, g, True), nTs[b % 2]
            if g == 0:
                nc.tensor.wait_ge(s["max_e"], b + 1)

            def free(i):
                if l == 2:
                    later(nc.tensor, s["exps"], max(3 * (b * G + g - 1) + i + 1, 0))
                elif i == 0 and g < 2:
                    nc.tensor.wait_ge(s["maxima"], (b + 1) * 3 * G)
                elif i == 0:
                    nc.tensor.wait_ge(s["exps"], b * 3 * G + 3 * (g - 1))

            for i in range(2):
                free(i)
                nc.tensor.matmul(bank[i][:, :].rearrange("p (n s) -> p n s", n=2)[:, :, 0:P], identb[:, :],
                                 masks[:, 1, None, 0:P].broadcast_to([P, 2, P]),
                                 start=True, stop=False, skip_group_check=True)
                for j in range(2):
                    h = 4 * g + 2 * i + j
                    nc.tensor.matmul(bank[i][:, j * S:(j + 1) * S], sel[:, h:h + 1].broadcast_to([PARTS * 32, P]),
                                     nT[:, :], start=False, stop=False, skip_group_check=True)
                    last = nc.tensor.matmul(bank[i][:, j * S:(j + 1) * S], k(h)[:, 0:P], q(h)[:, :],
                                            start=False, stop=j == 1, skip_group_check=True)
                last.then_inc(s["shifted"], 1)
            free(2)
            nc.tensor.matmul(bank[2][:, :].rearrange("p (n s) -> p n s", n=4), identb[:, :],
                             masks[:, 1, None, 0:P].broadcast_to([P, 4, P]),
                             start=True, stop=False, skip_group_check=True)
            for j in range(4):
                h = 4 * g + j
                nc.tensor.matmul(bank[2][:, j * P:(j + 1) * P], sel[:, h:h + 1].broadcast_to([PARTS * 32, P]),
                                 nT[:, P:S], start=False, stop=False, skip_group_check=True)
                last = nc.tensor.matmul(bank[2][:, j * P:(j + 1) * P], k(h)[:, P:S], q(h)[:, P:S],
                                        start=False, stop=j == 3, skip_group_check=True)
            last.then_inc(s["shifted"], 1)

        def pv_tensor(l, b, g):
            s = AT[l]
            G, q, k, v, hd, scale, wo = heads(l, b)
            va, n = values_of(l, b), g % 2
            nc.tensor.wait_ge(s["exps"], b * 3 * G + 3 * (g + 1))
            later(nc.tensor, s["pv_e"], b * G + g)
            if g == (2 if l else 0):
                later(nc.tensor, s["added"], b)
            if g == 0 and l == 0:
                nc.tensor.wait_ge(PA["evac_s"], (b + 1) * len(BY_S))
            elif g == 0:
                nc.tensor.wait_ge(s["values"], b + 1)
            for j in range(4):
                nc.tensor.matmul(BK[6][32 * j:32 * j + 32, 0:S], va[:, 0, v(4 * g + j), :],
                                 PT[:, n, j // 2, (j % 2) * S:(j % 2 + 1) * S],
                                 start=True, stop=False, skip_group_check=True, tile_position=(0, 32 * j))
            for j in range(4):
                last = nc.tensor.matmul(BK[6][32 * j:32 * j + 32, P:S], va[:, 1, v(4 * g + j), :],
                                        PT[:, n, 2, j * P:(j + 1) * P],
                                        start=False, stop=True, skip_group_check=True, tile_position=(0, 32 * j))
            last.then_inc(s["pv"], 1)

        def out_t_tensor(l, b, g):
            s = AT[l]
            G = heads(l)[0]
            nc.tensor.wait_ge(s["pv_e"], b * G + g + 1)
            later(nc.tensor, s["divided"], b * G + g)
            if g == 0:
                later(nc.tensor, s["all_e"], b)
            for t in range(2):
                last = nc.tensor.transpose(BK[7][:, t * P:(t + 1) * P], oun[:, g % 2, t * P:(t + 1) * P], ident[:, :])
            last.then_inc(s["out_t"], 1)

        def all_t_tensor(l, b):
            s = AT[l]
            G = heads(l)[0]
            nc.tensor.wait_ge(s["divided"], b * G + G)
            for kk in range(KD):
                for t in range(2):
                    last = nc.tensor.transpose(BK[7][:, (2 * kk + t) * P:(2 * kk + t + 1) * P],
                                               otok[:, t, kk * P:(kk + 1) * P], ident[:, :])
            last.then_inc(s["all_t"], 1)

        def project_tensor(l, b):
            s = AT[l]
            G, wo = heads(l)[0], heads(l)[6]
            nc.tensor.wait_ge(s["all_e"], b + 1)
            if l == 2 and b < B - 1:
                nc.tensor.wait_ge(s["pv_e"], (b + 1) * G + 2)
            for t in range(2):
                for kk in range(KD):
                    last = nc.tensor.matmul(BK[6][:, t * D:(t + 1) * D], oT[:, kk, t * P:(t + 1) * P], wo[:, kk, :],
                                            start=kk == 0, stop=kk == KD - 1)
            last.then_inc(s["projected"], 1)

        def add_vector(l, b):
            s = AT[l]
            nc.vector.wait_ge(s["projected"], b + 1)
            xb = xres[:, 2 * b:2 * b + 2, :]
            nc.vector.tensor_tensor(xb, xb, BK[6][:, :].rearrange("p (q d) -> p q d", q=2), ALU.add).then_inc(s["added"], 1)

        def maxima_vector(l, b, g):
            s = AT[l]
            G = heads(l)[0]
            bank = banks(l, g, False)
            nc.vector.wait_ge(s["scores"], b * 3 * G + 3 * g + 1)
            nc.vector.tensor_reduce(nmax[:, 0, 4 * g:4 * g + 4], bank[0][:, :].rearrange("p (n s) -> p n s", n=4),
                                    AX, ALU.max, negate=True).then_inc(s["maxima"], 1)
            for i in range(2):
                nc.vector.wait_ge(s["scores"], b * 3 * G + 3 * g + 2 + i)
                nc.vector.tensor_reduce(nmax[:, 1, 4 * g + 2 * i:4 * g + 2 * i + 2],
                                        bank[1 + i][:, :].rearrange("p (n s) -> p n s", n=2),
                                        AX, ALU.max, negate=True).then_inc(s["maxima"], 1)

        def parts_vector(l, b):
            s = AT[l]
            G = heads(l)[0]
            nh = 4 * G
            nc.vector.wait_ge(s["maxima"], (b + 1) * 3 * G)
            later(nc.vector, s["max_t"], b)
            link(nc.vector.tensor_copy(nparts[:, :, 0, 0:nh], nmax[:, :, 0:nh]))
            link(nc.vector.tensor_tensor(nrem[:, :, 0:nh], nmax[:, :, 0:nh], nparts[:, :, 0, 0:nh], ALU.subtract))
            link(nc.vector.tensor_copy(nparts[:, :, 1, 0:nh], nrem[:, :, 0:nh]))
            nc.vector.tensor_tensor(nparts[:, :, 2, 0:nh], nrem[:, :, 0:nh], nparts[:, :, 1, 0:nh], ALU.subtract).then_inc(s["lo"], 1)

        def pv_vector(l, b, g):
            s = AT[l]
            n = b * heads(l)[0] + g
            nc.vector.wait_ge(s["pv"], n + 1)
            later(nc.vector, s["out_t"], max(n - 1, 0))
            nc.vector.tensor_copy(oun[:, g % 2, :], BK[6][:, 0:S]).then_inc(s["pv_e"], 1)

        def divide_vector(l, b, g):
            s = AT[l]
            G, hd = heads(l)[0], heads(l)[4]
            tt = BK[7][:, 0:S].rearrange("p (q j c) -> p q j c", q=2, c=32)
            nc.vector.wait_ge(s["out_t"], b * G + g + 1)
            link(nc.vector.reciprocal(rec[:, :, :], tt[:, :, :, hd]))
            if g == 0:
                later(nc.vector, s["all_t"], b)
            nc.vector.tensor_tensor(otok[:, :, 4 * g * hd:4 * (g + 1) * hd].rearrange("p q (j c) -> p q j c", j=4),
                                    tt[:, :, :, 0:hd], rec[:, :, :, None].broadcast_to([P, 2, 4, hd]),
                                    ALU.mult).then_inc(s["divided"], 1)

        def max_scalar(l, b):
            s = AT[l]
            nc.scalar.wait_ge(s["max_t"], b + 1)
            nc.scalar.activation(nTs[b % 2][:, :], BK[5 if l else 7][0:PARTS * 32, :].bitcast(BF16)[:, 0:S],
                                 ACT.Copy).then_inc(s["max_e"], 1)

        def exps_scalar(l, b, g):
            s = AT[l]
            G, scale = heads(l)[0], heads(l)[5]
            n = b * G + g
            for i in range(3):
                nc.scalar.wait_ge(s["shifted"], 3 * n + i + 1)
                if i == 0:
                    later(nc.scalar, s["pv"], max(n - 1, 0))
                nc.scalar.activation(PT[:, g % 2, i, :], banks(l, g, True)[i][:, :], ACT.Exp, scale=scale).then_inc(s["exps"], 1)

        def out_scalar(l, b):
            s = AT[l]
            nc.scalar.wait_ge(s["all_t"], b + 1)
            nc.scalar.activation(oT[:, :, :], BK[7][:, :].rearrange("p (k s) -> p k s", k=KD), ACT.Copy).then_inc(s["all_e"], 1)

        def attend_a_tensor(b):
            max_tensor(0, b)
            nc.tensor.wait_ge(AT[0]["max_e"], b + 1)
            if b < B - 1:
                nc.tensor.wait_ge(PA["evac_v"], (b + 2) * len(BY_V))
                nc.tensor.wait_ge(PA["evac_s"], (b + 2) * len(BY_S))
            for g in range(GA + 2):
                if g < GA:
                    shifted_tensor(0, b, g)
                if 1 <= g <= GA:
                    pv_tensor(0, b, g - 1)
                if g >= 2:
                    out_t_tensor(0, b, g - 2)

        def maxima_a_vector(b):
            for g in range(GA):
                maxima_vector(0, b, g)
            parts_vector(0, b)
            if b > 0:
                add_vector(0, b - 1)

        def attend_a_vector(b):
            for g in range(GA):
                pv_vector(0, b, g)
                if g >= 1:
                    divide_vector(0, b, g - 1)
            divide_vector(0, b, GA - 1)

        def attend_a_scalar(b):
            max_scalar(0, b)
            for g in range(GA):
                exps_scalar(0, b, g)

        RUN = B * GB

        def scores_in(n):
            b, g = n // GB + 1, n % GB
            if b >= B or g == GB - 1:
                return []
            return [(b, 0), (b, 1)] if g == 0 else [(b, g + 1)]

        def attend_b_tensor():
            for g in range(GB):
                scores_tensor(2, 0, g)
            max_tensor(2, 0)
            for n in range(RUN + 3):
                b, g = n // GB, n % GB
                ahead = scores_in(n)
                if g == 0 and ahead:
                    scores_tensor(2, *ahead.pop(0))
                if n < RUN:
                    shifted_tensor(2, b, g)
                if g == 2 and b > 0:
                    all_t_tensor(2, b - 1)
                if g == 3 and b > 0 or n == RUN + 2:
                    project_tensor(2, b - 1)
                for bb, gg in ahead:
                    scores_tensor(2, bb, gg)
                if 1 <= n <= RUN:
                    pv_tensor(2, (n - 1) // GB, (n - 1) % GB)
                if 2 <= n < RUN + 2:
                    out_t_tensor(2, (n - 2) // GB, (n - 2) % GB)
                if g == GB - 1 and b < B - 1:
                    max_tensor(2, b + 1)

        def attend_b_vector():
            for g in range(GB):
                maxima_vector(2, 0, g)
            parts_vector(2, 0)
            for n in range(RUN + 3):
                b, g = n // GB, n % GB
                ahead = scores_in(n)
                if g == 0 and ahead:
                    maxima_vector(2, *ahead.pop(0))
                if g == 3 and b > 0 or n == RUN + 2:
                    add_vector(2, b - 1)
                for bb, gg in ahead:
                    maxima_vector(2, bb, gg)
                if g == GB - 1 and b < B - 1:
                    parts_vector(2, b + 1)
                if 1 <= n <= RUN:
                    pv_vector(2, (n - 1) // GB, (n - 1) % GB)
                if 2 <= n < RUN + 2:
                    divide_vector(2, (n - 2) // GB, (n - 2) % GB)

        def attend_b_scalar():
            max_scalar(2, 0)
            for n in range(RUN + 3):
                b, g = n // GB, n % GB
                if n < RUN:
                    exps_scalar(2, b, g)
                    if g == 0:
                        values_b_scalar(b)
                if g == 2 and b > 0:
                    out_scalar(2, b - 1)
                if g == GB - 1 and b < B - 1:
                    max_scalar(2, b + 1)

        ITEMS = 13
        BY_V = [1, 2, 3, 4, 5, 9, 10, 11, 12]
        BY_S = [0, 6, 7, 8]
        ROT = [2, 3, 4, 5, 9, 10, 11, 12]
        PLACED_A = 16 * (2 * 8 + 8)
        PLACED_K = 16 * 8

        def wait_item(eng, b, i):
            if i in BY_V:
                eng.wait_ge(PA["evac_v"], b * len(BY_V) + BY_V.index(i) + 1)
            else:
                eng.wait_ge(PA["evac_s"], b * len(BY_S) + BY_S.index(i) + 1)

        EARLY, LATE = range(ITEMS - 2), range(ITEMS - 2, ITEMS)

        def project_a_tensor(b, items=range(ITEMS)):
            if b < 2:
                nc.tensor.wait_ge(LN[0]["evac"], B)
            xb = [xnT[:, kk, bass.ds(b * S, S)] for kk in range(KD)]
            for i in items:
                bk = BK[i % 6]
                if b == 1 and i == LATE[0]:
                    nc.tensor.wait_ge(AT[0]["maxima"], 3 * GA)
                if i >= 6:
                    wait_item(nc.tensor, b, i - 6)
                elif b == 1:
                    wait_item(nc.tensor, 0, i + 6 if i else 12)
                elif b > 1 and i == 0:
                    nc.tensor.wait_ge(AT[0]["maxima"], b * 3 * GA)
                if i == 0:
                    ops = [(bk[0:CQH, m * S:(m + 1) * S], wdq[:, kk, m * CQH:(m + 1) * CQH], xb[kk], kk)
                           for m in range(2) for kk in range(KD)]
                elif i == 1:
                    ops = [(bk[0:CKV, 0:S], wdkv[:, kk, :], xb[kk], kk) for kk in range(KD)]
                elif i < 6:
                    ops = [(bk[:, a * S:(a + 1) * S], wkr[:, kk, ((i - 2) * 2 + a) * P:((i - 2) * 2 + a + 1) * P], xb[kk], kk)
                           for a in range(2) for kk in range(KD)]
                elif i == 6:
                    ops = [(bk[:, m * S:(m + 1) * S], wuq[:, kk, m * P:(m + 1) * P], cqT[:, kk, :], kk)
                           for m in range(2) for kk in range(2)]
                elif i == 7:
                    wait_item(nc.tensor, b, 1)
                    ops = [(bk[:, m * S:(m + 1) * S], wuk[:, m * P:(m + 1) * P], ckvT[:, :], None) for m in range(2)]
                elif i == 8:
                    ops = [(bk[:, m * D:(m + 1) * D], ckvT[:, m * P:(m + 1) * P], wuv[:, :], None) for m in range(2)]
                else:
                    ops = [(bk[:, a * S:(a + 1) * S], wqr[:, kk, ((i - 9) * 2 + a) * P:((i - 9) * 2 + a + 1) * P], cqT[:, kk, :], kk)
                           for a in range(2) for kk in range(2)]
                for dst, w, r, kk in ops:
                    last = nc.tensor.matmul(dst, w, r, start=kk in (0, None), stop=kk in (1, None))
                last.then_inc(PA["item"], 1)

        def project_a_vector(b, items=range(ITEMS)):
            for i in [i for i in BY_V if i in items]:
                bk = BK[i % 6]
                nc.vector.wait_ge(PA["item"], b * ITEMS + i + 1)
                if i == 1:
                    nc.vector.tensor_copy(ckvT[:, :], bk[0:CKV, 0:S]).then_inc(PA["evac_v"], 1)
                    continue
                r = ROT.index(i)
                if b * len(ROT) + r >= 2:
                    nc.vector.wait_ge(PA["summed"], b * len(ROT) + r - 1)
                v = bk[:, :].rearrange("p (a s) -> p a s", a=2)
                nc.vector.tensor_tensor(rt[:, r % 2, 0, :, :], v, rope[:, 0, None, :].broadcast_to([P, 2, S]), ALU.mult)
                nc.vector.tensor_tensor(rt[:, r % 2, 1, :, :], v, rope[:, 1, None, :].broadcast_to([P, 2, S]),
                                        ALU.mult).then_inc(PA["evac_v"], 1)

        def project_a_scalar(b):
            for i in BY_S:
                bk = BK[i % 6]
                nc.scalar.wait_ge(PA["item"], b * ITEMS + i + 1)
                if i == 0:
                    dst, src = cqT[:, :, :], bk[0:CQH, :].rearrange("p (a s) -> p a s", a=2)
                elif i == 6:
                    later(nc.scalar, AT[0]["placed"], b * PLACED_A)
                    dst, src = qc[:, :, :], bk[:, :].rearrange("p (a s) -> p a s", a=2)
                elif i == 7:
                    dst, src = kc[:, :, :], bk[:, :].rearrange("p (a s) -> p a s", a=2)
                else:
                    dst = (vaug if b % 2 else vaug2)[:, :].rearrange("p (n h c) -> p n h c", n=2, c=32)[:, :, :, 0:HDA]
                    src = bk[:, :].rearrange("p (n h c) -> p n h c", n=2, c=HDA)
                nc.scalar.activation(dst, src, ACT.Copy).then_inc(PA["evac_s"], 1)

        def project_a_gpsimd(b):
            for r in range(len(ROT)):
                nc.gpsimd.wait_ge(PA["evac_v"], b * len(BY_V) + BY_V.index(ROT[r]) + 1)
                dst = stage[r // 4][:, r % 4, :, :]
                if r == 0:
                    later(nc.gpsimd, PA["placed_k"], b * PLACED_K)
                if r == 4:
                    later(nc.gpsimd, AT[0]["placed"], b * PLACED_A)
                t = rt[:, r % 2, :, :, :]
                nc.gpsimd.tensor_tensor(dst[:, 0, :], t[:, 0, 0, :], t[:, 1, 1, :], ALU.subtract)
                nc.gpsimd.tensor_tensor(dst[:, 1, :], t[:, 0, 1, :], t[:, 1, 0, :], ALU.add).then_inc(PA["summed"], 1)

        def place_a_sync(b):
            if b >= 2:
                nc.sync.wait_ge(AT[0]["shifted"], (b - 1) * 3 * GA)

            def rotated(dst, n, s):
                nc.sync.wait_ge(PA["summed"], b * len(ROT) + 4 * (n + 1))
                for a in range(2):
                    for j in range(4):
                        nc.sync.dma_start(dst[32 + 32 * a:64 + 32 * a, j:HA:4, :],
                                          stage[n][32 * j:32 * j + 32, :, a, :]).then_inc(s, 16)

            rotated(kst[b % 2], 0, PA["placed_k"])
            for i, dst, src in ((6, qst[b % 2], qc), (7, kst[b % 2], kc)):
                wait_item(nc.sync, b, i)
                for j in range(8):
                    nc.sync.dma_start(dst[0:16, j:16:8, :], src[16 * j:16 * j + 16, :, :]).then_inc(AT[0]["placed"], 16)
            rotated(qst[b % 2], 1, AT[0]["placed"])

        PLACED_B = 16 * (PARTS + PARTS * PARTS)

        def project_b_tensor():
            s = PB
            for i in range(B + 1):
                bk = BK[i % 2]
                if i >= 2:
                    nc.tensor.wait_ge(s["prod"], i - 1)
                for a in range(2):
                    if i >= 1:
                        for kk in range(KD):
                            last = nc.tensor.matmul(bk[:, a * S:(a + 1) * S], wqb[:, kk, a * P:(a + 1) * P],
                                                    xnT[:, kk, (i - 1) * S:i * S], start=kk == 0, stop=kk == KD - 1)
                    else:
                        for b in range(B):
                            for kk in range(KD):
                                last = nc.tensor.matmul(bk[32 * b:32 * b + 32, a * S:(a + 1) * S],
                                                        wkvb[:, kk, a * 32:(a + 1) * 32], xnT[:, kk, b * S:(b + 1) * S],
                                                        start=kk == 0, stop=kk == KD - 1,
                                                        tile_position=(0, 32 * b), skip_group_check=True)
                last.then_inc(s["item"], 1)
            for t in range(NT):
                for kk in range(KD):
                    last = nc.tensor.matmul(BK[2][:, t * 64:(t + 1) * 64], xnT[:, kk, t * P:(t + 1) * P],
                                            wkvb[:, kk, 64:128], start=kk == 0, stop=kk == KD - 1)
            last.then_inc(s["item"], 1)

        def project_b_vector():
            s = PB
            def split(i):
                hi, mid, lo = (qparts[:, i % 2, n, :, :] for n in range(PARTS))
                rs = rsb[:, i % 2, :, :]
                nc.vector.wait_ge(s["summed"], i + 1)
                if i == 2:
                    nc.vector.wait_ge(s["stored_k"], 16 * B)
                elif i > 2:
                    nc.vector.wait_ge(s[f"stored{i % 2}"], 16)
                link(nc.vector.tensor_copy(hi, rs))
                link(nc.vector.tensor_tensor(rem[:, :, :], rs, hi, ALU.subtract))
                link(nc.vector.tensor_copy(mid, rem[:, :, :]))
                nc.vector.tensor_tensor(lo, rem[:, :, :], mid, ALU.subtract).then_inc(s["lo"], 1)

            for i in range(B + 1):
                bk = BK[i % 2][:, :].rearrange("p (a s) -> p a s", a=2)
                table = rope if i >= 1 else ropek
                nc.vector.wait_ge(s["item"], i + 1)
                if i >= 2:
                    nc.vector.wait_ge(s["summed"], i - 1)
                nc.vector.tensor_tensor(rtb[:, i % 2, 0, :, :], bk, table[:, 0, None, :].broadcast_to([P, 2, S]), ALU.mult)
                nc.vector.tensor_tensor(rtb[:, i % 2, 1, :, :], bk, table[:, 1, None, :].broadcast_to([P, 2, S]),
                                        ALU.mult).then_inc(s["prod"], 1)
                if i >= 1:
                    split(i - 1)
            split(B)
            nc.vector.wait_ge(s["stored0"], 16 * 2)
            nc.vector.wait_ge(s["stored1"], 16 * 2)

        def project_b_gpsimd():
            s = PB
            for i in range(B + 1):
                m = i % 2
                nc.gpsimd.wait_ge(s["prod"], i + 1)
                if i >= 2:
                    nc.gpsimd.wait_ge(s["lo"], i - 1)
                nc.gpsimd.tensor_tensor(rsb[:, m, 0, :], rtb[:, m, 0, 0, :], rtb[:, m, 1, 1, :], ALU.subtract)
                nc.gpsimd.tensor_tensor(rsb[:, m, 1, :], rtb[:, m, 0, 1, :], rtb[:, m, 1, 0, :], ALU.add).then_inc(s["summed"], 1)
            nc.gpsimd.wait_ge(s["summed"], B + 1)
            nc.gpsimd.memset(heads_b[1][64:RBZ, :], 0.0).then_inc(s["zeroed"], 1)

        def project_b_scalar():
            store_b_scalar()
            nc.scalar.wait_ge(PB["item"], B + 2)
            nc.scalar.activation(vall[:, :, :], BK[2][:, :].rearrange("p (t n) -> p t n", t=NT), ACT.Copy).then_inc(PB["vall"], 1)

        def values_b_scalar(b):
            va = values_of(2, b)
            nc.scalar.wait_ge(PB["vall"], 1)
            later(nc.scalar, AT[2]["pv"], b * GB)
            nc.scalar.activation(va[:, :, :, 0:HDB], vall[:, 2 * b:2 * b + 2, :].rearrange("p n (h c) -> p n h c", c=HDB),
                                 ACT.Copy).then_inc(AT[2]["values"], 1)

        def store_b_scalar():
            for i in range(B + 1):
                nc.scalar.wait_ge(PB["lo"], i + 1)
                for b in range(B) if i == 0 else [i - 1]:
                    if i == 0:
                        dst, src, stored = k_d[b], qparts[32 * b:32 * b + 32, 0, :, :, :], PB["stored_k"]
                    else:
                        dst, src, stored = q_d[b], qparts[:, i % 2, :, :, :], PB[f"stored{i % 2}"]
                    nc.scalar.dma_start(dst.rearrange("(m i) h s -> (i h) m s", i=HDB // 2),
                                        src.rearrange("p n a s -> p (n a) s")).then_inc(stored, 16)

        def place_b_sync(b):
            if b < 2:
                nc.sync.wait_ge(PB["zeroed"], b + 1)
            if b == 0:
                nc.sync.wait_ge(PB["stored_k"], 16 * B)
            nc.sync.wait_ge(PB[f"stored{(b + 1) % 2}"], 16 * (b // 2 + 1))
            if b == 1:
                nc.sync.wait_ge(AT[2]["placed"], PLACED_B)
                nc.sync.wait_ge(PB["placed_2"], PLACED_B)
            for half in range(2):
                if b >= 2:
                    nc.sync.wait_ge(AT[2]["shifted"], (b - 2) * 3 * GB + (half + 1) * 3 * GB // 2)
                s = PB["placed_2"] if half else AT[2]["placed"]
                hq, hk = slice(half * HB // 2, (half + 1) * HB // 2), slice(half * KVB // 2, (half + 1) * KVB // 2)
                for m in range(PARTS):
                    r = m * PARTS * HDB
                    nc.sync.dma_start(qsb[b % 2][r:r + PARTS * HDB, hq, :], q_d[b, :, hq, :]).then_inc(s, 16)
                    for n in range(PARTS):
                        nc.sync.dma_start(ksb[b % 2][r + n * HDB:r + (n + 1) * HDB, hk, :],
                                          k_d[b, m * HDB:(m + 1) * HDB, hk, :]).then_inc(s, 16)

        def route_tensor(l):
            s = FF[l]
            for t in range(NT):
                for kk in range(KD):
                    last = nc.tensor.matmul(BK[7][:, t * E:(t + 1) * E], xnT[:, kk, t * P:(t + 1) * P], rw[:, kk, :],
                                            start=kk == 0, stop=kk == KD - 1)
            last.then_inc(s["logits"], 1)
            nc.tensor.wait_ge(s["count"], 1)
            for t in range(NT + 1):
                for u in range(t + 1) if t < NT else range(NT):
                    if t < NT:
                        lhsT = tri if u == t else onesb
                        stop = u == t
                    else:
                        lhsT, stop = onesb, u == NT - 1
                    last = nc.tensor.matmul(BK[6][:, t * E:(t + 1) * E], lhsT[:, :], cnt[:, u * E:(u + 1) * E],
                                            start=u == 0, stop=stop)
            last.then_inc(s["rank1"], 1)

        def route_vector(l):
            s = FF[l]
            v = nc.vector

            v.wait_ge(s["consts"], 16 * 5)
            v.wait_ge(s["logits"], 1)
            link(v.tensor_copy(lg, BK[7][:, 0:NT * E].rearrange("p (t e) -> p t e", t=NT)))
            link(*[v.max(mx[:, t, :], lg[:, t, :]) for t in range(NT)])
            v.tensor_tensor(dlt, mx[:, :, 1], mx[:, :, 0], ALU.subtract).then_inc(s["dlt"], 1)
            link(*[v.max_index(mi[:, t, :], mx[:, t, :], lg[:, t, :]) for t in range(NT)])
            link(v.tensor_copy(idf, mi[:, :, 0:2].rearrange("p t k -> p k t")))
            link(*[v.tensor_tensor(oh[:, k, :, :], small[:, None, 0:E].broadcast_to([P, NT, E]),
                                   idf[:, k, :, None].broadcast_to([P, NT, E]), ALU.is_equal) for k in range(TOPK)])
            v.tensor_tensor(cnt.rearrange("p (t e) -> p t e", t=NT), oh[:, 0, :, :], oh[:, 1, :, :], ALU.add).then_inc(s["count"], 1)
            v.wait_ge(s["exp1"], 1)
            link(v.tensor_scalar_add(den, ex1, 1.0))
            link(v.reciprocal(w01[:, 0, :], den))
            link(v.tensor_tensor(w01[:, 1, :], ex1, w01[:, 0, :], ALU.mult))
            v.wait_ge(s["rank1"], 1)
            link(v.tensor_tensor(cmp, BK[6][:, NT * E:(NT + 1) * E, None].broadcast_to([P, E, 8]),
                                 small[:, 8:72].rearrange("p (e j) -> p e j", e=E), ALU.is_gt))
            link(v.tensor_reduce(ntl, cmp, AX, ALU.add))
            link(v.tensor_tensor(cmp, ntl[:, None, :].broadcast_to([P, E, E]),
                                 small[:, 72:136].rearrange("p (e j) -> p e j", e=E), ALU.mult))
            link(v.tensor_reduce(base, cmp, AX, ALU.add))
            link(v.scalar_tensor_tensor(out=posb, in0=base[:, None, :].broadcast_to([P, NT, E]), scalar=float(P),
                                        in1=BK[6][:, 0:NT * E].rearrange("p (t e) -> p t e", t=NT),
                                        op0=ALU.mult, op1=ALU.add))
            link(v.tensor_tensor(ohp, oh, posb[:, None, :, :].broadcast_to([P, 2, NT, E]), ALU.mult))
            link(v.tensor_reduce(slf.rearrange("p (k t) -> p k t", k=2), ohp, AX, ALU.add))
            v.tensor_copy(slot, slf).then_inc(s["slot"], 1)
            link(v.tensor_tensor(ecm, small[0:1, 136:160, None].broadcast_to([1, 24, 7]),
                                 base[0:1, None, 1:E].broadcast_to([1, 24, 7]), ALU.is_ge))
            link(v.tensor_reduce(eidf, ecm, AX, ALU.add))
            v.tensor_copy(eid, eidf).then_inc(s["eid"], 1)

        def route_scalar(l):
            s = FF[l]
            nc.scalar.wait_ge(s["dlt"], 1)
            nc.scalar.activation(ex1, dlt, ACT.Exp).then_inc(s["exp1"], 1)

        def scatter_gpsimd(l):
            s = FF[l]
            nc.gpsimd.wait_ge(s["slot"], 1)
            nc.gpsimd.wait_ge(s["consts"], 16 * 5)
            nc.gpsimd.wait_ge(LN[l]["normed"], NT)
            if l == 1:
                nc.gpsimd.wait_ge(s_zero, 16)
            for t in range(NT):
                for k in range(TOPK):
                    nc.gpsimd.indirect_dma_start(
                        xs_d[:, :], bass.IndirectOffsetOnAxis(ap=slot[:, k * NT + t:k * NT + t + 1], axis=0),
                        xn[:, t, :], None).then_inc(s["scatter"], 16)
            nc.gpsimd.wait_ge(s_rows, 16 * 2)
            for t in range(NT):
                for k in range(TOPK):
                    nc.gpsimd.indirect_dma_start(
                        rows_d[l][:, :], bass.IndirectOffsetOnAxis(ap=slot[:, k * NT + t:k * NT + t + 1], axis=0),
                        ids[:, k * NT + t:k * NT + t + 1], None).then_inc(s["rows"], 16)

        def load_tile(l, i, n, p):
            s = FF[l]
            nc.sync.dma_start(xs[:, p, :], xs_d[bass.ds(i * P, P), :]).then_inc(s[f"xs{p}"], 16)

        def tile_sync(l, i, n, p):
            nc.sync.wait_ge(FF[l]["x_t"], i + 1)
            load_tile(l, i + 2, n + 1, p)

        def load_rows(l, i, p):
            nc.gpsimd.dma_start(rows[:, p:p + 1], rows_d[l][bass.ds(i * P, P), :]).then_inc(FF[l][f"row{p}"], 16)

        def tile_gpsimd(l, i, n, p, nxt=True):
            s = FF[l]
            g = nc.gpsimd
            g.wait_ge(s[f"row{p}"], 16 * (n + 1))
            g.wait_ge(s["y_e"], i + 1)
            g.indirect_dma_start(y_d[:, :], bass.IndirectOffsetOnAxis(ap=rows[:, p:p + 1], axis=0),
                                 yo[:, p, :], None).then_inc(s[f"ys{p}"], 16)
            if nxt:
                g.wait_ge(s[f"ys{p}"], 16 * (n + 1))
                load_rows(l, i + 2, p)

        def tile_transpose(l, i, n, p):
            s = FF[l]
            nc.tensor.wait_ge(s[f"xs{p}"], 16 * (n + 1))
            later(nc.tensor, s["x_e"], i)
            for kk in range(KD):
                last = nc.tensor.transpose(BK[6][:, kk * P:(kk + 1) * P], xs[:, p, kk * P:(kk + 1) * P], ident[:, :])
            last.then_inc(s["x_t"], 1)

        def expert_of(i):
            return nc.tensor.value_load(eid[0:1, bass.ds(i, 1)], min_val=0, max_val=E - 1)

        def tile_up(l, i, n, p, e):
            s = FF[l]
            nc.tensor.wait_ge(s["x_e"], i + 1)
            for half in range(2):
                later(nc.tensor, s["hid"], 2 * i)
                for gu in range(2):
                    for kk in range(KD):
                        last = nc.tensor.matmul(BK[2 * half + gu][:, 0:IH], xsT[:, p, kk, :],
                                                wgu[:, bass.ds(e * (KD * GU) + (kk * GU + gu * I + half * IH), IH)],
                                                start=kk == 0, stop=kk == KD - 1)
                    last.then_inc(s["gu"], 1)

        def tile_hidden(l, i, n, p):
            s = FF[l]
            nc.tensor.wait_ge(s["hid"], 2 * i + 2)
            later(nc.tensor, s["hte_v"], i)
            later(nc.tensor, s["hte_s"], i)
            for c in range(6):
                last = nc.tensor.transpose(BK[4 + c // 4][0:CH[c], (c % 4) * P:(c % 4 + 1) * P],
                                           hh[:, CO[c]:CO[c] + CH[c]], ident[:, :])
                if c in (3, 5):
                    last.then_inc(s["hid_t"], 1)

        def tile_down(l, i, n, p, e):
            s = FF[l]
            nc.tensor.wait_ge(s["hte_v"], i + 1)
            nc.tensor.wait_ge(s["hte_s"], i + 1)
            later(nc.tensor, s["y_e"], i)
            for c in range(6):
                last = nc.tensor.matmul(BK[7][:, 0:D], hT[0:CH[c], p, c, :],
                                        wd[0:CH[c], bass.ds(e * (6 * D) + c * D, D)], start=c == 0, stop=c == 5)
            last.then_inc(s["down"], 1)

        def tile_scalar_x(l, i, n, p):
            s = FF[l]
            a = nc.scalar
            a.wait_ge(s["x_t"], i + 1)
            a.activation(xsT[:, p, :, :], BK[6][:, 0:S].rearrange("p (k s) -> p k s", k=KD), ACT.Copy).then_inc(s["x_e"], 1)

        def tile_scalar(l, i, n, p):
            s = FF[l]
            a = nc.scalar
            for half in range(2):
                a.wait_ge(s["gu"], 4 * i + 2 * half + 1)
                later(a, s["hid"], 2 * i)
                a.activation(sg[:, half * IH:(half + 1) * IH], BK[2 * half][:, 0:IH], ACT.Silu).then_inc(s["silu"], 1)

        def tile_scalar_2(l, i, n, p):
            s = FF[l]
            a = nc.scalar
            a.wait_ge(s["hid_t"], 2 * i + 2)
            a.activation(hT[0:CH[5], p, 4:6, :], BK[5][0:CH[5], 0:2 * P].rearrange("p (c s) -> p c s", c=2),
                         ACT.Copy).then_inc(s["hte_s"], 1)

        def tile_scalar_y(l, i, n, p):
            s = FF[l]
            a = nc.scalar
            a.wait_ge(s["down"], i + 1)
            later(a, s[f"ys{p}"], 16 * n)
            a.activation(yo[:, p, :], BK[7][:, 0:D], ACT.Copy).then_inc(s["y_e"], 1)

        def tile_vector(l, i, n, p):
            s = FF[l]
            v = nc.vector
            for half in range(2):
                v.wait_ge(s["silu"], 2 * i + half + 1)
                v.wait_ge(s["gu"], 4 * i + 2 * half + 2)
                later(v, s["hid_t"], 2 * i)
                v.tensor_tensor(hh[:, half * IH:(half + 1) * IH], sg[:, half * IH:(half + 1) * IH],
                                BK[2 * half + 1][:, 0:IH], ALU.mult).then_inc(s["hid"], 1)
            v.wait_ge(s["hid_t"], 2 * i + 1)
            v.tensor_copy(hT[:, p, 0:4, :], BK[4][0:CH[0], :].rearrange("p (c s) -> p c s", c=4)).then_inc(s["hte_v"], 1)

        def experts_tensor(l):
            s = FF[l]
            nc.tensor.wait_ge(s["eid"], 1)
            nc.tensor.wait_ge(s_wgu, 16 * (E if l == 1 else E + 2))

            def step(i, n, p, nxt=True):
                e, before = expert_of(i), expert_of(i - 1)
                tile_hidden(l, i - 1, n + p - 1, 1 - p)
                if nxt:
                    tile_transpose(l, i + 1, n + p, 1 - p)
                tile_up(l, i, n, p, e)
                tile_down(l, i - 1, n + p - 1, 1 - p, before)

            tile_transpose(l, 0, 0, 0)
            tile_transpose(l, 1, 0, 1)
            tile_up(l, 0, 0, 0, expert_of(0))
            nc.tensor.wait_ge(s_wd, 32 * E)
            step(1, 0, 1)
            step(2, 1, 0)
            with nc.tensor.Fori(1, (SLOTS_T - 3) // 2) as r:
                step(2 * r + 1, r, 1)
                step(2 * r + 2, r + 1, 0)
            step(SLOTS_T - 2, (SLOTS_T - 2) // 2, 1)
            step(SLOTS_T - 1, (SLOTS_T - 1) // 2, 0, nxt=False)
            tile_hidden(l, SLOTS_T - 1, (SLOTS_T - 1) // 2, 0)
            tile_down(l, SLOTS_T - 1, (SLOTS_T - 1) // 2, 0, expert_of(SLOTS_T - 1))

        def experts_scalar(l):
            def step(i, n, p, nxt=True):
                tile_scalar_2(l, i - 1, n + p - 1, 1 - p)
                if nxt:
                    tile_scalar_x(l, i + 1, n + p, 1 - p)
                tile_scalar(l, i, n, p)
                tile_scalar_y(l, i - 1, n + p - 1, 1 - p)

            tile_scalar_x(l, 0, 0, 0)
            tile_scalar_x(l, 1, 0, 1)
            tile_scalar(l, 0, 0, 0)
            step(1, 0, 1)
            step(2, 1, 0)
            with nc.scalar.Fori(1, (SLOTS_T - 3) // 2) as r:
                step(2 * r + 1, r, 1)
                step(2 * r + 2, r + 1, 0)
            step(SLOTS_T - 2, (SLOTS_T - 2) // 2, 1)
            step(SLOTS_T - 1, (SLOTS_T - 1) // 2, 0, nxt=False)
            tile_scalar_2(l, SLOTS_T - 1, (SLOTS_T - 1) // 2, 0)
            tile_scalar_y(l, SLOTS_T - 1, (SLOTS_T - 1) // 2, 0)

        def experts_vector(l):
            tile_vector(l, 0, 0, 0)
            with nc.vector.Fori(0, (SLOTS_T - 1) // 2) as r:
                tile_vector(l, 2 * r + 1, r, 1)
                tile_vector(l, 2 * r + 2, r + 1, 0)

        def experts_sync(l):
            s = FF[l]
            nc.sync.wait_ge(s["scatter"], 16 * TOPK * NT)
            load_tile(l, 0, 0, 0)
            load_tile(l, 1, 0, 1)
            with nc.sync.Fori(0, (SLOTS_T - 3) // 2) as r:
                tile_sync(l, 2 * r, r, 0)
                tile_sync(l, 2 * r + 1, r, 1)
            tile_sync(l, SLOTS_T - 3, (SLOTS_T - 3) // 2, 0)

        def experts_gpsimd(l):
            s = FF[l]
            nc.gpsimd.wait_ge(s["rows"], 16 * TOPK * NT)
            load_rows(l, 0, 0)
            load_rows(l, 1, 1)
            for i in range(SLOTS_T):
                tile_gpsimd(l, i, i // 2, i % 2, nxt=i + 2 < SLOTS_T)

        def fetch_sync(l):
            s = FF[l]
            nc.sync.wait_ge(s["ys0"], 16 * ((SLOTS_T + 1) // 2))
            nc.sync.wait_ge(s["ys1"], 16 * (SLOTS_T // 2))
            rows = y_d[0:TOPK * T, :].rearrange("(k t p) d -> t p k d", k=TOPK, p=P)
            for t in range(NT):
                if t >= 4:
                    nc.sync.wait_ge(s["added"], t - 3)
                nc.sync.dma_start(yg[:, t % 4, :, :], rows[t]).then_inc(s[f"g{t % 4}"], 16)
                if l == 3 and t >= 4:
                    output_sync(t - 4)

        def output_sync(t):
            nc.sync.wait_ge(FF[3]["added"], t + 1)
            nc.sync.dma_start(out[t * P:(t + 1) * P, :], xres[:, t, :]).then_inc(s_out, 16)

        def combine_vector(l, b):
            s = FF[l]
            v = nc.vector
            for t in range(2 * b, 2 * b + 2):
                v.wait_ge(s[f"g{t % 4}"], 16 * (t // 4 + 1))
                link(v.scalar_tensor_tensor(out=xres[:, t, :], in0=yg[:, t % 4, 0, :], scalar=w01[:, 0, t:t + 1],
                                                      in1=xres[:, t, :], op0=ALU.mult, op1=ALU.add))
                v.scalar_tensor_tensor(out=xres[:, t, :], in0=yg[:, t % 4, 1, :], scalar=w01[:, 1, t:t + 1],
                                       in1=xres[:, t, :], op0=ALU.mult, op1=ALU.add).then_inc(s["added"], 1)
            return s["added"], 2 * b + 2

        def load_gate_up(e):
            nc.sync.dma_start(wgu[:, e * KD * GU:(e + 1) * KD * GU].rearrange("p (k n) -> p k n", k=KD),
                              dr["wgu"][e].rearrange("(k p) n -> p k n", p=P)).then_inc(s_wgu, 16)

        def route_consts_sync(l):
            s = FF[l]
            nc.sync.wait_ge(AT[l - 1]["projected"], B)
            for dst, src in ((tri.bitcast(U16), "tri"), (onesb.bitcast(U16), "onesb"), (small, "small"), (rw, "rw"),
                             (ids, "ids")):
                nc.sync.dma_start(dst, dr[src]).then_inc(s["consts"], 16)

        INIT = 4

        block = ctx.enter_context(nc.Block())

        @block.sync
        def _(sp):
            xd = dr["x"].rearrange("(t p) d -> p t d", p=P)
            for t in range(0, NT, 2):
                sp.dma_start(xres[:, t:t + 2, :], xd[:, t:t + 2, :]).then_inc(s_x[t // 2], 16)
            for dst, src in ((ident[:, :], "ident"), (identb[:, :].bitcast(U16), "identb"), (masks[:, :, :].bitcast(U16), "masks"),
                             (sel[:, :].bitcast(U16), "sel"), (rope[:, :, :], "rope_a")):
                sp.dma_start(dst, dr[src]).then_inc(s_const, 16)
            for dst, src in ((wdq, "wdq"), (wdkv, "wdkv"), (wkr, "wkr"), (wuq, "wuq"), (wuk, "wuk"), (wuv, "wuv"),
                             (wqr, "wqr"), (woa, "woa")):
                sp.dma_start(dst, dr[src]).then_inc(s_wa, 16)
            sp.wait_ge(s_wa, 16 * 8)
            for e in range(3):
                load_gate_up(e)
            for dst, src in ((wqb[:, :, :], "wqb"), (wkvb[:, :, :], "wkvb"), (wob[:, :, :], "wob")):
                sp.dma_start(dst, dr[src].rearrange("(k p) n -> p k n", p=P)).then_inc(s_wb, 16)
            sp.wait_ge(s_init, INIT)
            for b in range(B):
                place_a_sync(b)
            sp.wait_ge(AT[0]["shifted"], (B - 1) * 3 * GA)
            sp.wait_ge(PA["placed_k"], B * PLACED_K)
            sp.wait_ge(AT[0]["placed"], B * PLACED_A)
            sp.wait_ge(s_zero, 16)
            wdv = R1[:, :].rearrange("p (e m) -> p e m", e=E)
            for e in range(E):
                sp.dma_start(wdv[0:CH[0], e, 0:4 * D], dr["wd4"][e]).then_inc(s_wd, 16)
                sp.dma_start(wdv[0:CH[5], e, 4 * D:6 * D], dr["wd2"][e]).then_inc(s_wd, 16)
            sp.wait_ge(AT[0]["pv"], (B - 1) * GA)
            for e in range(3, E):
                if e == 5:
                    sp.wait_ge(AT[0]["shifted"], B * 3 * GA)
                load_gate_up(e)
            route_consts_sync(1)
            experts_sync(1)
            fetch_sync(1)
            sp.wait_ge(PA["evac_v"], B * len(BY_V))
            sp.dma_start(rope[:, :, :], dr["rope_b"]).then_inc(s_const, 16)
            sp.wait_ge(FF[1]["eid"], 1)
            sp.dma_start(ropek, dr["rope_k"]).then_inc(s_const, 16)
            place_b_sync(0)
            for b in range(1, B):
                place_b_sync(b)
            sp.wait_ge(AT[2]["shifted"], (B - 1) * 3 * GB)
            for e in range(6, E):
                load_gate_up(e)
            route_consts_sync(3)
            experts_sync(3)
            fetch_sync(3)
            for t in range(NT - 4, NT):
                output_sync(t)
            sp.wait_ge(s_out, 16 * NT)

        @block.gpsimd
        def _(pool):
            pool.memset(vaug[:, :], 1.0).then_inc(s_init, 1)
            pool.memset(vaug2, 1.0).then_inc(s_init, 1)
            pool.memset(R1[0:32, 0:2 * HA * S], 0.0).then_inc(s_init, 1)
            pool.memset(room(ODD, 2 * HA * S)[0:32, :], 0.0).then_inc(s_init, 1)
            pool.wait_ge(s_init, INIT)
            for b in range(B):
                project_a_gpsimd(b)
                if b == 1:
                    pool.dma_start(xs_d.rearrange("(n p) d -> p n d", p=16),
                                   R1[16:32, None, 0:D].broadcast_to([16, SLOTS // 16, D])).then_inc(s_zero, 16)
            for l in (1, 3):
                pool.dma_start(rows_d[l].rearrange("(n p) o -> n (p o)", p=P), dr["unused"]).then_inc(s_rows, 16)
            scatter_gpsimd(1)
            experts_gpsimd(1)
            pool.wait_ge(AT[0]["pv"], B * GA)
            pool.memset(vaug[:, :], 1.0).then_inc(s_init, 1)
            project_b_gpsimd()
            scatter_gpsimd(3)
            experts_gpsimd(3)

        @block.vector
        def _(dve):
            norm_vector(0, lambda b: (s_x[b], 16))
            dve.wait_ge(LN[0]["transposed"], B)
            dve.memset(nparts[:, :, :, :], 0.0)
            dve.wait_ge(s_const, 16 * 5)
            project_a_vector(0)
            project_a_vector(1, EARLY)
            for b in range(B):
                maxima_a_vector(b)
                if b == 0:
                    project_a_vector(1, LATE)
                if 0 < b < B - 1:
                    project_a_vector(b + 1)
                attend_a_vector(b)
            add_vector(0, B - 1)
            norm_vector(1, lambda b: (AT[0]["added"], B))
            route_vector(1)
            experts_vector(1)
            dve.wait_ge(FF[1]["gu"], 4 * SLOTS_T)
            dve.memset(heads_b[0][64:RBZ, :], 0.0).then_inc(PB["zeroed"], 1)
            norm_vector(2, lambda b: combine_vector(1, b))
            dve.wait_ge(s_const, 16 * 7)
            project_b_vector()
            attend_b_vector()
            norm_vector(3, lambda b: (AT[2]["added"], B))
            route_vector(3)
            experts_vector(3)
            for b in range(B):
                combine_vector(3, b)

        @block.scalar
        def _(act):
            norm_scalar(0)
            act.wait_ge(s_init, INIT)
            project_a_scalar(0)
            project_a_scalar(1)
            for b in range(B):
                if b > 0:
                    out_scalar(0, b - 1)
                if 0 < b < B - 1:
                    project_a_scalar(b + 1)
                attend_a_scalar(b)
            out_scalar(0, B - 1)
            norm_scalar(1)
            route_scalar(1)
            experts_scalar(1)
            norm_scalar(2)
            project_b_scalar()
            act.wait_ge(s_init, INIT + 1)
            attend_b_scalar()
            norm_scalar(3)
            route_scalar(3)
            experts_scalar(3)

        @block.tensor
        def _(pe):
            pe.wait_ge(s_const, 16 * 5)
            for b in range(B):
                norm_tensor(0, b)
            pe.wait_ge(s_wa, 16 * 8)
            project_a_tensor(0)
            project_a_tensor(1, EARLY)
            for b in range(B):
                for g in range(GA):
                    scores_tensor(0, b, g)
                if b == 0:
                    project_a_tensor(1, LATE)
                else:
                    all_t_tensor(0, b - 1)
                    project_tensor(0, b - 1)
                if 0 < b < B - 1:
                    project_a_tensor(b + 1)
                attend_a_tensor(b)
            all_t_tensor(0, B - 1)
            project_tensor(0, B - 1)
            for b in range(B):
                norm_tensor(1, b)
            pe.wait_ge(LN[1]["evac"], B)
            pe.wait_ge(FF[1]["consts"], 16 * 5)
            route_tensor(1)
            experts_tensor(1)
            for b in range(B):
                norm_tensor(2, b)
            pe.wait_ge(LN[2]["evac"], B)
            pe.wait_ge(s_wb, 16 * 3)
            project_b_tensor()
            attend_b_tensor()
            for b in range(B):
                norm_tensor(3, b)
            pe.wait_ge(LN[3]["evac"], B)
            pe.wait_ge(FF[3]["consts"], 16 * 5)
            route_tensor(3)
            experts_tensor(3)


def kernel(**inputs):
    import concourse.bacc as bacc
    from concourse.bass_utils import run_bass_kernel_spmd

    a = {n: np.asarray(v) for n, v in inputs.items()}
    f = "L0_attn_a_"

    def rotated(w, k):
        w = w.reshape(GA, 4, 2, 32, -1).transpose(4, 0, 2, 1, 3).reshape(-1, HA * RD)
        return w.reshape(k, -1, HA * RD).transpose(1, 0, 2)

    def chunked(w, k):
        return w.T.reshape(k, -1, w.shape[0]).transpose(1, 0, 2)

    def even_odd(w, h):
        return w.reshape(D, h, HDB // 2, 2).transpose(0, 3, 2, 1).reshape(D, -1)

    down = a["L0_ffn_Wd"].transpose(0, 2, 1)
    arrays = {
        "x": a[f + "x"].reshape(T, D),
        "wdq": chunked(a[f + "w_dq"], KD), "wdkv": chunked(a[f + "w_dkv"], KD),
        "wuq": chunked(a[f + "w_uq"], 2), "wqr": rotated(a[f + "w_qr"], 2), "wkr": rotated(a[f + "w_kr"], KD),
        "wuk": a[f + "w_uk"].T, "wuv": a[f + "w_uv"].T, "woa": chunked(a[f + "w_out"], KD),
        "wqb": even_odd(a["L0_attn_b_Wq"], HB),
        "wkvb": np.concatenate([even_odd(a["L0_attn_b_Wk"], KVB), a["L0_attn_b_Wv"]], 1),
        "wob": a["L0_attn_b_Wo"],
        "rw": chunked(a["L0_ffn_router_w"], KD),
        "wgu": np.concatenate([a["L0_ffn_Wg"].transpose(0, 2, 1), a["L0_ffn_Wu"].transpose(0, 2, 1)], 2),
        "wd4": down[:, 0:CO[4]].reshape(E, 4, CH[0], D).transpose(0, 2, 1, 3).reshape(E, CH[0], 4 * D),
        "wd2": down[:, CO[4]:I].reshape(E, 2, CH[5], D).transpose(0, 2, 1, 3).reshape(E, CH[5], 2 * D),
        **shape_constants(),
    }
    arrays = {n: np.ascontiguousarray(v) for n, v in arrays.items()}
    nc = bacc.Bacc("TRN2", target_bir_lowering=False, num_devices=1)
    dr = {n: nc.dram_tensor(f"in_{n}", v.shape, mybir.dt.from_np(v.dtype), kind="ExternalInput").ap()
          for n, v in arrays.items()}
    out = nc.dram_tensor("out", [T, D], F32, kind="ExternalOutput").ap()
    build_hybrid(nc, dr, out)
    r = run_bass_kernel_spmd(nc, [{f"in_{n}": v for n, v in arrays.items()}], core_ids=[0])
    return r.results[0]["out"].reshape(B, S, D)
```
